# Optimizing a Trainium2 kernel written in Bass

```python
import numpy as np
import jax
import jax.numpy as jnp

def _softmax(x, axis=-1):
    return jax.nn.softmax(x, axis=axis)

def _gelu(x):
    return jax.nn.gelu(x, approximate=True)

def _silu(x):
    return jax.nn.silu(x)

def _sigmoid(x):
    return jax.nn.sigmoid(x)

def _layernorm(x, axis=-1, eps=1e-05):
    m = jnp.mean(x, axis=axis, keepdims=True)
    v = jnp.var(x, axis=axis, keepdims=True)
    return (x - m) / jnp.sqrt(v + eps)

def _scatter_add(tgt, idx, src, axis=0):
    return tgt.at[idx].add(src)

def _segment_sum(src, seg, n):
    return jax.ops.segment_sum(src, seg, n)
kernel_name = 'mk_gnn_resnorm_d4_gnn_r32_5e44c4'

def setup_inputs(seed: int=0):
    np.random.seed(seed)
    _w = jnp.asarray

    def _rec_inputs():
        import jax
        import jax.numpy as jnp
        _gk = jax.random.key(seed)
        x = -0.0005121 + 1.001 * jax.random.normal(jax.random.fold_in(_gk, 1), (50000, 64), jnp.float32)
        src = jax.random.randint(jax.random.fold_in(_gk, 2), (50000,), 0, 50000, jnp.int32)
        dst = jax.random.randint(jax.random.fold_in(_gk, 3), (50000,), 0, 50000, jnp.int32)
        _o = jnp.argsort(dst, stable=True)
        src = src[_o]
        dst = dst[_o]
        edge_attr_16 = -0.00010739 + 0.99994 * jax.random.normal(jax.random.fold_in(_gk, 12), (50000, 16), jnp.float32)
        edge_attr_64 = -8.16379e-05 + 0.999858 * jax.random.normal(jax.random.fold_in(_gk, 13), (50000, 64), jnp.float32)
        edge_type_3 = jax.random.randint(jax.random.fold_in(_gk, 15), (50000,), 0, 3, jnp.int32)
        edge_weight = jax.random.uniform(jax.random.fold_in(_gk, 16), (50000,), jnp.float32, 0.0, 0.999999)
        node_type_2 = jax.random.randint(jax.random.fold_in(_gk, 17), (50000,), 0, 2, jnp.int32)
        return (x, src, dst, edge_attr_16, edge_attr_64, edge_type_3, edge_weight, node_type_2)
    x, src, dst, edge_attr_16, edge_attr_64, edge_type_3, edge_weight, node_type_2 = _rec_inputs()

    def _L0_gnn_setup():
        import jax, jax.numpy as jnp
        import numpy as np
        N_NODES = 50000
        N_EDGES = 50000
        D = 64
        H = 128
        key = jax.random.key(seed)
        ks = jax.random.split(key, 10)
        s = 0.05
        return {'nodes': jax.random.normal(ks[0], (N_NODES, D), jnp.float32), 'edges': jax.random.normal(ks[1], (N_EDGES, D), jnp.float32), 'senders': jax.random.randint(ks[2], (N_EDGES,), 0, N_NODES, jnp.int32), 'receivers': jax.random.randint(ks[3], (N_EDGES,), 0, N_NODES, jnp.int32), 'We1': jax.random.normal(ks[4], (3 * D, H), jnp.float32) * s, 'be1': jnp.zeros((H,), jnp.float32), 'We2': jax.random.normal(ks[5], (H, D), jnp.float32) * s, 'be2': jnp.zeros((D,), jnp.float32), 'Wn1': jax.random.normal(ks[6], (3 * D, H), jnp.float32) * s, 'bn1': jnp.zeros((H,), jnp.float32), 'Wn2': jax.random.normal(ks[7], (H, D), jnp.float32) * s, 'bn2': jnp.zeros((D,), jnp.float32)}
    _L0_gnn_all = _L0_gnn_setup()
    _L0_gnn_in = {k: v for k, v in _L0_gnn_all.items() if k in ('We1', 'be1', 'We2', 'be2', 'Wn1', 'bn1', 'Wn2', 'bn2')}
    del _L0_gnn_all

    def _L1_gnn_setup():
        import jax, jax.numpy as jnp
        import numpy as np
        N = 3125
        E = 50000
        D = 64
        ALPHA1 = 0.1

        def _gcn_conv(x, edge_index, edge_weight, W, b):
            n = x.shape[0]
            src, dst = (edge_index[0], edge_index[1])
            loop = jnp.arange(n, dtype=src.dtype)
            src_f = jnp.concatenate([src, loop])
            dst_f = jnp.concatenate([dst, loop])
            ew_f = jnp.concatenate([edge_weight, jnp.ones((n,), dtype=edge_weight.dtype)])
            deg = jax.ops.segment_sum(ew_f, dst_f, num_segments=n)
            dis = jnp.where(deg > 0, jax.lax.rsqrt(jnp.where(deg > 0, deg, 1.0)), 0.0)
            norm = dis[src_f] * ew_f * dis[dst_f]
            h = x @ W
            msgs = norm[:, None] * h[src_f]
            out = jax.ops.segment_sum(msgs, dst_f, num_segments=n)
            return out + b
        key = jax.random.key(seed)
        k1, k2, k3, k4 = jax.random.split(key, 4)
        x = jax.random.normal(k1, (N, D), dtype=jnp.float32)
        edge_index = jax.random.randint(k2, (2, E), 0, N, dtype=jnp.int64)
        edge_weight = jax.random.uniform(k3, (E,), dtype=jnp.float32)
        W = jax.random.normal(k4, (D, D), dtype=jnp.float32) * (1.0 / np.sqrt(D))
        b = jnp.zeros((D,), dtype=jnp.float32)
        return {'x': x, 'edge_index': edge_index, 'edge_weight': edge_weight, 'W': W, 'b': b}
    _L1_gnn_all = _L1_gnn_setup()
    _L1_gnn_in = {k: v for k, v in _L1_gnn_all.items() if k in ('W', 'b')}
    del _L1_gnn_all

    def _L2_gnn_setup():
        import jax, jax.numpy as jnp
        import numpy as np
        N, M = (3125, 25000)
        F_IN, F_E, H = (64, 16, 64)
        T_NODE, T_EDGE = (2, 3)
        HEAD_DIM = 16.0

        def _node_proj(x, W, b, node_type):
            p = jnp.einsum('nf,tfh->tnh', x, W) + b[:, None, :]
            return jnp.take_along_axis(p, node_type[None, :, None], axis=0)[0]
        key = jax.random.key(seed)
        ks = jax.random.split(key, 16)
        inp = {'x': jax.random.normal(ks[0], (N, F_IN), jnp.float32), 'edge_feat': jax.random.normal(ks[1], (M, F_E), jnp.float32), 'node_type': jax.random.randint(ks[2], (N,), 0, T_NODE, jnp.int32), 'edge_src': jax.random.randint(ks[3], (M,), 0, N, jnp.int32), 'edge_dst': jax.random.randint(ks[4], (M,), 0, N, jnp.int32), 'edge_type': jax.random.randint(ks[5], (M,), 0, T_EDGE, jnp.int32)}
        s_n = 1.0 / np.sqrt(F_IN)
        s_e = 1.0 / np.sqrt(F_E)
        for i, name in enumerate(['W1', 'W2', 'W3', 'W4']):
            inp[name] = jax.random.normal(ks[6 + i], (T_NODE, F_IN, H), jnp.float32) * s_n
            inp['b' + name[1]] = jax.random.normal(ks[10 + i], (T_NODE, H), jnp.float32) * 0.01
        inp['W5'] = jax.random.normal(ks[14], (T_EDGE, F_E, H), jnp.float32) * s_e
        inp['b5'] = jax.random.normal(ks[15], (T_EDGE, H), jnp.float32) * 0.01
        return inp
    _L2_gnn_all = _L2_gnn_setup()
    _L2_gnn_in = {k: v for k, v in _L2_gnn_all.items() if k in ('W1', 'b1', 'W2', 'b2', 'W3', 'b3', 'W4', 'b4', 'W5', 'b5')}
    del _L2_gnn_all

    def _L3_gnn_setup():
        import jax, jax.numpy as jnp
        import numpy as np
        N_NODES = 3125
        N_EDGES = 31250
        D_IN = 64
        D_OUT = 64
        EPS = 1e-12
        key = jax.random.key(seed)
        k1, k2, k3, k4, k5, k6 = jax.random.split(key, 6)
        feature = jax.random.normal(k1, (N_NODES, D_IN), dtype=jnp.float32)
        edge_sign = jax.random.normal(k2, (N_EDGES,), dtype=jnp.float32)
        src = jax.random.randint(k3, (N_EDGES,), 0, N_NODES)
        dst = jax.random.randint(k4, (N_EDGES,), 0, N_NODES)
        bound = 1.0 / np.sqrt(3 * D_IN)
        W = jax.random.uniform(k5, (D_OUT, 3 * D_IN), dtype=jnp.float32, minval=-bound, maxval=bound)
        b = jax.random.uniform(k6, (D_OUT,), dtype=jnp.float32, minval=-bound, maxval=bound)
        return {'feature': feature, 'edge_sign': edge_sign, 'W': W, 'b': b, 'src': src, 'dst': dst}
    _L3_gnn_all = _L3_gnn_setup()
    _L3_gnn_in = {k: v for k, v in _L3_gnn_all.items() if k in ('W', 'b')}
    del _L3_gnn_all
    return {'x': x, 'src': src, 'dst': dst, 'edge_attr_16': edge_attr_16, 'edge_attr_64': edge_attr_64, 'edge_type_3': edge_type_3, 'edge_weight': edge_weight, 'node_type_2': node_type_2, 'L0_gnn_We1': _L0_gnn_in['We1'], 'L0_gnn_be1': _L0_gnn_in['be1'], 'L0_gnn_We2': _L0_gnn_in['We2'], 'L0_gnn_be2': _L0_gnn_in['be2'], 'L0_gnn_Wn1': _L0_gnn_in['Wn1'], 'L0_gnn_bn1': _L0_gnn_in['bn1'], 'L0_gnn_Wn2': _L0_gnn_in['Wn2'], 'L0_gnn_bn2': _L0_gnn_in['bn2'], 'L1_gnn_W': _L1_gnn_in['W'], 'L1_gnn_b': _L1_gnn_in['b'], 'L2_gnn_W1': _L2_gnn_in['W1'], 'L2_gnn_b1': _L2_gnn_in['b1'], 'L2_gnn_W2': _L2_gnn_in['W2'], 'L2_gnn_b2': _L2_gnn_in['b2'], 'L2_gnn_W3': _L2_gnn_in['W3'], 'L2_gnn_b3': _L2_gnn_in['b3'], 'L2_gnn_W4': _L2_gnn_in['W4'], 'L2_gnn_b4': _L2_gnn_in['b4'], 'L2_gnn_W5': _L2_gnn_in['W5'], 'L2_gnn_b5': _L2_gnn_in['b5'], 'L3_gnn_W': _L3_gnn_in['W'], 'L3_gnn_b': _L3_gnn_in['b']}

def reference(x, src, dst, edge_attr_16, edge_attr_64, edge_type_3, edge_weight, node_type_2, L0_gnn_We1, L0_gnn_be1, L0_gnn_We2, L0_gnn_be2, L0_gnn_Wn1, L0_gnn_bn1, L0_gnn_Wn2, L0_gnn_bn2, L1_gnn_W, L1_gnn_b, L2_gnn_W1, L2_gnn_b1, L2_gnn_W2, L2_gnn_b2, L2_gnn_W3, L2_gnn_b3, L2_gnn_W4, L2_gnn_b4, L2_gnn_W5, L2_gnn_b5, L3_gnn_W, L3_gnn_b):
    import jax
    import jax.numpy as jnp

    def _L0_gnn_ref(nodes, edges, senders, receivers, We1, be1, We2, be2, Wn1, bn1, Wn2, bn2):
        import jax, jax.numpy as jnp
        import numpy as np
        N_NODES = 50000
        N_EDGES = 50000
        D = 64
        H = 128
        edge_in = jnp.concatenate([edges, nodes[senders], nodes[receivers]], axis=-1)
        e = jax.nn.relu(edge_in @ We1 + be1) @ We2 + be2
        sent_agg = jax.ops.segment_sum(e, senders, num_segments=N_NODES)
        recv_agg = jax.ops.segment_sum(e, receivers, num_segments=N_NODES)
        node_in = jnp.concatenate([nodes, sent_agg, recv_agg], axis=-1)
        n = jax.nn.relu(node_in @ Wn1 + bn1) @ Wn2 + bn2
        return nodes + n

    def _L1_gnn_ref(x, edge_index, edge_weight, W, b):
        import jax, jax.numpy as jnp
        import numpy as np
        N = 3125
        E = 50000
        D = 64
        ALPHA1 = 0.1

        def _gcn_conv(x, edge_index, edge_weight, W, b):
            n = x.shape[0]
            src, dst = (edge_index[0], edge_index[1])
            loop = jnp.arange(n, dtype=src.dtype)
            src_f = jnp.concatenate([src, loop])
            dst_f = jnp.concatenate([dst, loop])
            ew_f = jnp.concatenate([edge_weight, jnp.ones((n,), dtype=edge_weight.dtype)])
            deg = jax.ops.segment_sum(ew_f, dst_f, num_segments=n)
            dis = jnp.where(deg > 0, jax.lax.rsqrt(jnp.where(deg > 0, deg, 1.0)), 0.0)
            norm = dis[src_f] * ew_f * dis[dst_f]
            h = x @ W
            msgs = norm[:, None] * h[src_f]
            out = jax.ops.segment_sum(msgs, dst_f, num_segments=n)
            return out + b
        conv = _gcn_conv(x, edge_index, edge_weight, W, b)
        out = (1.0 - ALPHA1) * conv + ALPHA1 * x
        return jax.nn.elu(out)

    def _L2_gnn_ref(x, edge_feat, W1, b1, W2, b2, W3, b3, W4, b4, W5, b5, node_type, edge_src, edge_dst, edge_type):
        import jax, jax.numpy as jnp
        import numpy as np
        N, M = (3125, 25000)
        F_IN, F_E, H = (64, 16, 64)
        T_NODE, T_EDGE = (2, 3)
        HEAD_DIM = 16.0

        def _node_proj(x, W, b, node_type):
            p = jnp.einsum('nf,tfh->tnh', x, W) + b[:, None, :]
            return jnp.take_along_axis(p, node_type[None, :, None], axis=0)[0]
        n = x.shape[0]
        h1 = _node_proj(x, W1, b1, node_type)
        h2 = _node_proj(x, W2, b2, node_type)
        h3 = _node_proj(x, W3, b3, node_type)
        h4 = _node_proj(x, W4, b4, node_type)
        w5e = jnp.einsum('mf,mfh->mh', edge_feat, W5[edge_type]) + b5[edge_type]
        num = jnp.sum(h3[edge_dst] * (h4[edge_src] + w5e), axis=-1)
        score = jax.nn.softmax((num / jnp.sqrt(HEAD_DIM))[:, None], axis=-1)[:, 0]
        msg = score[:, None] * (h2[edge_src] + w5e)
        out = h1 + jax.ops.segment_sum(msg, edge_dst, num_segments=n)
        return out

    def _L3_gnn_ref(feature, edge_sign, W, b, src, dst):
        import jax, jax.numpy as jnp
        import numpy as np
        N_NODES = 3125
        N_EDGES = 31250
        D_IN = 64
        D_OUT = 64
        EPS = 1e-12
        n = feature.shape[0]
        dt = feature.dtype
        pos_e = (edge_sign >= 0).astype(dt)
        neg_e = (edge_sign < 0).astype(dt)
        msg = feature[src]
        pos_sum = jax.ops.segment_sum(msg * pos_e[:, None], dst, num_segments=n)
        neg_sum = jax.ops.segment_sum(msg * neg_e[:, None], dst, num_segments=n)
        deg = jax.ops.segment_sum(jnp.ones((src.shape[0],), dt), dst, num_segments=n)
        denom = jnp.maximum(deg, 1.0)[:, None]
        pos_out = pos_sum / denom
        neg_out = neg_sum / denom
        h = jnp.concatenate([pos_out, neg_out, feature], axis=1)
        out = h @ W.T + b
        nrm = jnp.sqrt(jnp.sum(out * out, axis=-1, keepdims=True))
        return out / jnp.maximum(nrm, EPS)
    edge_index = jnp.stack([src, dst])
    x = _layernorm(x + _L0_gnn_ref(x, edge_attr_64, src, dst, L0_gnn_We1, L0_gnn_be1, L0_gnn_We2, L0_gnn_be2, L0_gnn_Wn1, L0_gnn_bn1, L0_gnn_Wn2, L0_gnn_bn2), axis=-1)
    x = _layernorm(x + _L1_gnn_ref(x, edge_index, edge_weight, L1_gnn_W, L1_gnn_b), axis=-1)
    x = _layernorm(x + _L2_gnn_ref(x, edge_attr_16, L2_gnn_W1, L2_gnn_b1, L2_gnn_W2, L2_gnn_b2, L2_gnn_W3, L2_gnn_b3, L2_gnn_W4, L2_gnn_b4, L2_gnn_W5, L2_gnn_b5, node_type_2, src, dst, edge_type_3), axis=-1)
    x = _layernorm(x + _L3_gnn_ref(x, edge_weight, L3_gnn_W, L3_gnn_b, src, dst), axis=-1)
    return x

_drawn_inputs = setup_inputs


def setup_inputs(seed=0):
    import zlib

    import numpy as np

    out = dict(_drawn_inputs(seed))
    spreads = {'L0_gnn_be1': (0.0, 0.8),
     'L0_gnn_be2': (0.0, 0.481),
     'L0_gnn_bn1': (0.0, 0.442),
     'L0_gnn_bn2': (0.0, 0.1),
     'L1_gnn_b': (0.0, 0.1)}
    factors = {'edge_attr_64': 4.101,
     'L2_gnn_b1': 8.0,
     'L2_gnn_b2': 8.0,
     'L2_gnn_b5': 8.0,
     'L3_gnn_b': 3.824}
    for name, (base, spread) in spreads.items():
        noise = np.random.default_rng([zlib.crc32(name.encode()), seed]).standard_normal(out[name].shape)
        drawn = base * np.exp(spread * noise) if base else spread * noise
        out[name] = jnp.asarray(drawn.astype(out[name].dtype))
    for name, factor in factors.items():
        out[name] = (out[name] * factor).astype(out[name].dtype)
    return out
```

```python
from contextlib import ExitStack, contextmanager

import concourse.bass as bass
from concourse import mybir

P = 128
N = 50000
D = 64
HID = 128
F_EDGE = 16
NODE_TYPES = 2
EDGE_TYPES = 3
TILES = 4
GROUP = TILES * P
GROUPS = 2 * -(-N // (2 * GROUP))
WIDE = 8
WIDE_GROUPS = GROUPS * TILES // WIDE
IN_SLOT = [-(-WIDE_GROUPS // 2), WIDE_GROUPS // 2]
assert WIDE_GROUPS % 2 == 1
STEPS = GROUPS // 2
ROWS = GROUPS * GROUP
DUMP = ROWS
TABLE = ROWS + P
EW_COL, ONE_COL = D, D + 1
EDGE_TILES = ROWS // P
WINDOW_TILES = WIDE + 1
WINDOW = WINDOW_TILES * P
D_RECV = D + 2
LN_EPS = 1e-5
NORM_EPS = 1e-12
ALPHA = 0.1
HEAD_DIM = 16.0

f32 = mybir.dt.float32
i32 = mybir.dt.int32
ALU = mybir.AluOpType
ACT = mybir.ActivationFunctionType
AX = mybir.AxisListType


def linker(engine, sem, it, per_step):
    made = [0]

    def link(ins):
        made[0] += 1
        ins.then_inc(sem, 1)
        engine.wait_ge(sem, it * per_step + made[0])

    def end():
        assert made[0] == per_step, made[0]

    return link, end


class Group:

    def __init__(self, it, k, ahead=2):
        self.it, self.k, self.ahead = it, k, ahead
        self.g, self.h, self.round = it * 2 + k, k % 2, it + k // 2
        self.tiles = bass.ds(self.g * WIDE, WIDE)

    def next(self):
        return Group(self.it, self.k + 1)

    def last(self):
        return Group(self.it, self.k - 1)


def pipeline(engine, step, links=None):
    step(Group(0, 0), True, False)
    rounds = (WIDE_GROUPS - 3) // 2
    with engine.Fori(0, rounds, 1) as it:
        if links:
            links.enter(it)
        step(Group(it, 1), False, False)
        step(Group(it, 2), False, False)
        if links:
            links.leave(rounds)
    step(Group(0, WIDE_GROUPS - 2, 1), False, False)
    step(Group(0, WIDE_GROUPS - 1, 0), False, True)


class Links:

    def __init__(self, engine, sem, per_round, passed=None):
        self.engine, self.sem, self.per_round, self.passed = engine, sem, per_round, passed
        self.it, self.made, self.base = 0, 0, 0

    def link(self, ins):
        ins.then_inc(self.sem, 1)
        self.made += 1
        self.engine.wait_ge(self.sem, self.it * self.per_round + (self.base + self.made))
        if self.passed is not None:
            self.engine.sem_inc(self.passed, 1)

    def enter(self, it):
        self.it, self.base, self.made = it, self.base + self.made, 0

    def leave(self, rounds):
        assert self.made == self.per_round, self.made
        self.it, self.base, self.made = 0, self.base + rounds * self.made, 0


@contextmanager
def phase_semaphores(nc, tag, names):
    sems = {n: nc.alloc_semaphore(name=tag + n) for n in names}
    yield sems
    nc.all_engine_barrier()
    nc.clear_and_free_semaphores(list(sems.values()))
    nc.all_engine_barrier()


def over_features(columns):
    return columns.unsqueeze(2).to_broadcast([P, TILES, D])


def build(nc, io):
    with ExitStack() as whole:
        def sb(name, shape, dt=f32):
            return whole.enter_context(nc.sbuf_tensor(name, shape, dt))

        def ps(name, shape):
            return whole.enter_context(nc.psum_tensor(name, shape, f32))

        def sem(name):
            return whole.enter_context(nc.semaphore(name))

        def table(name, width, n=ROWS):
            return nc.dram_tensor(name, (n, width), f32).ap()

        sent_sum = [table(f"sent_sum{k}", D, TABLE) for k in range(2)]
        messages_t = table("messages_t", D_RECV, ROWS + WINDOW)
        recv_sum = table("recv_sum", D_RECV, TABLE)
        conv_sum = [table(f"conv_sum{k}", D, TABLE) for k in range(2)]
        attn_sum = [table(f"attn_sum{k}", D, TABLE) for k in range(2)]
        sign_sum = [table(f"sign_sum{k}", D, TABLE) for k in range(2)]
        y1_t = table("y1_t", D)
        h24_t = table("h24_t", 2 * D)
        h3_t = table("h3_t", D)
        z3_t = table("z3_t", 2 * D)
        f3_t = table("f3_t", D)
        z3_halves = z3_t.rearrange("r (s d) -> (r s) d", s=2)

        def group_of(tab, g, width=D):
            return tab.rearrange("(q t) d -> q t d", t=TILES)[bass.ds(g * P, P), :, 0:width]

        def wide_group_of(tab, g, width=D):
            return tab.rearrange("(q t) d -> q t d", t=WIDE)[bass.ds(g * P, P), :, 0:width]

        x_all = sb("x_all", [P, WIDE_GROUPS * WIDE, D])
        ident = sb("ident", [P, P])
        earlier = sb("earlier", [P, P])
        dump_row_i, dump_row = sb("dump_row_i", [P, 1], i32), sb("dump_row", [P, 1])
        ew_all = sb("ew_all", [P, GROUPS * TILES])
        etype_all = sb("etype_all", [P, GROUPS * TILES], i32)
        ntype_all = sb("ntype_all", [P, GROUPS * TILES], i32)
        recv_all = sb("recv_all", [P, GROUPS * TILES], i32)
        dis_all = sb("dis_all", [P, GROUPS * TILES])
        rcount_all = sb("rcount_all", [P, GROUPS * TILES])
        We1a, We1b, We2 = sb("We1a", [P, HID]), sb("We1b", [D, HID]), sb("We2", [HID, D])
        Wn1a, Wn1b, Wn2 = sb("Wn1a", [P, HID]), sb("Wn1b", [P, HID]), sb("Wn2", [HID, D])
        be1, bn1 = sb("be1", [HID, 1]), sb("bn1", [HID, 1])
        be2, bn2 = sb("be2", [P, D]), sb("bn2", [P, D])
        Wconv = sb("Wconv", [D + 1, D])
        W1234 = sb("W1234", [P, 4 * D])
        b1234 = sb("b1234", [WIDE * NODE_TYPES, WIDE, 4 * D])
        W5 = sb("W5", [EDGE_TYPES * (F_EDGE + 1), 2, D])
        Wsign = sb("Wsign", [D + 1, 3 * D])
        Wsign_rows = sb("Wsign_rows", [D, 3 * D])

        starts_t = nc.dram_tensor("starts_t", (4 * P,), i32).ap()
        starts = sb("starts", [1, 4 * P], i32)
        sorted_flag = sb("sorted_flag", [1, 1], i32)
        band_i, band = sb("band_i", [P, 3 * P], i32), sb("band", [P, 3 * P])
        band_from_i, band_from = sb("band_from_i", [P, WINDOW_TILES], i32), sb("band_from", [P, WINDOW_TILES])

        wide_bank = [ps(f"bank{2 * n}_{2 * n + 1}", [P, 2 * GROUP]) for n in range(4)]
        bank = [wide_bank[n // 2][:, n % 2 * GROUP:(n % 2 + 1) * GROUP] for n in range(8)]

        gath_a = [[sem(f"gath_a{h}{t}") for t in range(TILES)] for h in range(2)]
        gath_b = [[sem(f"gath_b{h}{t}") for t in range(TILES)] for h in range(2)]
        passed = sem("passed")
        sent_done, recv_done = [sem(f"sent_done{k}") for k in range(2)], sem("recv_done")
        idx_loaded = [sem(f"idx_loaded{h}") for h in range(2)]
        loaded = [sem(f"loaded{h}") for h in range(2)]
        feat_loaded = [sem(f"feat_loaded{h}") for h in range(2)]
        in_free = [sem(f"in_free{h}") for h in range(2)]
        stored = [sem(f"stored{h}") for h in range(2)]
        added = [sem(f"added{k}") for k in range(2)]
        pe_passed = sem("pe_passed")
        ready = sem("ready")
        setup_load = sem("setup_load")
        late_load = sem("late_load")
        cleared = sem("cleared")
        cleared_later = sem("cleared_later")

        def fill(tab):
            return tab.rearrange("(p r) d -> p (r d)", p=P)

        ZEROS = TABLE * D_RECV // P // 6 + 1
        zeros = x_all[:].rearrange("p t d -> p (t d)")[:, 0:ZEROS]

        def clear(eng, tab, done):
            flat = fill(tab)
            part = flat.shape[1] // 6
            assert part * 6 == flat.shape[1] and part <= ZEROS
            for n in range(6):
                eng.dma_start(flat[:, n * part:(n + 1) * part], zeros[:, 0:part]).then_inc(done, 16)
            return 96

        def edge_buffers(c, tag):
            def eb(name, shape, dt=f32):
                return c.enter_context(nc.sbuf_tensor(tag + name, shape, dt))

            idx = [eb(f"idx{h}", [P, 2 * TILES], i32) for h in range(2)]
            cat = [eb(f"cat{h}", [P, TILES, 2 * D]) for h in range(2)]
            side = [eb(f"side{h}", [P, TILES, D_RECV]) for h in range(2)]
            extra = [eb(f"extra{h}", [P, TILES, D]) for h in range(2)]
            feat = [eb(f"feat{h}", [P, TILES, F_EDGE]) for h in range(2)]
            scat_idx = [eb(f"scat_idx{h}", [P, 2 * TILES], i32) for h in range(2)]
            rows_a = [eb(f"rows_a{h}", [P, TILES, D_RECV]) for h in range(2)]
            rows_b = [eb(f"rows_b{h}", [P, TILES, D]) for h in range(2)]
            idx_f = eb("idx_f", [P, 2 * TILES])
            gidx = [eb(f"gidx{h}", [P, TILES], i32) for h in range(2)]
            same = eb("same", [P, 2 * TILES, P])
            masked = eb("masked", [P, 2 * TILES, P])
            small = [eb(f"small{n}", [P, 2 * TILES]) for n in range(8)]
            msg = eb("msg", [P, TILES, D_RECV])
            typed = eb("typed", [P, TILES, EDGE_TYPES * (F_EDGE + 1)])
            catT = eb("catT", [P, GROUP])
            sideT = eb("sideT", [D, GROUP])
            hiddenT = eb("hiddenT", [HID, GROUP])
            work = [eb(f"work{n}", [P, TILES, D]) for n in range(1)]
            hw = eb("hw", [P, TILES, 2 * D])
            return (idx, cat, side, extra, feat, scat_idx, rows_a, rows_b, idx_f, gidx,
                    same, masked, small, msg, typed, catT, sideT, hiddenT, work, hw)

        with ExitStack() as c:
            zeroed, wsign_ready, wsign_t = c.enter_context(phase_semaphores(
                nc, "setup_", ("zeroed", "wsign_ready", "wsign_t"))).values()
            block = c.enter_context(nc.Block())
            loads = [
                (ew_all, io["ew_cols"]), (etype_all, io["etype_cols"]), (ntype_all, io["ntype_cols"]),
                (We1a, io["We1"][0:P]), (We1b, io["We1"][P:P + D]), (We2, io["We2"]),
                (Wn1a, io["Wn1"][0:P]), (Wn1b[0:D, :], io["Wn1"][D:2 * D]), (Wn1b[D:2 * D, :], io["Wn1"][P:P + D]), (Wn2, io["Wn2"]),
                (be1, io["be1"].unsqueeze(1)), (bn1, io["bn1"].unsqueeze(1)),
                (be2, io["be2"].unsqueeze(0).to_broadcast([P, D])),
                (bn2, io["bn2"].unsqueeze(0).to_broadcast([P, D])),
                (Wconv[0:D, :], io["W_conv"]), (Wconv[D:D + 1, :], io["b_conv"].unsqueeze(0)),
                (Wsign_rows, io["W_sign"]),
            ]
            late = []
            for m, k in enumerate((2, 4, 3, 1)):
                cols = slice(m * D, (m + 1) * D)
                late.append((W1234[:, cols], io[f"W{k}"].rearrange("a f h -> (a f) h")))
                for t in range(WIDE):
                    late.append((b1234[2 * t:2 * t + 2, t, cols], io[f"b{k}"]))
            for m in range(2):
                late.append((W5[0:EDGE_TYPES * F_EDGE, m, :], io["W5"].rearrange("a f h -> (a f) h")))
                late.append((W5[EDGE_TYPES * F_EDGE:EDGE_TYPES * (F_EDGE + 1), m, :], io["b5"]))
            late.append((Wsign[D:D + 1, 2 * D:3 * D], io["b_sign"].unsqueeze(0)))

            @block.sync
            def _(sp):
                for dst, src in loads:
                    sp.dma_start(dst[:] if not isinstance(dst, bass.AP) else dst, src).then_inc(setup_load, 16)
                sp.wait_ge(zeroed, 4)
                for dst, src in late:
                    sp.dma_start(dst, src).then_inc(late_load, 16)
                sp.wait_ge(setup_load, 16 * len(loads))
                sp.wait_ge(late_load, 16 * len(late))

            @block.gpsimd
            def _(pool):
                pool.memset(ident[:], 0.0).then_inc(ready, 1)
                pool.memset(earlier[:], 1.0).then_inc(ready, 1)
                pool.iota(dump_row_i[:], [[0, 1]], base=DUMP, channel_multiplier=1).then_inc(ready, 1)
                pool.wait_ge(ready, 3)
                pool.affine_select(out=ident[:], in_=ident[:], compare_op=ALU.not_equal, fill=1.0,
                                   base=0, pattern=[[-1, P]], channel_multiplier=1).then_inc(ready, 1)
                pool.affine_select(out=earlier[:], in_=earlier[:], compare_op=ALU.is_gt, fill=0.0,
                                   base=0, pattern=[[-1, P]], channel_multiplier=1).then_inc(ready, 1)
                pool.tensor_copy(dump_row[:], dump_row_i[:]).then_inc(ready, 1)

            @block.scalar
            def _(act):
                act.wait_ge(zeroed, 4)
                for tab in sent_sum:
                    clear(act, tab, cleared)

            @block.vector
            def _(dve):
                dve.memset(zeros, 0.0).then_inc(zeroed, 1)
                dve.memset(b1234[:], 0.0).then_inc(zeroed, 1)
                dve.memset(Wsign[D:D + 1, :], 0.0).then_inc(zeroed, 1)
                dve.memset(W5[:], 0.0).then_inc(zeroed, 1)
                dve.wait_ge(setup_load, 16 * len(loads))
                dve.tensor_scalar(Wconv[:], Wconv[:], 1.0 - ALPHA, None, ALU.mult).then_inc(wsign_ready, 1)
                dve.wait_ge(wsign_t, 3)
                dve.tensor_copy(Wsign[0:D, :], bank[0][0:D, 0:3 * D]).then_inc(wsign_ready, 1)

            @block.tensor
            def _(pe):
                pe.wait_ge(ready, 6)
                pe.wait_ge(setup_load, 16 * len(loads))
                for m in range(3):
                    pe.transpose(bank[0][0:D, m * D:(m + 1) * D], Wsign_rows[:, m * D:(m + 1) * D],
                                 ident[0:D, 0:D]).then_inc(wsign_t, 1)

        gathers_a = gathers_b = adds = idx_at = free_at = 0

        loaded_at, stored_at = [0, 0], [0, 0]

        with ExitStack() as c:
            s = c.enter_context(phase_semaphores(nc, "fi_", (
                "loaded", "iota", "tile", "gathered", "start", "stored", "back", "link", "bad", "total", "flag")))
            COLS = 4
            STARTS = COLS * P

            def buf(name, shape, dt=f32):
                return c.enter_context(nc.sbuf_tensor("fi_" + name, shape, dt))

            firsts_i, firsts = buf("firsts_i", [P, EDGE_TILES], i32), buf("firsts", [P, EDGE_TILES])
            here_i, next_i = buf("here_i", [P, EDGE_TILES], i32), buf("next_i", [P, EDGE_TILES], i32)
            compare = buf("compare", [P, EDGE_TILES])
            limit_i, limit = buf("limit_i", [P, COLS], i32), buf("limit", [P, COLS])
            before_n, tile_i = buf("before_n", [P, COLS]), buf("tile_i", [P, COLS], i32)
            tile_dst_i, tile_dst = buf("tile_dst_i", [P, COLS, P], i32), buf("tile_dst", [P, COLS, P])
            inside, start_i = buf("inside", [P, COLS]), buf("start_i", [P, COLS], i32)
            own_i, after_i, own = buf("own_i", [WIDE_GROUPS, WIDE], i32), buf("after_i", [WIDE_GROUPS, WIDE], i32), buf("own", [WIDE_GROUPS, WIDE + 1])
            low_i, low = buf("low_i", [WIDE_GROUPS, WIDE + 1], i32), buf("low", [WIDE_GROUPS, WIDE + 1])
            high = buf("high", [WIDE_GROUPS, WIDE + 1])
            bad = buf("bad", [P, 4])
            ones = buf("ones", [P, 1])
            flag = buf("flag", [1, 2])
            block = c.enter_context(nc.Block())

            @block.sync
            def _(sp):
                sp.dma_start(firsts_i[:], io["dst_firsts"].unsqueeze(0).to_broadcast([P, EDGE_TILES])).then_inc(s["loaded"], 16)
                sp.dma_start(here_i[:], io["dst_lin"][0:ROWS].rearrange("(p n) -> p n", p=P)).then_inc(s["loaded"], 16)
                sp.dma_start(next_i[:], io["dst_lin"][1:ROWS + 1].rearrange("(p n) -> p n", p=P)).then_inc(s["loaded"], 16)
                sp.wait_ge(s["start"], 1)
                sp.dma_start(starts_t.rearrange("(p c) -> p c", p=P), start_i[:]).then_inc(s["stored"], 16)
                sp.wait_ge(s["stored"], 16)
                sp.dma_start(starts[:], starts_t.unsqueeze(0)).then_inc(s["back"], 16)
                sp.dma_start(own_i[:], starts_t[0:WIDE_GROUPS * WIDE].rearrange("(g k) -> g k", k=WIDE)).then_inc(s["back"], 16)
                sp.dma_start(after_i[:], starts_t[WIDE:(WIDE_GROUPS + 1) * WIDE].rearrange("(g k) -> g k", k=WIDE)
                             ).then_inc(s["back"], 16)
                sp.wait_ge(s["back"], 48)
                sp.wait_ge(s["flag"], 1)

            @block.gpsimd
            def _(pool):
                pool.iota(limit_i[:], [[P, COLS]], base=0, channel_multiplier=COLS * P).then_inc(s["iota"], 1)
                pool.iota(low_i[:], [[P, WIDE + 1]], base=-P, channel_multiplier=0).then_inc(s["iota"], 1)
                pool.iota(band_i[:], [[1, 3 * P]], base=0, channel_multiplier=0).then_inc(s["iota"], 1)
                pool.iota(band_from_i[:], [[P, WINDOW_TILES]], base=-P, channel_multiplier=0).then_inc(s["iota"], 1)
                pool.wait_ge(s["tile"], 1)
                for k in range(COLS):
                    pool.indirect_dma_start(tile_dst_i[:, k, :], None, io["dst_lin"].rearrange("(m q) -> m q", q=P),
                                            bass.IndirectOffsetOnAxis(ap=tile_i[:, k:k + 1], axis=0)
                                            ).then_inc(s["gathered"], 16)

            @block.vector
            def _(dve):
                links = Links(dve, s["link"], 0)
                link = links.link
                dve.wait_ge(s["iota"], 4)
                link(dve.tensor_copy(band[:], band_i[:]))
                link(dve.tensor_copy(band_from[:], band_from_i[:]))
                link(dve.memset(bad[:], 0.0))
                link(dve.memset(ones[:], 1.0))
                link(dve.tensor_copy(limit[:], limit_i[:]))
                link(dve.tensor_copy(low[:], low_i[:]))
                dve.wait_ge(s["loaded"], 48)
                link(dve.tensor_copy(firsts[:], firsts_i[:]))
                for k in range(COLS):
                    link(dve.tensor_scalar(compare[:], firsts[:], limit[:, k:k + 1], None, ALU.is_lt))
                    link(dve.tensor_reduce(before_n[:, k:k + 1], compare[:], AX.X, ALU.add))
                link(dve.tensor_scalar(before_n[:], before_n[:], -1.0, 0.0, ALU.add, ALU.max))
                dve.tensor_copy(tile_i[:], before_n[:]).then_inc(s["tile"], 1)
                link(dve.tensor_tensor(compare[:], here_i[:], next_i[:], ALU.is_gt))
                link(dve.tensor_reduce(bad[:, 0:1], compare[:], AX.X, ALU.add))
                dve.wait_ge(s["gathered"], 16 * COLS)
                link(dve.tensor_copy(tile_dst[:], tile_dst_i[:]))
                for k in range(COLS):
                    link(dve.tensor_scalar(compare[:, 0:P], tile_dst[:, k, :], limit[:, k:k + 1], None, ALU.is_lt))
                    link(dve.tensor_reduce(inside[:, k:k + 1], compare[:, 0:P], AX.X, ALU.add))
                dve.scalar_tensor_tensor(start_i[:], before_n[:], float(P), inside[:], ALU.mult, ALU.add).then_inc(s["start"], 1)
                dve.wait_ge(s["back"], 48)
                link(dve.tensor_copy(own[:, 0:WIDE], own_i[:]))
                link(dve.tensor_copy(own[:, WIDE:WIDE + 1], after_i[:, 0:1]))
                link(dve.tensor_scalar(high[:], own[:], own[:, 0:1], None, ALU.subtract))
                link(dve.tensor_tensor(own[:], high[:], low[:], ALU.is_lt))
                link(dve.tensor_reduce(bad[0:WIDE_GROUPS, 1:2], own[:, 1:WIDE], AX.X, ALU.add))
                link(dve.tensor_scalar(low[:], low[:], 2.0 * P, None, ALU.add))
                link(dve.tensor_tensor(own[:], high[:], low[:], ALU.is_gt))
                link(dve.tensor_reduce(bad[0:WIDE_GROUPS, 2:3], own[:, 1:WIDE + 1], AX.X, ALU.add))
                dve.tensor_reduce(bad[:, 3:4], bad[:, 0:3], AX.X, ALU.add).then_inc(s["bad"], 1)
                dve.wait_ge(s["total"], 1)
                link(dve.tensor_scalar(flag[:, 0:1], bank[0][0:1, 0:1], 0.5, None, ALU.is_lt))
                dve.tensor_copy(sorted_flag[:], flag[:, 0:1]).then_inc(s["flag"], 1)

            @block.tensor
            def _(pe):
                pe.wait_ge(s["bad"], 1)
                nc.tensor.matmul(bank[0][0:1, 0:1], bad[:, 3:4], ones[:], start=True, stop=True).then_inc(s["total"], 1)

        is_sorted = nc.values_load(sorted_flag[0:1, 0:1], min_val=0, max_val=1)

        def window_sums(tag, table_rows, sums, width, gathered_from=None, signed=False):
            gathers = gathered_from is not None
            with ExitStack() as c:
                s = c.enter_context(phase_semaphores(nc, tag, (
                    "numbers_f", "numbers_psum", "columns", "S", "agg", "out", "link", "numbers_loaded0", "numbers_loaded1",
                    "rows_loaded0", "rows_loaded1", "out_stored0", "out_stored1", "sp_passed")))
                numbers_loaded = [s[f"numbers_loaded{h}"] for h in range(2)]
                rows_loaded = [s[f"rows_loaded{h}"] for h in range(2)]
                out_stored = [s[f"out_stored{h}"] for h in range(2)]

                def buf(name, shape, dt=f32, slots=2):
                    return [c.enter_context(nc.sbuf_tensor(f"{tag}{name}{h}", shape, dt)) for h in range(slots)]

                K = WINDOW_TILES
                numbers_i, numbers_f = buf("numbers_i", [K, 2, P], i32), buf("numbers_f", [K, 2, P], slots=1)[0]
                weights = buf("weights", [K, P])
                columns = buf("columns", [P, 3 * K])
                at = buf("at", [P, K])
                negative = buf("negative", [P, K], slots=1)[0]
                index = buf("index", [P, K], i32)
                in_rows = buf("rows", [P, K, width])
                S = buf("S", [P, K, 3 * P])
                out = buf("out", [P, WIDE, width])
                band_at = buf("band_at", [P, K], slots=1)[0]
                sums_psum = wide_bank[0][:].rearrange("p (b n) -> p b n", b=2)[:, :, 0:4 * width].rearrange("p b (t d) -> p b t d", t=4)
                block = c.enter_context(nc.Block())

                @block.sync
                def _(sp):
                    def load_numbers(b, early):
                        if not early:
                            sp.wait_ge(s["numbers_psum"], b.g - 1)
                        sp.sem_inc(s["sp_passed"], 1)
                        start = sp.value_load(starts[0:1, bass.ds(b.g * WIDE, 1)], min_val=0, max_val=ROWS)
                        window = bass.ds(start, WINDOW)
                        sp.dma_start(numbers_i[b.h][:, 0, :], io["dst_lin"][window].rearrange("(k p) -> k p", p=P)).then_inc(numbers_loaded[b.h], 16)
                        if gathers:
                            sp.dma_start(numbers_i[b.h][:, 1, :], io["src_lin"][window].rearrange("(k p) -> k p", p=P)).then_inc(numbers_loaded[b.h], 16)
                            sp.dma_start(weights[b.h][:], io["ew_lin"][window].rearrange("(k p) -> k p", p=P)).then_inc(numbers_loaded[b.h], 16)

                    def load_rows(b, early):
                        if not early:
                            sp.wait_ge(s["agg"], b.g - 1)
                        sp.sem_inc(s["sp_passed"], 1)
                        start = sp.value_load(starts[0:1, bass.ds(b.g * WIDE, 1)], min_val=0, max_val=ROWS)
                        sp.dma_start(in_rows[b.h][:], table_rows[bass.ds(start, WINDOW), :].rearrange("(k p) d -> p k d", p=P)
                                     ).then_inc(rows_loaded[b.h], 16)

                    def store(b):
                        sp.wait_ge(s["out"], b.g + 1)
                        sp.dma_start(sums[bass.ds(b.g * WIDE * P, WIDE * P), :].rearrange("(t p) d -> p t d", p=P), out[b.h][:]
                                     ).then_inc(out_stored[b.h], 16)

                    def step(b, first, last):
                        if first:
                            load_numbers(b, True)
                            load_numbers(b.next(), True)
                            if not gathers:
                                load_rows(b, True)
                        if b.ahead > 1:
                            load_numbers(b.next().next(), False)
                        if not gathers and not last:
                            load_rows(b.next(), first)
                        if not first:
                            store(b.last())
                        if last:
                            store(b)

                    pipeline(sp, step)
                    for h in range(2):
                        sp.wait_ge(out_stored[h], 16 * IN_SLOT[h])

                if gathers:
                    @block.gpsimd
                    def _(pool):
                        def gather(b, early):
                            pool.wait_ge(s["columns"], b.g + 1)
                            if not early:
                                pool.wait_ge(s["agg"], b.g - 1)
                            pool.sem_inc(passed, 1)
                            for k in range(K):
                                pool.indirect_dma_start(in_rows[b.h][:, k, :], None, gathered_from,
                                                        bass.IndirectOffsetOnAxis(ap=index[b.h][:, k:k + 1], axis=0)
                                                        ).then_inc(rows_loaded[b.h], 16)

                        def step(b, first, last):
                            if first:
                                gather(b, True)
                            if not last:
                                gather(b.next(), first)

                        pipeline(pool, step)

                @block.tensor
                def _(pe):
                    def transposes(b, first):
                        if not first:
                            pe.wait_ge(s["columns"], b.g)
                        pe.wait_ge(s["numbers_f"], b.g + 1)
                        pe.sem_inc(pe_passed, 1)
                        for n in range(3 if gathers else 1):
                            source = weights[b.h][:] if n == 2 else numbers_f[:, n, :]
                            ins = nc.tensor.transpose(bank[2][:, n * K:(n + 1) * K], source, ident[0:K, 0:K])
                        ins.then_inc(s["numbers_psum"], 1)

                    def step(b, first, last):
                        if first:
                            transposes(b, True)
                            transposes(b.next(), False)
                        if b.ahead > 1:
                            transposes(b.next().next(), False)
                        if not first:
                            pe.wait_ge(s["out"], b.g)
                        pe.wait_ge(s["S"], b.g + 1)
                        pe.wait_ge(rows_loaded[b.h], (b.round + 1) * (16 * K if gathers else 16))
                        pe.sem_inc(pe_passed, 1)
                        for t in range(WIDE):
                            tiles = [k for k in (t - 1, t, t + 1) if k >= 0]
                            for k in tiles:
                                block_of = t - (k - 1)
                                ins = nc.tensor.matmul(sums_psum[:, t // 4, t % 4, :], S[b.h][:, k, block_of * P:(block_of + 1) * P],
                                                       in_rows[b.h][:, k, :], start=(k == tiles[0]), stop=(k == tiles[-1]))
                        ins.then_inc(s["agg"], 1)

                    pipeline(pe, step)

                @block.scalar
                def _(act):
                    def step(b, first, last):
                        act.wait_ge(out_stored[b.h], b.round * 16)
                        act.wait_ge(s["agg"], b.g + 1)
                        nc.scalar.activation(out[b.h][:].rearrange("p (b t) d -> p b t d", b=2), sums_psum, ACT.Copy).then_inc(s["out"], 1)

                    pipeline(act, step)

                @block.vector
                def _(dve):
                    links = Links(dve, s["link"], 2 * (6 if signed else 5 if gathers else 4))
                    link = links.link
                    dve.tensor_copy(band_at[:], band_from[:]).then_inc(s["link"], 1)
                    dve.wait_ge(s["link"], 1)
                    links.base = 1

                    def as_floats(b, first):
                        if not first:
                            dve.wait_ge(s["numbers_psum"], b.g)
                        dve.wait_ge(numbers_loaded[b.h], (b.round + 1) * (48 if gathers else 16))
                        n = 2 if gathers else 1
                        nc.vector.tensor_scalar(numbers_f[:, 0:n, :], numbers_i[b.h][:, 0:n, :], 1.0, None, ALU.mult).then_inc(s["numbers_f"], 1)

                    def take_columns(b, early):
                        if gathers and not early:
                            dve.wait_ge(rows_loaded[b.h], b.round * 16 * K)
                        dve.wait_ge(s["numbers_psum"], b.g + 1)
                        n = 3 if gathers else 1
                        link(nc.vector.tensor_scalar(columns[b.h][:, 0:n * K], bank[2][:, 0:n * K], 1.0, None, ALU.mult))
                        link(nc.vector.tensor_tensor(at[b.h][:], columns[b.h][:, 0:K], band_at[:], ALU.subtract))
                        link(nc.vector.tensor_scalar(band_at[:], band_at[:], float(WIDE * P), None, ALU.add))
                        if signed:
                            link(nc.vector.tensor_scalar(negative[:], columns[b.h][:, 2 * K:3 * K], 0.0, None, ALU.is_lt))
                            link(nc.vector.scalar_tensor_tensor(index[b.h][:], columns[b.h][:, K:2 * K], 2.0, negative[:], ALU.mult, ALU.add))
                        elif gathers:
                            link(nc.vector.tensor_scalar(index[b.h][:], columns[b.h][:, K:2 * K], 1.0, None, ALU.mult))
                        dve.sem_inc(s["columns"], 1)

                    def step(b, first, last):
                        if first:
                            as_floats(b, True)
                            take_columns(b, True)
                            as_floats(b.next(), False)
                            take_columns(b.next(), True)
                        if b.ahead > 1:
                            as_floats(b.next().next(), False)
                        if not first:
                            dve.wait_ge(s["agg"], b.g - 1)
                        for k in range(K):
                            low, high = (P if k == 0 else 0), {WIDE - 1: 2 * P, WIDE: P}.get(k, 3 * P)
                            here = (S[b.h][:, k, low:high], band[:, low:high], at[b.h][:, k:k + 1])
                            if gathers and not signed:
                                ins = nc.vector.tensor_scalar(*here, columns[b.h][:, 2 * K + k:2 * K + k + 1], ALU.is_equal, ALU.mult)
                            else:
                                ins = nc.vector.tensor_scalar(*here, None, ALU.is_equal)
                        link(ins)
                        dve.sem_inc(s["S"], 1)
                        if b.ahead > 1:
                            take_columns(b.next().next(), False)

                    pipeline(dve, step, links)

        def window_attention(tag, sums):
            with ExitStack() as c:
                s = c.enter_context(phase_semaphores(nc, tag, (
                    "numbers_f", "numbers_psum", "columns", "S", "agg", "out", "typed", "w", "score", "exp", "hw", "product",
                    "msg", "type_ids", "link", "numbers_loaded0", "numbers_loaded1", "feat_loaded0", "feat_loaded1",
                    "rows_loaded0", "rows_loaded1", "out_stored0", "out_stored1", "sp_passed")))
                numbers_loaded = [s[f"numbers_loaded{h}"] for h in range(2)]
                feat_loaded = [s[f"feat_loaded{h}"] for h in range(2)]
                rows_loaded = [s[f"rows_loaded{h}"] for h in range(2)]
                out_stored = [s[f"out_stored{h}"] for h in range(2)]

                def buf(name, shape, dt=f32, slots=2):
                    return [c.enter_context(nc.sbuf_tensor(f"{tag}{name}{h}", shape, dt)) for h in range(slots)]

                K = WINDOW_TILES
                TW = EDGE_TYPES * (F_EDGE + 1)
                numbers_i, numbers_f = buf("numbers_i", [K, 2, P], i32), buf("numbers_f", [K, 2, P], slots=1)[0]
                columns, at = buf("columns", [P, 2 * K]), buf("at", [P, K])
                src_index, dst_index = buf("src_index", [P, K], i32), buf("dst_index", [P, K], i32)
                h24_rows, h3_rows = buf("h24_rows", [P, K, 2 * D]), buf("h3_rows", [P, K, D])
                feat, types = buf("feat", [TW, WINDOW], slots=1)[0], buf("types", [TW, WINDOW], i32, slots=1)[0]
                typedT = buf("typedT", [TW, WINDOW], slots=1)[0]
                type_id_i, type_id = buf("type_id_i", [TW, 1], i32, slots=1)[0], buf("type_id", [TW, 1], slots=1)[0]
                S = buf("S", [P, K, 3 * P], slots=1)[0]
                product, msg = buf("product", [P, K, D], slots=1)[0], buf("msg", [P, K, D], slots=1)[0]
                score, top, below, exped, total, quotient, weight = [buf(f"number{n}_", [P, K], slots=1)[0] for n in range(7)]
                out = buf("out", [P, WIDE, D])
                band_at = buf("band_at", [P, K], slots=1)[0]
                sums_psum, numbers_psum = bank[4], bank[5]
                w_psum, w_last_psum = wide_bank[0], bank[2]
                block = c.enter_context(nc.Block())

                @block.sync
                def _(sp):
                    def load_numbers(b, early):
                        if not early:
                            sp.wait_ge(s["numbers_psum"], b.g - 1)
                        sp.sem_inc(s["sp_passed"], 1)
                        start = sp.value_load(starts[0:1, bass.ds(b.g * WIDE, 1)], min_val=0, max_val=ROWS)
                        window = bass.ds(start, WINDOW)
                        for n, name in enumerate(("dst_lin", "src_lin")):
                            sp.dma_start(numbers_i[b.h][:, n, :], io[name][window].rearrange("(k p) -> k p", p=P)).then_inc(numbers_loaded[b.h], 16)

                    def load_feat(b, early):
                        if not early:
                            sp.wait_ge(s["typed"], b.g)
                        sp.sem_inc(s["sp_passed"], 1)
                        start = sp.value_load(starts[0:1, bass.ds(b.g * WIDE, 1)], min_val=0, max_val=ROWS)
                        window = bass.ds(start, WINDOW)
                        sp.dma_start(feat[:], io["edge16_T"][:, window]).then_inc(feat_loaded[b.h], 16)
                        sp.dma_start(types[:], io["etype_lin"].unsqueeze(0)[:, window].to_broadcast([TW, WINDOW])).then_inc(feat_loaded[b.h], 16)

                    def store(b):
                        sp.wait_ge(s["out"], b.g + 1)
                        sp.dma_start(sums[bass.ds(b.g * WIDE * P, WIDE * P), :].rearrange("(t p) d -> p t d", p=P), out[b.h][:]
                                     ).then_inc(out_stored[b.h], 16)

                    def step(b, first, last):
                        if first:
                            load_numbers(b, True)
                            load_numbers(b.next(), True)
                            load_feat(b, True)
                        if b.ahead > 1:
                            load_numbers(b.next().next(), False)
                        if not last:
                            load_feat(b.next(), False)
                        if not first:
                            store(b.last())
                        if last:
                            store(b)

                    pipeline(sp, step)
                    for h in range(2):
                        sp.wait_ge(out_stored[h], 16 * IN_SLOT[h])

                @block.gpsimd
                def _(pool):
                    pool.iota(type_id_i[:], [[0, 1]], base=0, channel_multiplier=1).then_inc(s["type_ids"], 1)

                    def gather(b, early):
                        pool.wait_ge(s["columns"], b.g + 1)
                        if not early:
                            pool.wait_ge(s["product"], b.g - 1)
                        pool.sem_inc(passed, 1)
                        for k in range(K):
                            pool.indirect_dma_start(h24_rows[b.h][:, k, :], None, h24_t,
                                                    bass.IndirectOffsetOnAxis(ap=src_index[b.h][:, k:k + 1], axis=0)
                                                    ).then_inc(rows_loaded[b.h], 16)
                            pool.indirect_dma_start(h3_rows[b.h][:, k, :], None, h3_t,
                                                    bass.IndirectOffsetOnAxis(ap=dst_index[b.h][:, k:k + 1], axis=0)
                                                    ).then_inc(rows_loaded[b.h], 16)

                    def step(b, first, last):
                        if first:
                            gather(b, True)
                        if not last:
                            gather(b.next(), first)

                    pipeline(pool, step)

                @block.tensor
                def _(pe):
                    def transposes(b, first):
                        if not first:
                            pe.wait_ge(s["columns"], b.g)
                        pe.wait_ge(s["numbers_f"], b.g + 1)
                        pe.sem_inc(pe_passed, 1)
                        for n in range(2):
                            ins = nc.tensor.transpose(numbers_psum[:, n * K:(n + 1) * K], numbers_f[:, n, :], ident[0:K, 0:K])
                        ins.then_inc(s["numbers_psum"], 1)

                    def features(b, first):
                        if not first:
                            pe.wait_ge(s["hw"], b.g)
                        pe.wait_ge(s["typed"], b.g + 1)
                        pe.sem_inc(pe_passed, 1)
                        for k in range(K):
                            to = w_psum[:, k * 2 * D:(k + 1) * 2 * D] if k < WIDE else w_last_psum[:, 0:2 * D]
                            ins = nc.tensor.matmul(to, typedT[:, k * P:(k + 1) * P], W5[:].rearrange("p a d -> p (a d)"), start=True, stop=True)
                        ins.then_inc(s["w"], 1)

                    def step(b, first, last):
                        if first:
                            transposes(b, True)
                            transposes(b.next(), False)
                            features(b, True)
                        if b.ahead > 1:
                            transposes(b.next().next(), False)
                        if not last:
                            features(b.next(), False)
                        if not first:
                            pe.wait_ge(s["out"], b.g)
                        pe.wait_ge(s["S"], b.g + 1)
                        pe.wait_ge(s["msg"], b.g + 1)
                        pe.sem_inc(pe_passed, 1)
                        for t in range(WIDE):
                            tiles = [k for k in (t - 1, t, t + 1) if k >= 0]
                            for k in tiles:
                                block_of = t - (k - 1)
                                ins = nc.tensor.matmul(sums_psum[:, t * D:(t + 1) * D], S[:, k, block_of * P:(block_of + 1) * P],
                                                       msg[:, k, :], start=(k == tiles[0]), stop=(k == tiles[-1]))
                        ins.then_inc(s["agg"], 1)

                    pipeline(pe, step)

                @block.scalar
                def _(act):
                    def step(b, first, last):
                        act.wait_ge(s["score"], b.g + 1)
                        nc.scalar.activation(exped[:], below[:], ACT.Exp).then_inc(s["exp"], 1)
                        act.wait_ge(out_stored[b.h], b.round * 16)
                        act.wait_ge(s["agg"], b.g + 1)
                        nc.scalar.activation(out[b.h][:], wide_rows(sums_psum), ACT.Copy).then_inc(s["out"], 1)

                    pipeline(act, step)

                @block.vector
                def _(dve):
                    links = Links(dve, s["link"], 2 * 12)
                    link = links.link
                    dve.wait_ge(s["type_ids"], 1)
                    link(dve.tensor_copy(type_id[:], type_id_i[:]))
                    link(dve.tensor_copy(band_at[:], band_from[:]))
                    link(dve.tensor_scalar(columns[0][0:TW, 0:1], type_id[:], float(F_EDGE), None, ALU.is_ge))
                    link(dve.tensor_scalar(columns[0][0:TW, 1:2], type_id[:], 2.0 * F_EDGE, None, ALU.is_ge))
                    link(dve.tensor_tensor(columns[0][0:TW, 2:3], columns[0][0:TW, 0:1], columns[0][0:TW, 1:2], ALU.add))
                    link(dve.tensor_scalar(columns[0][0:TW, 3:4], type_id[:], 3.0 * F_EDGE, None, ALU.is_ge))
                    link(dve.tensor_scalar(columns[0][0:TW, 4:5], type_id[:], -3.0 * F_EDGE - 2.0, None, ALU.add))
                    link(dve.tensor_tensor(columns[0][0:TW, 4:5], columns[0][0:TW, 4:5], columns[0][0:TW, 3:4], ALU.mult))
                    link(dve.tensor_tensor(type_id[:], columns[0][0:TW, 4:5], columns[0][0:TW, 2:3], ALU.add))

                    def as_floats(b, first):
                        if not first:
                            dve.wait_ge(s["numbers_psum"], b.g)
                        dve.wait_ge(numbers_loaded[b.h], (b.round + 1) * 32)
                        nc.vector.tensor_scalar(numbers_f[:], numbers_i[b.h][:], 1.0, None, ALU.mult).then_inc(s["numbers_f"], 1)

                    def take_columns(b, early):
                        if not early:
                            dve.wait_ge(rows_loaded[b.h], b.round * 32 * K)
                        dve.wait_ge(s["numbers_psum"], b.g + 1)
                        link(nc.vector.tensor_scalar(columns[b.h][:], numbers_psum[:, 0:2 * K], 1.0, None, ALU.mult))
                        link(nc.vector.tensor_tensor(at[b.h][:], columns[b.h][:, 0:K], band_at[:], ALU.subtract))
                        link(nc.vector.tensor_scalar(band_at[:], band_at[:], float(WIDE * P), None, ALU.add))
                        nc.vector.tensor_scalar(dst_index[b.h][:], columns[b.h][:, 0:K], float(ROWS - 1), None, ALU.min)
                        link(nc.vector.tensor_scalar(src_index[b.h][:], columns[b.h][:, K:2 * K], 1.0, None, ALU.mult))
                        dve.sem_inc(s["columns"], 1)

                    def by_type(b, first):
                        if not first:
                            dve.wait_ge(s["w"], b.g)
                        dve.wait_ge(feat_loaded[b.h], (b.round + 1) * 32)
                        nc.vector.scalar_tensor_tensor(typedT[:], types[:], type_id[:, 0:1], feat[:], ALU.is_equal, ALU.mult).then_inc(s["typed"], 1)

                    def step(b, first, last):
                        if first:
                            as_floats(b, True)
                            take_columns(b, True)
                            as_floats(b.next(), False)
                            take_columns(b.next(), True)
                            by_type(b, True)
                        if b.ahead > 1:
                            as_floats(b.next().next(), False)
                        if not first:
                            dve.wait_ge(s["agg"], b.g)
                        for k in range(K):
                            low, high = (P if k == 0 else 0), {WIDE - 1: 2 * P, WIDE: P}.get(k, 3 * P)
                            ins = nc.vector.tensor_scalar(S[:, k, low:high], band[:, low:high], at[b.h][:, k:k + 1], None, ALU.is_equal)
                        ins.then_inc(s["S"], 1)
                        dve.wait_ge(rows_loaded[b.h], (b.round + 1) * 32 * K)
                        dve.wait_ge(s["w"], b.g + 1)
                        h24 = h24_rows[b.h]
                        nc.vector.tensor_tensor(h24[:, 0:WIDE, :], h24[:, 0:WIDE, :], wide_rows(w_psum, 2 * D), ALU.add)
                        nc.vector.tensor_tensor(h24[:, WIDE, :], h24[:, WIDE, :], w_last_psum[:, 0:2 * D], ALU.add).then_inc(s["hw"], 1)
                        dve.wait_ge(s["hw"], b.g + 1)
                        link(nc.vector.tensor_tensor(product[:], h3_rows[b.h][:], h24[:, :, D:2 * D], ALU.mult))
                        if not last:
                            by_type(b.next(), False)
                        link(nc.vector.tensor_reduce(score[:], product[:], AX.X, ALU.add))
                        link(nc.vector.tensor_scalar(weight[:], score[:], HEAD_DIM ** -0.5, None, ALU.mult))
                        link(nc.vector.tensor_reduce(top[:], weight[:].unsqueeze(2), AX.X, ALU.max))
                        nc.vector.tensor_tensor(below[:], weight[:], top[:], ALU.subtract).then_inc(s["score"], 1)
                        if b.ahead > 1:
                            take_columns(b.next().next(), False)
                        dve.wait_ge(s["exp"], b.g + 1)
                        link(nc.vector.tensor_reduce(total[:], exped[:].unsqueeze(2), AX.X, ALU.add))
                        link(nc.vector.reciprocal(quotient[:], total[:]))
                        link(nc.vector.tensor_tensor(weight[:], exped[:], quotient[:], ALU.mult))
                        link(nc.vector.tensor_tensor(msg[:], h24[:, :, 0:D], weight[:].unsqueeze(2).to_broadcast([P, K, D]), ALU.mult))
                        dve.sem_inc(s["msg"], 1)
                        dve.sem_inc(s["product"], 1)

                    pipeline(dve, step, links)

        def by_order(in_order, in_any_order):
            with nc.If(is_sorted == 1):
                nc.all_engine_barrier()
                in_order()
                nc.all_engine_barrier()
            with nc.Else():
                nc.all_engine_barrier()
                in_any_order()
                nc.all_engine_barrier()

        def edge_messages(tag, in_order):
            indices = TILES if in_order else 2 * TILES
            with ExitStack() as c:
                s = c.enter_context(phase_semaphores(nc, tag, (
                    "idx_f", "wide", "same", "scat_idx", "transposed", "in_T", "hidden", "hidden_T",
                    "out", "msg", "sums", "rows", "rows_free", "link", "ones_set", "msg_stored0", "msg_stored1")))
                msg_stored = [s["msg_stored0"], s["msg_stored1"]]
                (idx, cat, side, extra, feat, scat_idx, rows_a, rows_b, idx_f, gidx,
                 same, masked, small, msg, typed, catT, sideT, hiddenT, work, hw) = edge_buffers(c, tag)
                msg = [c.enter_context(nc.sbuf_tensor(f"{tag}messages{h}", [P, TILES, D_RECV], f32)) for h in range(2)]
                block = c.enter_context(nc.Block())

                @block.sync
                def _(sp):
                    def load(h, it):
                        sp.wait_ge(in_free[h], it + free_at)
                        sp.dma_start(idx[h][:], io["idx"][bass.ds((it * 2 + h) * P, P), :]).then_inc(idx_loaded[h], 16)
                        sp.dma_start(cat[h][:, :, 0:D], group_of(io["edge64"], it * 2 + h)).then_inc(loaded[h], 16)

                    def store(h, it):
                        if in_order:
                            sp.wait_ge(s["msg"], (it * 2 + h) * 2 + 2)
                            sp.dma_start(group_of(messages_t, it * 2 + h, D_RECV), msg[h][:]).then_inc(msg_stored[h], 16)

                    for h in range(2):
                        load(h, 0)
                    with sp.Fori(0, STEPS - 1, 1) as it:
                        for h in range(2):
                            load(h, it + 1)
                            store(h, it)
                    for h in range(2):
                        store(h, STEPS - 1)
                    if in_order:
                        for h in range(2):
                            sp.wait_ge(msg_stored[h], STEPS * 16)

                @block.gpsimd
                def _(pool):
                    def gather(t, h, it):
                        pool.wait_ge(idx_loaded[h], it * 16 + 16 + idx_at)
                        pool.sem_inc(passed, 1)
                        pool.indirect_dma_start(cat[h][:, t, D:2 * D], None, io["x"],
                                                bass.IndirectOffsetOnAxis(ap=idx[h][:, t:t + 1], axis=0)
                                                ).then_inc(gath_a[h][t], 16)
                        pool.indirect_dma_start(side[h][:, t, 0:D], None, io["x"],
                                                bass.IndirectOffsetOnAxis(ap=idx[h][:, TILES + t:TILES + t + 1], axis=0)
                                                ).then_inc(gath_b[h][t], 16)

                    def scatter(t, h, g):
                        k = t % 2
                        pool.wait_ge(sent_done[k], g * (16 * TILES // 2) + 16 * (t // 2))
                        if t == 0:
                            pool.wait_ge(s["scat_idx"], g + 1)
                            pool.wait_ge(s["rows"], g + 1)
                        if not in_order:
                            pool.wait_ge(recv_done, g * (16 * TILES) + 16 * t)
                        if t == 1:
                            pool.sem_inc(s["rows_free"], 1)
                        pool.sem_inc(passed, 1)
                        pool.indirect_dma_start(sent_sum[k], bass.IndirectOffsetOnAxis(ap=scat_idx[h][:, t:t + 1], axis=0),
                                                rows_b[h][:, t, :], None, compute_op=ALU.add
                                                ).then_inc(sent_done[k], 16)
                        if not in_order:
                            pool.indirect_dma_start(recv_sum, bass.IndirectOffsetOnAxis(ap=scat_idx[h][:, TILES + t:TILES + t + 1], axis=0),
                                                    rows_a[h][:, t, :], None, compute_op=ALU.add
                                                    ).then_inc(recv_done, 16)

                    for t in range(TILES):
                        gather(t, 0, 0)
                    for t in range(TILES):
                        gather(t, 1, 0)
                    pool.wait_ge(cleared, 2 * 96 + (16 if in_order else 96))
                    with pool.Fori(0, STEPS - 1, 1) as it:
                        for h in range(2):
                            for t in range(TILES):
                                gather(t, h, it + 1)
                                scatter(t, h, it * 2 + h)
                    for h in range(2):
                        for t in range(TILES):
                            scatter(t, h, GROUPS - 2 + h)
                    for k in range(2):
                        pool.wait_ge(sent_done[k], GROUPS * TILES // 2 * 16)
                    if not in_order:
                        pool.wait_ge(recv_done, GROUPS * TILES * 16)
                    pool.wait_ge(cleared_later, (3 if in_order else 6) * 96)

                @block.vector
                def _(dve):
                    n = indices
                    for h in range(2):
                        dve.memset(msg[h][:, :, ONE_COL:ONE_COL + 1], 1.0).then_inc(s["ones_set"], 1)
                    dve.wait_ge(ready, 6)
                    with dve.Fori(0, STEPS, 1) as it:
                        link, end = linker(dve, s["link"], it, 10 if in_order else 12)
                        for h in range(2):
                            g = it * 2 + h
                            dve.wait_ge(s["wide"], g)
                            dve.wait_ge(s["scat_idx"], g)
                            dve.wait_ge(idx_loaded[h], it * 16 + 16 + idx_at)
                            nc.vector.tensor_copy(idx_f[:], idx[h][:]).then_inc(s["idx_f"], 1)
                            dve.wait_ge(s["sums"], g)
                            if in_order:
                                dve.wait_ge(msg_stored[h], it * 16)
                            nc.vector.tensor_scalar(msg[h][:, :, EW_COL], ew_all[:, bass.ds(g * TILES, TILES)], 1.0, None, ALU.mult
                                                    ).then_inc(s["msg"], 1)
                            dve.wait_ge(s["idx_f"], g + 1)
                            dve.wait_ge(s["wide"], g + 1)
                            link(nc.vector.tensor_tensor(
                                same[:, 0:n, :], wide_bank[0][:, 0:n * P].rearrange("p (t j) -> p t j", t=n),
                                idx_f[:, 0:n].unsqueeze(2).to_broadcast([P, n, P]), ALU.is_equal))
                            dve.sem_inc(s["same"], 1)
                            link(nc.vector.tensor_tensor(masked[:, 0:n, :], same[:, 0:n, :], earlier[:].unsqueeze(1).to_broadcast([P, n, P]), ALU.mult))
                            link(nc.vector.tensor_reduce(small[0][:, 0:n], masked[:, 0:n, :], AX.X, ALU.add))
                            link(nc.vector.tensor_scalar(small[1][:, 0:n], idx_f[:, 0:n], dump_row[:, 0:1], -1.0, ALU.subtract, ALU.mult))
                            link(nc.vector.scalar_tensor_tensor(small[2][:, 0:n], small[0][:, 0:n], 1.0, small[1][:, 0:n], ALU.min, ALU.mult))
                            dve.wait_ge(s["out"], g + 1)
                            nc.vector.tensor_tensor(msg[h][:, :, 0:D], bank[5][:, 0:TILES * D].rearrange("p (t d) -> p t d", t=TILES),
                                                    be2[:].unsqueeze(1).to_broadcast([P, TILES, D]), ALU.add).then_inc(s["msg"], 1)
                            dve.wait_ge(s["rows_free"], g)
                            if not in_order:
                                link(nc.vector.tensor_tensor(recv_all[:, bass.ds(g * TILES, TILES)], small[2][:, TILES:2 * TILES],
                                                             idx_f[:, TILES:2 * TILES], ALU.add))
                            nc.vector.tensor_tensor(scat_idx[h][:, 0:n], small[2][:, 0:n], idx_f[:, 0:n], ALU.add).then_inc(s["scat_idx"], 1)
                        end()

                @block.tensor
                def _(pe):
                    pe.wait_ge(ready, 6)
                    pe.wait_ge(s["ones_set"], 2)
                    with pe.Fori(0, STEPS, 1) as it:
                        for h in range(2):
                            g = it * 2 + h
                            pe.wait_ge(s["same"], g)
                            pe.wait_ge(s["idx_f"], g + 1)
                            for k in range(indices):
                                last = nc.tensor.transpose(wide_bank[0][:, k * P:(k + 1) * P], idx_f[:, k:k + 1].to_broadcast([P, P]), ident[:])
                            last.then_inc(s["wide"], 1)
                            pe.wait_ge(s["in_T"], g)
                            pe.wait_ge(loaded[h], it * 16 + 16 + loaded_at[h])
                            for t in range(TILES):
                                pe.wait_ge(gath_a[h][t], it * 16 + 16)
                                pe.wait_ge(gath_b[h][t], it * 16 + 16)
                                pe.wait_ge(ready, 6)
                                nc.tensor.transpose(bank[2][:, t * P:(t + 1) * P], cat[h][:, t, :], ident[:])
                                last = nc.tensor.transpose(bank[3][0:D, t * P:(t + 1) * P], side[h][:, t, 0:D], ident[:])
                            last.then_inc(s["transposed"], 1)
                            pe.wait_ge(s["transposed"], g + 1)
                            pe.sem_inc(in_free[h], 1)
                            pe.wait_ge(s["in_T"], g + 1)
                            nc.tensor.matmul(bank[4][:], We1a[:], catT[:], start=True, stop=False)
                            nc.tensor.matmul(bank[4][:], We1b[:], sideT[0:D, :], start=False, stop=True).then_inc(s["hidden"], 1)
                            pe.wait_ge(s["hidden_T"], g + 1)
                            for t in range(TILES):
                                last = nc.tensor.matmul(bank[5][:, t * D:(t + 1) * D], hiddenT[:, t * P:(t + 1) * P], We2[:], start=True, stop=True)
                            last.then_inc(s["out"], 1)
                            pe.wait_ge(s["rows"], g)
                            pe.wait_ge(s["same"], g + 1)
                            pe.wait_ge(s["msg"], g * 2 + 2)
                            for t in range(TILES):
                                last = nc.tensor.matmul(bank[6][:, t * D:(t + 1) * D], same[:, t, :], msg[h][:, t, 0:D], start=True, stop=True)
                                if not in_order:
                                    last = nc.tensor.matmul(bank[7][:, t * D_RECV:(t + 1) * D_RECV], same[:, TILES + t, :], msg[h][:, t, :], start=True, stop=True)
                            last.then_inc(s["sums"], 1)

                @block.scalar
                def _(act):
                    if in_order:
                        act.dma_start(messages_t[ROWS:ROWS + WINDOW, :].rearrange("(p r) d -> p (r d)", p=P), zeros[:, 0:WINDOW_TILES * D_RECV]
                                      ).then_inc(cleared, 16)
                        for tab in (conv_sum[1], attn_sum[1], sign_sum[1]):
                            clear(act, tab, cleared_later)
                    else:
                        clear(act, recv_sum, cleared)
                        for tab in conv_sum + attn_sum + sign_sum:
                            clear(act, tab, cleared_later)
                    with act.Fori(0, STEPS, 1) as it:
                        for h in range(2):
                            g = it * 2 + h
                            act.wait_ge(s["hidden"], g)
                            act.wait_ge(s["transposed"], g + 1)
                            nc.scalar.activation(catT[:], bank[2][:], ACT.Copy)
                            nc.scalar.activation(sideT[0:D, :], bank[3][0:D, :], ACT.Copy).then_inc(s["in_T"], 1)
                            act.wait_ge(s["out"], g)
                            act.wait_ge(s["hidden"], g + 1)
                            nc.scalar.activation(hiddenT[:], bank[4][:], ACT.Relu, bias=be1[:, 0:1]).then_inc(s["hidden_T"], 1)
                            act.wait_ge(s["rows_free"], g)
                            act.wait_ge(s["sums"], g + 1)
                            if not in_order:
                                nc.scalar.activation(rows_a[h][:], bank[7][:, 0:TILES * D_RECV].rearrange("p (t d) -> p t d", t=TILES), ACT.Copy)
                            nc.scalar.activation(rows_b[h][:], bank[6][:, 0:TILES * D].rearrange("p (t d) -> p t d", t=TILES), ACT.Copy
                                                 ).then_inc(s["rows"], 1)

        def layer_0_in_order():
            edge_messages("m0_", in_order=True)
            window_sums("w0_", messages_t, recv_sum, D_RECV)

        by_order(layer_0_in_order, lambda: edge_messages("e0_", in_order=False))
        gathers_a += STEPS * 16
        gathers_b += STEPS * 16
        idx_at += STEPS * 16
        loaded_at = [at + STEPS * 16 for at in loaded_at]
        free_at += STEPS

        def wide_buffers(c, tag):
            def rows(name, width=D, slots=None):
                def one(n):
                    return c.enter_context(nc.sbuf_tensor(tag + n, [P, WIDE, width], f32))
                return one(name) if slots is None else [one(f"{name}{h}") for h in range(slots)]

            def numbers(*names):
                return [c.enter_context(nc.sbuf_tensor(tag + n, [P, WIDE], f32)) for n in names]
            return rows, numbers

        def per_row(numbers):
            return numbers.unsqueeze(2).to_broadcast([P, WIDE, D])

        def wide_rows(flat, width=D):
            return flat[:, 0:WIDE * width].rearrange("p (t d) -> p t d", t=WIDE)

        class Norm:

            def __init__(self, rows, numbers):
                self.centred, self.square = rows("centred"), rows("square")
                self.total, self.mean, self.sum_sq, self.var, self.std, self.rstd = numbers(
                    "total", "mean", "sum_sq", "var", "std", "rstd")

            def centre(self, link, v, centred):
                link(nc.vector.tensor_reduce(self.total[:], v, AX.X, ALU.add))
                link(nc.vector.tensor_scalar(self.mean[:], self.total[:], 1.0 / D, None, ALU.mult))
                nc.vector.tensor_tensor(self.centred[:], v, per_row(self.mean[:]), ALU.subtract).then_inc(centred, 1)

            def variance(self, dve, link, g, square, var):
                dve.wait_ge(square, g + 1)
                link(nc.vector.tensor_reduce(self.sum_sq[:], self.square[:], AX.X, ALU.add))
                nc.vector.tensor_scalar(self.var[:], self.sum_sq[:], 1.0 / D, LN_EPS, ALU.mult, ALU.add).then_inc(var, 1)

            def scale(self, dve, link, out, g, std, done):
                dve.wait_ge(std, g + 1)
                link(nc.vector.reciprocal(self.rstd[:], self.std[:]))
                nc.vector.tensor_tensor(out, self.centred[:], per_row(self.rstd[:]), ALU.mult).then_inc(done, 1)

            def act_square(self, act, g, centred, square):
                act.wait_ge(centred, g + 1)
                nc.scalar.activation(self.square[:], self.centred[:], ACT.Square).then_inc(square, 1)

            def act_root(self, act, g, var, std):
                act.wait_ge(var, g + 1)
                nc.scalar.activation(self.std[:], self.var[:], ACT.Sqrt).then_inc(std, 1)

        with ExitStack() as c:
            s = c.enter_context(phase_semaphores(nc, "n0_", (
                "transposed", "in_T", "hidden", "hidden_T", "out", "x1", "y1", "biased", "deg", "root_deg",
                "dis", "centred", "square", "var", "std", "link", "pool_link")))
            rows, numbers = wide_buffers(c, "n0_")
            norm = Norm(rows, numbers)
            inp = rows("in", 2 * D, 2)
            received = rows("received", D + D_RECV, 2)
            biased, x1, y1 = rows("biased", D, 2), rows("x1_", D, 2), rows("y1_", D, 2)
            v = rows("v")
            degree, kept, not_positive, safe, root, rroot, at_least_1, positive = numbers(
                "degree", "kept", "not_positive", "safe", "root", "rroot", "at_least_1", "positive")
            dis = numbers("dis0", "dis1")
            inT = c.enter_context(nc.sbuf_tensor("n0_inT", [P, WIDE * P], f32))
            receivedT = c.enter_context(nc.sbuf_tensor("n0_receivedT", [P, WIDE * P], f32))
            hidT = c.enter_context(nc.sbuf_tensor("n0_hidT", [HID, WIDE * P], f32))
            in_psum, received_psum, hid_psum, out_psum = wide_bank[0], wide_bank[1], wide_bank[2], bank[6]
            block = c.enter_context(nc.Block())

            @block.sync
            def _(sp):
                def load(b, early):
                    if not early:
                        sp.wait_ge(s["biased"], b.g - 1)
                        sp.wait_ge(s["transposed"], b.g - 1)
                        sp.wait_ge(s["dis"], b.g - 1)
                    sp.dma_start(inp[b.h][:, :, 0:D], wide_group_of(io["x"], b.g)).then_inc(loaded[b.h], 16)
                    sp.dma_start(inp[b.h][:, :, D:2 * D], wide_group_of(sent_sum[0], b.g)).then_inc(loaded[b.h], 16)
                    sp.dma_start(received[b.h][:, :, 0:D], wide_group_of(sent_sum[1], b.g)).then_inc(loaded[b.h], 16)
                    sp.dma_start(received[b.h][:, :, D:D + D_RECV], wide_group_of(recv_sum, b.g, D_RECV)).then_inc(loaded[b.h], 16)

                def store(b):
                    sp.wait_ge(s["y1"], b.g + 1)
                    sp.dma_start(wide_group_of(y1_t, b.g), y1[b.h][:]).then_inc(stored[b.h], 16)

                def step(b, first, last):
                    if first:
                        load(b, True)
                    if not last:
                        load(b.next(), first)
                    if not first:
                        store(b.last())
                    if last:
                        store(b)

                pipeline(sp, step)
                for h in range(2):
                    sp.wait_ge(stored[h], stored_at[h] + 16 * IN_SLOT[h])

            @block.tensor
            def _(pe):
                def transposes(b, first):
                    if not first:
                        pe.wait_ge(s["in_T"], b.g)
                    pe.wait_ge(loaded[b.h], b.round * 64 + 64 + loaded_at[b.h])
                    pe.sem_inc(pe_passed, 1)
                    for t in range(WIDE):
                        nc.tensor.transpose(in_psum[:, t * P:(t + 1) * P], inp[b.h][:, t, :], ident[:])
                        last = nc.tensor.transpose(received_psum[:, t * P:(t + 1) * P], received[b.h][:, t, 0:2 * D], ident[:])
                    last.then_inc(s["transposed"], 1)

                def hidden(b, first):
                    if not first:
                        pe.wait_ge(s["hidden_T"], b.g)
                    pe.wait_ge(s["in_T"], b.g + 1)
                    for half in range(2):
                        cols = slice(half * 4 * P, (half + 1) * 4 * P)
                        nc.tensor.matmul(hid_psum[:, cols], Wn1a[:], inT[:, cols], start=True, stop=False)
                        last = nc.tensor.matmul(hid_psum[:, cols], Wn1b[:], receivedT[:, cols], start=False, stop=True)
                    last.then_inc(s["hidden"], 1)

                def step(b, first, last):
                    if first:
                        transposes(b, True)
                        hidden(b, True)
                    if not last:
                        transposes(b.next(), False)
                    if not first:
                        pe.wait_ge(s["centred"], b.g)
                    pe.wait_ge(s["hidden_T"], b.g + 1)
                    for t in range(WIDE):
                        out = nc.tensor.matmul(out_psum[:, t * D:(t + 1) * D], hidT[:, t * P:(t + 1) * P], Wn2[:], start=True, stop=True)
                    out.then_inc(s["out"], 1)
                    if not last:
                        hidden(b.next(), False)

                pipeline(pe, step)

            @block.scalar
            def _(act):
                def inputs(b, first):
                    if not first:
                        act.wait_ge(s["hidden"], b.g)
                    act.wait_ge(s["transposed"], b.g + 1)
                    nc.scalar.activation(inT[:], in_psum[:], ACT.Copy)
                    nc.scalar.activation(receivedT[:], received_psum[:], ACT.Copy).then_inc(s["in_T"], 1)

                def degree_root(b):
                    act.wait_ge(s["deg"], b.g + 1)
                    nc.scalar.activation(root[:], safe[:], ACT.Sqrt).then_inc(s["root_deg"], 1)

                def relu(b, first):
                    if not first:
                        act.wait_ge(s["out"], b.g)
                    act.wait_ge(s["hidden"], b.g + 1)
                    nc.scalar.activation(hidT[:], hid_psum[:], ACT.Relu, bias=bn1[:, 0:1]).then_inc(s["hidden_T"], 1)

                def step(b, first, last):
                    if first:
                        inputs(b, True)
                        degree_root(b)
                        relu(b, True)
                    if not last:
                        inputs(b.next(), False)
                    norm.act_square(act, b.g, s["centred"], s["square"])
                    if not last:
                        degree_root(b.next())
                    norm.act_root(act, b.g, s["var"], s["std"])
                    if not last:
                        relu(b.next(), False)

                pipeline(act, step)

            @block.gpsimd
            def _(pool):
                links = Links(pool, s["pool_link"], 2, passed)

                def double(b, first):
                    if not first:
                        pool.wait_ge(s["centred"], b.g - 1)
                    pool.wait_ge(loaded[b.h], b.round * 64 + 64 + loaded_at[b.h])
                    pool.sem_inc(passed, 1)
                    links.link(pool.tensor_scalar(biased[b.h][:], inp[b.h][:, :, 0:D], 2.0, None, ALU.mult))
                    pool.tensor_tensor(biased[b.h][:], biased[b.h][:], bn2[:].unsqueeze(1).to_broadcast([P, WIDE, D]), ALU.add
                                       ).then_inc(s["biased"], 1)

                def step(b, first, last):
                    if first:
                        double(b, True)
                    if not last:
                        double(b.next(), False)
                    pool.wait_ge(s["dis"], b.g + 1)
                    pool.wait_ge(s["x1"], b.g + 1)
                    pool.sem_inc(passed, 1)
                    pool.tensor_copy(x_all[:, b.tiles, :], x1[b.h][:])
                    pool.wait_ge(stored[b.h], b.round * 16 + stored_at[b.h])
                    pool.sem_inc(passed, 1)
                    pool.tensor_tensor(y1[b.h][:], x1[b.h][:], per_row(dis[b.h][:]), ALU.mult).then_inc(s["y1"], 1)

                pipeline(pool, step, links)

            @block.vector
            def _(dve):
                links = Links(dve, s["link"], 2 * 14)
                link = links.link

                def degrees(b):
                    deg, count = received[b.h][:, :, D + EW_COL], received[b.h][:, :, D + ONE_COL]
                    dve.wait_ge(loaded[b.h], b.round * 64 + 64 + loaded_at[b.h])
                    link(nc.vector.tensor_scalar(degree[:], deg, 1.0, None, ALU.add))
                    link(nc.vector.tensor_scalar(positive[:], degree[:], 0.0, None, ALU.is_gt))
                    link(nc.vector.tensor_tensor(kept[:], degree[:], positive[:], ALU.mult))
                    link(nc.vector.tensor_scalar(not_positive[:], positive[:], -1.0, 1.0, ALU.mult, ALU.add))
                    nc.vector.tensor_tensor(safe[:], kept[:], not_positive[:], ALU.add).then_inc(s["deg"], 1)
                    link(nc.vector.tensor_scalar(at_least_1[:], count, 1.0, None, ALU.max))
                    link(nc.vector.reciprocal(rcount_all[:, b.tiles], at_least_1[:]))

                def dis_of(b, first):
                    if not first:
                        dve.wait_ge(s["y1"], b.g - 1)
                    dve.wait_ge(s["root_deg"], b.g + 1)
                    link(nc.vector.reciprocal(rroot[:], root[:]))
                    link(nc.vector.tensor_tensor(dis[b.h][:], rroot[:], positive[:], ALU.mult))
                    link(nc.vector.tensor_copy(dis_all[:, b.tiles], dis[b.h][:]))
                    dve.sem_inc(s["dis"], 1)

                def step(b, first, last):
                    if first:
                        degrees(b)
                        dis_of(b, True)
                    dve.wait_ge(s["biased"], b.g + 1)
                    dve.wait_ge(s["out"], b.g + 1)
                    link(nc.vector.tensor_tensor(v[:], biased[b.h][:], wide_rows(out_psum), ALU.add))
                    norm.centre(link, v[:], s["centred"])
                    if not last:
                        degrees(b.next())
                    norm.variance(dve, link, b.g, s["square"], s["var"])
                    if not last:
                        dis_of(b.next(), False)
                    norm.scale(dve, link, x1[b.h][:], b.g, s["std"], s["x1"])

                pipeline(dve, step, links)
        loaded_at = [loaded_at[h] + IN_SLOT[h] * 64 for h in range(2)]
        stored_at = [stored_at[h] + IN_SLOT[h] * 16 for h in range(2)]

        def tiled(flat, width, tiles=TILES):
            return flat[:, 0:tiles * width].rearrange("p (t d) -> p t d", t=tiles)

        def edge_sums(tag, gathered_from, sums, signed):
            before, adds_before = gathers_a, adds
            with ExitStack() as c:
                s = c.enter_context(phase_semaphores(nc, tag, (
                    "idx_f", "wide", "same", "gidx", "scat_idx", "msg", "sums", "rows", "rows_free", "link")))
                (idx, cat, side, extra, feat, scat_idx, rows_a, rows_b, idx_f, gidx,
                 same, masked, small, msg, typed, catT, sideT, hiddenT, work, hw) = edge_buffers(c, tag)
                block = c.enter_context(nc.Block())

                @block.sync
                def _(sp):
                    with sp.Fori(0, STEPS, 1) as it:
                        for h in range(2):
                            g = it * 2 + h
                            sp.wait_ge(in_free[h], it + free_at)
                            sp.dma_start(idx[h][:], io["idx"][bass.ds(g * P, P), :]).then_inc(idx_loaded[h], 16)

                @block.gpsimd
                def _(pool):
                    def gather(t, h, it):
                        if t == 0 and signed:
                            pool.wait_ge(s["gidx"], it * 2 + h + 1)
                        pool.wait_ge(idx_loaded[h], it * 16 + 16 + idx_at)
                        pool.sem_inc(passed, 1)
                        index = gidx[h] if signed else idx[h]
                        pool.indirect_dma_start(cat[h][:, t, 0:D], None, gathered_from,
                                                bass.IndirectOffsetOnAxis(ap=index[:, t:t + 1], axis=0)
                                                ).then_inc(gath_a[h][t], 16)

                    def scatter(t, h, g):
                        k = t % 2
                        pool.wait_ge(added[k], g * (16 * TILES // 2) + 16 * (t // 2) + adds_before)
                        if t == 0:
                            pool.wait_ge(s["scat_idx"], g + 1)
                            pool.wait_ge(s["rows"], g + 1)
                        if t == 1:
                            pool.sem_inc(s["rows_free"], 1)
                        pool.sem_inc(passed, 1)
                        pool.indirect_dma_start(sums[k], bass.IndirectOffsetOnAxis(ap=scat_idx[h][:, t:t + 1], axis=0),
                                                rows_b[h][:, t, :], None, compute_op=ALU.add).then_inc(added[k], 16)

                    for t in range(TILES):
                        gather(t, 0, 0)
                    with pool.Fori(0, STEPS - 1, 1) as it:
                        for t in range(TILES):
                            gather(t, 1, it)
                            scatter(t, 0, it * 2)
                        for t in range(TILES):
                            gather(t, 0, it + 1)
                            scatter(t, 1, it * 2 + 1)
                    for t in range(TILES):
                        gather(t, 1, STEPS - 1)
                        scatter(t, 0, GROUPS - 2)
                    for t in range(TILES):
                        scatter(t, 1, GROUPS - 1)
                    for k in range(2):
                        pool.wait_ge(added[k], GROUPS * TILES * 8 + adds_before)

                @block.vector
                def _(dve):
                    with dve.Fori(0, STEPS, 1) as it:
                        link, end = linker(dve, s["link"], it, 2 if signed else 0)
                        for h in range(2):
                            g = it * 2 + h
                            cols = bass.ds(g * TILES, TILES)
                            dve.wait_ge(s["wide"], g)
                            dve.wait_ge(s["same"], g)
                            if signed:
                                dve.wait_ge(s["gidx"], g)
                            dve.wait_ge(idx_loaded[h], it * 16 + 16 + idx_at)
                            nc.vector.tensor_copy(idx_f[:], idx[h][:]).then_inc(s["idx_f"], 1)
                            if signed:
                                link(nc.vector.tensor_scalar(small[0][:, 0:TILES], ew_all[:, cols], 0.0, None, ALU.is_lt))
                                dve.wait_ge(s["idx_f"], g + 1)
                                nc.vector.scalar_tensor_tensor(gidx[h][:], idx_f[:, 0:TILES], 2.0, small[0][:, 0:TILES], ALU.mult, ALU.add
                                                               ).then_inc(s["gidx"], 1)
                            dve.wait_ge(s["idx_f"], g + 1)
                            dve.wait_ge(s["sums"], g)
                            dve.wait_ge(s["wide"], g + 1)
                            nc.vector.tensor_tensor(same[:, 0:TILES, :], tiled(bank[g_wide], P),
                                                    idx_f[:, TILES:2 * TILES].unsqueeze(2).to_broadcast([P, TILES, P]), ALU.is_equal
                                                    ).then_inc(s["same"], 1)
                            dve.wait_ge(s["rows_free"], g)
                            nc.vector.tensor_scalar(scat_idx[h][:, 0:TILES], recv_all[:, cols], 1.0, None, ALU.mult).then_inc(s["scat_idx"], 1)
                            if not signed:
                                for t in range(TILES):
                                    dve.wait_ge(gath_a[h][t], it * 16 + 16 + before)
                                nc.vector.tensor_tensor(msg[:, :, 0:D], cat[h][:, :, 0:D], over_features(ew_all[:, cols]), ALU.mult
                                                        ).then_inc(s["msg"], 1)
                        end()

                @block.tensor
                def _(pe):
                    with pe.Fori(0, STEPS, 1) as it:
                        for h in range(2):
                            g = it * 2 + h
                            pe.wait_ge(s["same"], g)
                            pe.wait_ge(s["idx_f"], g + 1)
                            for t in range(TILES):
                                last = nc.tensor.transpose(bank[g_wide][:, t * P:(t + 1) * P],
                                                           idx_f[:, TILES + t:TILES + t + 1].to_broadcast([P, P]), ident[:])
                            last.then_inc(s["wide"], 1)
                            pe.wait_ge(s["rows"], g)
                            if signed:
                                for t in range(TILES):
                                    pe.wait_ge(gath_a[h][t], it * 16 + 16 + before)
                            else:
                                pe.wait_ge(s["msg"], g + 1)
                            pe.wait_ge(s["same"], g + 1)
                            for t in range(TILES):
                                rows = cat[h][:, t, 0:D] if signed else msg[:, t, 0:D]
                                last = nc.tensor.matmul(bank[6][:, t * D:(t + 1) * D], same[:, t, :], rows, start=True, stop=True)
                            last.then_inc(s["sums"], 1)
                            pe.wait_ge(s["sums"], g + 1)
                            pe.sem_inc(in_free[h], 1)

                @block.scalar
                def _(act):
                    with act.Fori(0, STEPS, 1) as it:
                        for h in range(2):
                            g = it * 2 + h
                            act.wait_ge(s["rows_free"], g)
                            act.wait_ge(s["sums"], g + 1)
                            nc.scalar.activation(rows_b[h][:], tiled(bank[6], D), ACT.Copy).then_inc(s["rows"], 1)

        g_wide = 0
        by_order(lambda: window_sums("w1_", None, conv_sum[0], D, gathered_from=y1_t),
                 lambda: edge_sums("e1_", y1_t, conv_sum, signed=False))
        gathers_a += STEPS * 16
        idx_at += STEPS * 16
        free_at += STEPS
        adds += GROUPS * TILES * 8

        with ExitStack() as c:
            s = c.enter_context(phase_semaphores(nc, "n1_", (
                "t", "t_psum", "t_T", "conv", "o", "neg", "exp", "x2", "onehot", "typed", "typed_psum", "typed_T",
                "proj", "h", "u", "centred", "square", "var", "log", "std", "link", "pool_link", "ones_set")))
            rows, numbers = wide_buffers(c, "n1_")
            norm = Norm(rows, numbers)
            sum0, sum1 = rows("sum0", D, 2), rows("sum1", D, 2)
            y, t_in, o, neg, exped, v = rows("y"), rows("t"), rows("o"), rows("neg"), rows("exped"), rows("v")
            x2 = rows("x2_", D, 2)
            x_typed = rows("x_typed", 2 * D)
            h_out = rows("h_out", 4 * D)
            ntype, log = numbers("ntype", "log")
            onehot = c.enter_context(nc.sbuf_tensor("n1_onehot", [P, WIDE, NODE_TYPES], f32))
            onehotT = c.enter_context(nc.sbuf_tensor("n1_onehotT", [WIDE * NODE_TYPES, P], f32))
            tT = c.enter_context(nc.sbuf_tensor("n1_tT", [D + 1, WIDE * P], f32))
            typedT = c.enter_context(nc.sbuf_tensor("n1_typedT", [P, WIDE * P], f32))
            t_psum, conv_psum, onehot_psum, typed_psum = wide_bank[0], bank[2], bank[3], wide_bank[2]
            pair_psum = bank[6:8]
            block = c.enter_context(nc.Block())

            @block.sync
            def _(sp):
                def load(b, early):
                    if not early:
                        sp.wait_ge(s["t"], b.g - 1)
                    sp.dma_start(sum0[b.h][:], wide_group_of(conv_sum[0], b.g)).then_inc(loaded[b.h], 16)
                    sp.dma_start(sum1[b.h][:], wide_group_of(conv_sum[1], b.g)).then_inc(loaded[b.h], 16)

                def step(b, first, last):
                    if first:
                        load(b, True)
                        load(b.next(), True)
                    if b.ahead > 1:
                        load(b.next().next(), False)
                    for half in range(2):
                        tiles = slice(half * 4, half * 4 + 4)
                        sp.wait_ge(s["h"], b.g * 4 + half * 2 + 2)
                        sp.dma_start(wide_group_of(h24_t, b.g, 2 * D)[:, tiles, :], h_out[:, tiles, 0:2 * D]).then_inc(stored[half], 16)
                        sp.dma_start(wide_group_of(h3_t, b.g)[:, tiles, :], h_out[:, tiles, 2 * D:3 * D]).then_inc(stored[half], 16)

                pipeline(sp, step)
                for half in range(2):
                    sp.wait_ge(stored[half], stored_at[half] + 32 * WIDE_GROUPS)

            @block.gpsimd
            def _(pool):
                links = Links(pool, s["pool_link"], 2 * 6, passed)
                link = links.link

                def summed(b, first):
                    if not first:
                        pool.wait_ge(s["t_psum"], b.g)
                    pool.wait_ge(loaded[b.h], b.round * 32 + 32 + loaded_at[b.h])
                    pool.sem_inc(passed, 1)
                    link(pool.tensor_tensor(sum0[b.h][:], sum0[b.h][:], sum1[b.h][:], ALU.add))
                    link(pool.tensor_tensor(y[:], x_all[:, b.tiles, :], per_row(dis_all[:, b.tiles]), ALU.mult))
                    link(pool.tensor_tensor(sum0[b.h][:], sum0[b.h][:], y[:], ALU.add))
                    pool.tensor_tensor(t_in[:], sum0[b.h][:], per_row(dis_all[:, b.tiles]), ALU.mult).then_inc(s["t"], 1)

                def step(b, first, last):
                    if first:
                        summed(b, True)
                        summed(b.next(), False)
                    if not first:
                        pool.wait_ge(s["typed_psum"], b.g)
                        pool.sem_inc(passed, 1)
                    link(pool.tensor_copy(ntype[:], ntype_all[:, b.tiles]))
                    link(pool.tensor_copy(onehot[:, :, 1], ntype[:]))
                    pool.tensor_scalar(onehot[:, :, 0], ntype[:], -1.0, 1.0, ALU.mult, ALU.add).then_inc(s["onehot"], 1)
                    pool.wait_ge(s["x2"], b.g + 1)
                    pool.sem_inc(passed, 1)
                    link(pool.tensor_tensor(x_typed[:, :, D:2 * D], x2[b.h][:], per_row(ntype[:]), ALU.mult))
                    pool.tensor_tensor(x_typed[:, :, 0:D], x2[b.h][:], x_typed[:, :, D:2 * D], ALU.subtract).then_inc(s["typed"], 1)
                    if b.ahead > 1:
                        summed(b.next().next(), False)

                pipeline(pool, step, links)

            @block.tensor
            def _(pe):
                def transposes(b, first):
                    if not first:
                        pe.wait_ge(s["t_T"], b.g)
                    pe.wait_ge(s["t"], b.g + 1)
                    pe.sem_inc(pe_passed, 1)
                    for t in range(WIDE):
                        last = nc.tensor.transpose(t_psum[0:D, t * P:(t + 1) * P], t_in[:, t, :], ident[:])
                    last.then_inc(s["t_psum"], 1)

                def conv(b, first):
                    if not first:
                        pe.wait_ge(s["o"], b.g)
                    pe.wait_ge(s["t_T"], b.g + 1)
                    pe.sem_inc(pe_passed, 1)
                    for t in range(WIDE):
                        last = nc.tensor.matmul(conv_psum[:, t * D:(t + 1) * D], tT[:, t * P:(t + 1) * P], Wconv[:], start=True, stop=True)
                    last.then_inc(s["conv"], 1)

                def step(b, first, last):
                    if first:
                        transposes(b, True)
                        pe.wait_ge(s["ones_set"], 1)
                        conv(b, True)
                        transposes(b.next(), False)
                        conv(b.next(), False)
                    if not first:
                        pe.wait_ge(s["typed_T"], b.g)
                    pe.wait_ge(s["onehot"], b.g + 1)
                    pe.wait_ge(s["typed"], b.g + 1)
                    pe.sem_inc(pe_passed, 1)
                    nc.tensor.transpose(onehot_psum[0:WIDE * NODE_TYPES, 0:P], onehot[:].rearrange("p t k -> p (t k)"), ident[:])
                    for t in range(WIDE):
                        ins = nc.tensor.transpose(typed_psum[:, t * P:(t + 1) * P], x_typed[:, t, :], ident[:])
                    ins.then_inc(s["typed_psum"], 1)
                    pe.wait_ge(s["typed_T"], b.g + 1)
                    pe.sem_inc(pe_passed, 1)
                    for pair in range(WIDE // 2):
                        if not (first and pair < 2):
                            pe.wait_ge(s["h"], b.g * 4 + pair - 1)
                            pe.sem_inc(pe_passed, 1)
                        for k in range(2):
                            t = 2 * pair + k
                            out = pair_psum[pair % 2][:, k * 4 * D:(k + 1) * 4 * D]
                            nc.tensor.matmul(out, typedT[:, t * P:(t + 1) * P], W1234[:], start=True, stop=False)
                            ins = nc.tensor.matmul(out, onehotT[:], b1234[:, t, :], start=False, stop=True)
                        ins.then_inc(s["proj"], 1)
                        if b.ahead > 1 and pair == 0:
                            transposes(b.next().next(), False)
                        if b.ahead > 1 and pair == 1:
                            conv(b.next().next(), False)

                pipeline(pe, step)

            @block.scalar
            def _(act):
                act.preload_act_table_set("natural_log_exp_and_others")

                def t_copied(b, first):
                    if not first:
                        act.wait_ge(s["conv"], b.g)
                    act.wait_ge(s["t_psum"], b.g + 1)
                    nc.scalar.activation(tT[0:D, :], t_psum[0:D, :], ACT.Copy).then_inc(s["t_T"], 1)

                def exponential(b):
                    act.wait_ge(s["o"], b.g + 1)
                    nc.scalar.activation(neg[:], o[:], ACT.Relu, scale=-1.0).then_inc(s["neg"], 1)
                    act.wait_ge(s["neg"], b.g + 1)
                    nc.scalar.activation(exped[:], neg[:], ACT.Exp, scale=-1.0).then_inc(s["exp"], 1)

                def root(b):
                    act.wait_ge(s["var"], b.g + 1)
                    nc.scalar.activation(log[:], norm.var[:], ACT.Ln).then_inc(s["log"], 1)
                    act.wait_ge(s["log"], b.g + 1)
                    nc.scalar.activation(norm.std[:], log[:], ACT.Exp, scale=0.5).then_inc(s["std"], 1)

                def pair_copied(b, pair):
                    act.wait_ge(s["proj"], b.g * 4 + pair + 1)
                    nc.scalar.activation(h_out[:, 2 * pair:2 * pair + 2, :], pair_psum[pair % 2][:, :].rearrange("p (t d) -> p t d", t=2), ACT.Copy
                                         ).then_inc(s["h"], 1)

                def step(b, first, last):
                    if first:
                        t_copied(b, True)
                        exponential(b)
                        t_copied(b.next(), False)
                        norm.act_square(act, b.g, s["centred"], s["square"])
                        exponential(b.next())
                        root(b)
                    act.wait_ge(s["typed_psum"], b.g + 1)
                    if not first:
                        act.wait_ge(s["proj"], b.g * 4)
                    nc.scalar.activation(onehotT[:], onehot_psum[0:WIDE * NODE_TYPES, 0:P], ACT.Copy)
                    nc.scalar.activation(typedT[:], typed_psum[:], ACT.Copy).then_inc(s["typed_T"], 1)
                    if not first:
                        act.wait_ge(s["u"], b.g)
                    act.wait_ge(stored[0], b.g * 32 + stored_at[0])
                    pair_copied(b, 0)
                    if b.ahead > 1:
                        t_copied(b.next().next(), False)
                    pair_copied(b, 1)
                    if not last:
                        norm.act_square(act, b.next().g, s["centred"], s["square"])
                    if b.ahead > 1:
                        exponential(b.next().next())
                    if not last:
                        root(b.next())
                    act.wait_ge(stored[1], b.g * 32 + stored_at[1])
                    pair_copied(b, 2)
                    pair_copied(b, 3)

                pipeline(act, step)

            @block.vector
            def _(dve):
                links = Links(dve, s["link"], 2 * 6)
                link = links.link
                dve.memset(tT[D:D + 1, :], 1.0).then_inc(s["ones_set"], 1)

                def kept(b):
                    dve.wait_ge(s["h"], b.g * 4 + 4)
                    nc.vector.tensor_tensor(x_all[:, b.tiles, :], h_out[:, :, 3 * D:4 * D], x2[b.h][:], ALU.add).then_inc(s["u"], 1)

                def convolved(b, first):
                    dve.wait_ge(s["conv"], b.g + 1)
                    if not first:
                        dve.wait_ge(s["exp"], b.g)
                    nc.vector.scalar_tensor_tensor(o[:], x_all[:, b.tiles, :], ALPHA, wide_rows(conv_psum), ALU.mult, ALU.add).then_inc(s["o"], 1)

                def step(b, first, last):
                    if first:
                        convolved(b, True)
                    dve.wait_ge(s["o"], b.g + 1)
                    dve.wait_ge(s["exp"], b.g + 1)
                    link(nc.vector.scalar_tensor_tensor(v[:], o[:], 0.0, exped[:], ALU.max, ALU.add))
                    link(nc.vector.scalar_tensor_tensor(v[:], v[:], -1.0, x_all[:, b.tiles, :], ALU.add, ALU.add))
                    norm.centre(link, v[:], s["centred"])
                    if not last:
                        convolved(b.next(), False)
                    norm.variance(dve, link, b.g, s["square"], s["var"])
                    if not first:
                        dve.wait_ge(s["typed"], b.g - 1)
                    norm.scale(dve, link, x2[b.h][:], b.g, s["std"], s["x2"])
                    if not first:
                        kept(b.last())
                    if last:
                        kept(b)

                pipeline(dve, step, links)
        loaded_at = [loaded_at[h] + IN_SLOT[h] * 32 for h in range(2)]
        stored_at = [at + WIDE_GROUPS * 32 for at in stored_at]

        def edge_attention():
            with ExitStack() as c:
                s = c.enter_context(phase_semaphores(nc, "e2_", (
                    "idx_f", "wide", "same", "typed", "typed_psum", "typed_T", "w", "score", "exp",
                    "scat_idx", "msg", "sums", "rows", "rows_free", "link")))
                (idx, cat, side, extra, feat, scat_idx, rows_a, rows_b, idx_f, gidx,
                 same, masked, small, msg, typed, catT, sideT, hiddenT, work, hw) = edge_buffers(c, "e2_")
                block = c.enter_context(nc.Block())
                before_a, before_b, adds_before = gathers_a, gathers_b, adds

                @block.sync
                def _(sp):
                    with sp.Fori(0, STEPS, 1) as it:
                        for h in range(2):
                            g = it * 2 + h
                            sp.wait_ge(in_free[h], it + free_at)
                            sp.dma_start(idx[h][:], io["idx"][bass.ds(g * P, P), :]).then_inc(idx_loaded[h], 16)
                            sp.dma_start(feat[h][:], group_of(io["edge16"], g, F_EDGE)).then_inc(feat_loaded[h], 16)

                @block.gpsimd
                def _(pool):
                    def gather(t, h, it):
                        pool.wait_ge(idx_loaded[h], it * 16 + 16 + idx_at)
                        pool.sem_inc(passed, 1)
                        pool.indirect_dma_start(cat[h][:, t, :], None, h24_t,
                                                bass.IndirectOffsetOnAxis(ap=idx[h][:, t:t + 1], axis=0)
                                                ).then_inc(gath_a[h][t], 16)
                        pool.indirect_dma_start(extra[h][:, t, :], None, h3_t,
                                                bass.IndirectOffsetOnAxis(ap=idx[h][:, TILES + t:TILES + t + 1], axis=0)
                                                ).then_inc(gath_b[h][t], 16)

                    def scatter(t, h, g):
                        k = t % 2
                        pool.wait_ge(added[k], g * (16 * TILES // 2) + 16 * (t // 2) + adds_before)
                        if t == 0:
                            pool.wait_ge(s["scat_idx"], g + 1)
                            pool.wait_ge(s["rows"], g + 1)
                        if t == 1:
                            pool.sem_inc(s["rows_free"], 1)
                        pool.sem_inc(passed, 1)
                        pool.indirect_dma_start(attn_sum[k], bass.IndirectOffsetOnAxis(ap=scat_idx[h][:, t:t + 1], axis=0),
                                                rows_b[h][:, t, :], None, compute_op=ALU.add).then_inc(added[k], 16)

                    for t in range(TILES):
                        gather(t, 0, 0)
                    with pool.Fori(0, STEPS - 1, 1) as it:
                        for t in range(TILES):
                            gather(t, 1, it)
                            scatter(t, 0, it * 2)
                        for t in range(TILES):
                            gather(t, 0, it + 1)
                            scatter(t, 1, it * 2 + 1)
                    for t in range(TILES):
                        gather(t, 1, STEPS - 1)
                        scatter(t, 0, GROUPS - 2)
                    for t in range(TILES):
                        scatter(t, 1, GROUPS - 1)
                    for k in range(2):
                        pool.wait_ge(added[k], GROUPS * TILES * 8 + adds_before)

                @block.vector
                def _(dve):
                    FW = F_EDGE * EDGE_TYPES
                    with dve.Fori(0, STEPS, 1) as it:
                        link, end = linker(dve, s["link"], it, 20)
                        for h in range(2):
                            g = it * 2 + h
                            cols = bass.ds(g * TILES, TILES)
                            dve.wait_ge(s["wide"], g)
                            dve.wait_ge(s["same"], g)
                            dve.wait_ge(idx_loaded[h], it * 16 + 16 + idx_at)
                            nc.vector.tensor_copy(idx_f[:], idx[h][:]).then_inc(s["idx_f"], 1)
                            dve.wait_ge(s["typed_psum"], g)
                            link(nc.vector.tensor_copy(small[0][:, 0:TILES], etype_all[:, cols]))
                            for k in range(EDGE_TYPES):
                                last = nc.vector.tensor_scalar(typed[:, :, FW + k], small[0][:, 0:TILES], float(k), None, ALU.is_equal)
                            link(last)
                            dve.wait_ge(feat_loaded[h], it * 16 + 16)
                            for k in range(EDGE_TYPES):
                                last = nc.vector.tensor_tensor(typed[:, :, k * F_EDGE:(k + 1) * F_EDGE], feat[h][:],
                                                               typed[:, :, FW + k:FW + k + 1].to_broadcast([P, TILES, F_EDGE]), ALU.mult)
                            last.then_inc(s["typed"], 1)
                            dve.wait_ge(s["idx_f"], g + 1)
                            dve.wait_ge(s["sums"], g)
                            dve.wait_ge(s["wide"], g + 1)
                            nc.vector.tensor_tensor(same[:, 0:TILES, :], tiled(bank[0], P),
                                                    idx_f[:, TILES:2 * TILES].unsqueeze(2).to_broadcast([P, TILES, P]), ALU.is_equal
                                                    ).then_inc(s["same"], 1)
                            dve.wait_ge(s["rows_free"], g)
                            nc.vector.tensor_scalar(scat_idx[h][:, 0:TILES], recv_all[:, cols], 1.0, None, ALU.mult).then_inc(s["scat_idx"], 1)
                            for t in range(TILES):
                                dve.wait_ge(gath_a[h][t], it * 16 + 16 + before_a)
                                dve.wait_ge(gath_b[h][t], it * 16 + 16 + before_b)
                            dve.wait_ge(s["w"], g + 1)
                            link(nc.vector.tensor_tensor(hw[:], cat[h][:], tiled(bank[5], 2 * D), ALU.add))
                            link(nc.vector.tensor_tensor(work[0][:], extra[h][:], hw[:, :, D:2 * D], ALU.mult))
                            dve.sem_inc(in_free[h], 1)
                            link(nc.vector.tensor_reduce(small[1][:, 0:TILES], work[0][:], AX.X, ALU.add))
                            score = small[1][:, TILES:2 * TILES]
                            link(nc.vector.tensor_scalar(score, small[1][:, 0:TILES], HEAD_DIM ** -0.5, None, ALU.mult))
                            link(nc.vector.tensor_reduce(small[2][:, 0:TILES], score.unsqueeze(2), AX.X, ALU.max))
                            nc.vector.tensor_tensor(small[2][:, TILES:2 * TILES], score, small[2][:, 0:TILES], ALU.subtract).then_inc(s["score"], 1)
                            dve.wait_ge(s["exp"], g + 1)
                            link(nc.vector.tensor_reduce(small[4][:, 0:TILES], small[3][:, 0:TILES].unsqueeze(2), AX.X, ALU.add))
                            link(nc.vector.reciprocal(small[4][:, TILES:2 * TILES], small[4][:, 0:TILES]))
                            link(nc.vector.tensor_tensor(small[5][:, 0:TILES], small[3][:, 0:TILES], small[4][:, TILES:2 * TILES], ALU.mult))
                            nc.vector.tensor_tensor(msg[:, :, 0:D], hw[:, :, 0:D], over_features(small[5][:, 0:TILES]), ALU.mult).then_inc(s["msg"], 1)
                            dve.wait_ge(s["msg"], g + 1)
                        end()

                @block.tensor
                def _(pe):
                    TW = EDGE_TYPES * (F_EDGE + 1)
                    with pe.Fori(0, STEPS, 1) as it:
                        for h in range(2):
                            g = it * 2 + h
                            pe.wait_ge(s["same"], g)
                            pe.wait_ge(s["idx_f"], g + 1)
                            for t in range(TILES):
                                last = nc.tensor.transpose(bank[0][:, t * P:(t + 1) * P],
                                                           idx_f[:, TILES + t:TILES + t + 1].to_broadcast([P, P]), ident[:])
                            last.then_inc(s["wide"], 1)
                            pe.wait_ge(s["typed_T"], g)
                            pe.wait_ge(s["typed"], g + 1)
                            pe.sem_inc(pe_passed, 1)
                            for t in range(TILES):
                                last = nc.tensor.transpose(bank[3][0:TW, t * P:(t + 1) * P], typed[:, t, :], ident[:])
                            last.then_inc(s["typed_psum"], 1)
                            pe.wait_ge(s["msg"], g)
                            pe.wait_ge(s["typed_T"], g + 1)
                            pe.sem_inc(pe_passed, 1)
                            for t in range(TILES):
                                last = nc.tensor.matmul(bank[5][:, t * P:(t + 1) * P], catT[0:TW, t * P:(t + 1) * P],
                                                        W5[:].rearrange("p a d -> p (a d)"), start=True, stop=True)
                            last.then_inc(s["w"], 1)
                            pe.wait_ge(s["rows"], g)
                            pe.wait_ge(s["same"], g + 1)
                            pe.wait_ge(s["msg"], g + 1)
                            for t in range(TILES):
                                last = nc.tensor.matmul(bank[6][:, t * D:(t + 1) * D], same[:, t, :], msg[:, t, 0:D], start=True, stop=True)
                            last.then_inc(s["sums"], 1)

                @block.scalar
                def _(act):
                    TW = EDGE_TYPES * (F_EDGE + 1)
                    with act.Fori(0, STEPS, 1) as it:
                        for h in range(2):
                            g = it * 2 + h
                            act.wait_ge(s["w"], g)
                            act.wait_ge(s["typed_psum"], g + 1)
                            nc.scalar.activation(catT[0:TW, :], bank[3][0:TW, :], ACT.Copy).then_inc(s["typed_T"], 1)
                            act.wait_ge(s["score"], g + 1)
                            nc.scalar.activation(small[3][:, 0:TILES], small[2][:, TILES:2 * TILES], ACT.Exp).then_inc(s["exp"], 1)
                            act.wait_ge(s["rows_free"], g)
                            act.wait_ge(s["sums"], g + 1)
                            nc.scalar.activation(rows_b[h][:], tiled(bank[6], D), ACT.Copy).then_inc(s["rows"], 1)

        by_order(lambda: window_attention("w2_", attn_sum[0]), edge_attention)
        gathers_a += STEPS * 16
        gathers_b += STEPS * 16
        idx_at += STEPS * 16
        free_at += STEPS
        adds += GROUPS * TILES * 8

        with ExitStack() as c:
            s = c.enter_context(phase_semaphores(nc, "n2_", (
                "sum", "x3", "kept", "x3_psum", "x3_T", "prod", "z", "f", "centred", "square", "var", "std", "link", "ones_set")))
            rows, numbers = wide_buffers(c, "n2_")
            norm = Norm(rows, numbers)
            sum0, sum1 = rows("sum0", D, 2), rows("sum1", D, 2)
            v, x3 = rows("v"), rows("x3_", D, 2)
            z_out, f_out = rows("z_out", 2 * D, 2), rows("f_out", D, 2)
            x3T = c.enter_context(nc.sbuf_tensor("n2_x3T", [D + 1, WIDE * P], f32))
            x3_psum, z_psum, f_psum = wide_bank[0], wide_bank[1], bank[4]
            block = c.enter_context(nc.Block())

            @block.sync
            def _(sp):
                def load(b, early):
                    if not early:
                        sp.wait_ge(s["centred"], b.g - 1)
                    sp.dma_start(sum0[b.h][:], wide_group_of(attn_sum[0], b.g)).then_inc(loaded[b.h], 16)
                    sp.dma_start(sum1[b.h][:], wide_group_of(attn_sum[1], b.g)).then_inc(loaded[b.h], 16)

                def store(b):
                    sp.wait_ge(s["z"], b.g + 1)
                    sp.dma_start(wide_group_of(z3_t, b.g, 2 * D), z_out[b.h][:]).then_inc(stored[b.h], 16)
                    sp.wait_ge(s["f"], b.g + 1)
                    sp.dma_start(wide_group_of(f3_t, b.g), f_out[b.h][:]).then_inc(stored[b.h], 16)

                def step(b, first, last):
                    if first:
                        load(b, True)
                    if not last:
                        load(b.next(), first)
                    if not first:
                        store(b.last())
                    if last:
                        store(b)

                pipeline(sp, step)
                for h in range(2):
                    sp.wait_ge(stored[h], stored_at[h] + 32 * IN_SLOT[h])

            @block.gpsimd
            def _(pool):
                def summed(b):
                    pool.wait_ge(loaded[b.h], b.round * 32 + 32 + loaded_at[b.h])
                    pool.sem_inc(passed, 1)
                    pool.tensor_tensor(sum0[b.h][:], sum0[b.h][:], sum1[b.h][:], ALU.add).then_inc(s["sum"], 1)

                def step(b, first, last):
                    if first:
                        summed(b)
                    if not last:
                        summed(b.next())
                    pool.wait_ge(s["x3"], b.g + 1)
                    pool.sem_inc(passed, 1)
                    pool.tensor_copy(x_all[:, b.tiles, :], x3[b.h][:]).then_inc(s["kept"], 1)

                pipeline(pool, step)

            @block.tensor
            def _(pe):
                def step(b, first, last):
                    if not first:
                        pe.wait_ge(s["x3_T"], b.g)
                    pe.wait_ge(s["x3"], b.g + 1)
                    pe.sem_inc(pe_passed, 1)
                    for t in range(WIDE):
                        ins = nc.tensor.transpose(x3_psum[0:D, t * P:(t + 1) * P], x3[b.h][:, t, :], ident[:])
                    ins.then_inc(s["x3_psum"], 1)
                    if first:
                        pe.wait_ge(s["ones_set"], 1)
                    else:
                        pe.wait_ge(s["f"], b.g)
                    pe.wait_ge(s["x3_T"], b.g + 1)
                    pe.sem_inc(pe_passed, 1)
                    for t in range(WIDE):
                        nc.tensor.matmul(z_psum[:, t * 2 * D:(t + 1) * 2 * D], x3T[:, t * P:(t + 1) * P], Wsign[:, 0:2 * D], start=True, stop=True)
                        ins = nc.tensor.matmul(f_psum[:, t * D:(t + 1) * D], x3T[:, t * P:(t + 1) * P], Wsign[:, 2 * D:3 * D], start=True, stop=True)
                    ins.then_inc(s["prod"], 1)

                pipeline(pe, step)

            @block.scalar
            def _(act):
                def step(b, first, last):
                    if first:
                        norm.act_square(act, b.g, s["centred"], s["square"])
                        norm.act_root(act, b.g, s["var"], s["std"])
                    if not first:
                        act.wait_ge(s["prod"], b.g)
                    act.wait_ge(s["x3_psum"], b.g + 1)
                    nc.scalar.activation(x3T[0:D, :], x3_psum[0:D, :], ACT.Copy).then_inc(s["x3_T"], 1)
                    if not last:
                        norm.act_square(act, b.next().g, s["centred"], s["square"])
                        norm.act_root(act, b.next().g, s["var"], s["std"])
                    act.wait_ge(stored[b.h], b.round * 32 + stored_at[b.h])
                    act.wait_ge(s["prod"], b.g + 1)
                    nc.scalar.activation(z_out[b.h][:], wide_rows(z_psum, 2 * D), ACT.Copy).then_inc(s["z"], 1)
                    nc.scalar.activation(f_out[b.h][:], wide_rows(f_psum), ACT.Copy).then_inc(s["f"], 1)

                pipeline(act, step)

            @block.vector
            def _(dve):
                links = Links(dve, s["link"], 2 * 5)
                link = links.link
                dve.memset(x3T[D:D + 1, :], 1.0).then_inc(s["ones_set"], 1)

                def step(b, first, last):
                    dve.wait_ge(s["sum"], b.g + 1)
                    link(nc.vector.tensor_tensor(v[:], sum0[b.h][:], x_all[:, b.tiles, :], ALU.add))
                    norm.centre(link, v[:], s["centred"])
                    norm.variance(dve, link, b.g, s["square"], s["var"])
                    if not first:
                        dve.wait_ge(s["kept"], b.g - 1)
                        dve.wait_ge(s["x3_psum"], b.g - 1)
                    norm.scale(dve, link, x3[b.h][:], b.g, s["std"], s["x3"])

                pipeline(dve, step, links)
        loaded_at = [loaded_at[h] + IN_SLOT[h] * 32 for h in range(2)]
        stored_at = [stored_at[h] + IN_SLOT[h] * 32 for h in range(2)]

        by_order(lambda: window_sums("w3_", None, sign_sum[0], D, gathered_from=z3_halves, signed=True),
                 lambda: edge_sums("e3_", z3_halves, sign_sum, signed=True))
        free_at += STEPS


        with ExitStack() as c:
            s = c.enter_context(phase_semaphores(nc, "n3_", (
                "o", "o_square", "o_sum_sq", "o_root", "y", "centred", "square", "var", "std", "link", "pool_link")))
            rows, numbers = wide_buffers(c, "n3_")
            norm = Norm(rows, numbers)
            sum0, sum1, own = rows("sum0", D, 2), rows("sum1", D, 2), rows("own", D, 2)
            o, y = rows("o", D, 2), rows("y", D, 2)
            o_square, unit, v = rows("o_square"), rows("unit"), rows("v")
            o_sum_sq, o_root, guarded, o_scale = numbers("o_sum_sq", "o_root", "guarded", "o_scale")
            block = c.enter_context(nc.Block())

            @block.sync
            def _(sp):
                def load(b, early):
                    if not early:
                        sp.wait_ge(s["o"], b.g - 1)
                    sp.dma_start(sum0[b.h][:], wide_group_of(sign_sum[0], b.g)).then_inc(loaded[b.h], 16)
                    sp.dma_start(sum1[b.h][:], wide_group_of(sign_sum[1], b.g)).then_inc(loaded[b.h], 16)
                    sp.dma_start(own[b.h][:], wide_group_of(f3_t, b.g)).then_inc(loaded[b.h], 16)

                def store(b):
                    sp.wait_ge(s["y"], b.g + 1)
                    sp.dma_start(wide_group_of(io["out"], b.g), y[b.h][:]).then_inc(stored[b.h], 16)

                def step(b, first, last):
                    if first:
                        load(b, True)
                    if not last:
                        load(b.next(), first)
                    if not first:
                        store(b.last())
                    if last:
                        store(b)

                pipeline(sp, step)
                for h in range(2):
                    sp.wait_ge(stored[h], stored_at[h] + 16 * IN_SLOT[h])

            @block.gpsimd
            def _(pool):
                links = Links(pool, s["pool_link"], 2 * 2, passed)
                link = links.link

                def step(b, first, last):
                    if not first:
                        pool.wait_ge(s["centred"], b.g - 1)
                    pool.wait_ge(loaded[b.h], b.round * 48 + 48 + loaded_at[b.h])
                    pool.sem_inc(passed, 1)
                    link(pool.tensor_tensor(sum0[b.h][:], sum0[b.h][:], sum1[b.h][:], ALU.add))
                    link(pool.tensor_tensor(sum1[b.h][:], sum0[b.h][:], per_row(rcount_all[:, b.tiles]), ALU.mult))
                    pool.tensor_tensor(o[b.h][:], sum1[b.h][:], own[b.h][:], ALU.add).then_inc(s["o"], 1)

                pipeline(pool, step, links)

            @block.scalar
            def _(act):
                def o_squared(b):
                    act.wait_ge(s["o"], b.g + 1)
                    nc.scalar.activation(o_square[:], o[b.h][:], ACT.Square).then_inc(s["o_square"], 1)

                def o_rooted(b):
                    act.wait_ge(s["o_sum_sq"], b.g + 1)
                    nc.scalar.activation(o_root[:], o_sum_sq[:], ACT.Sqrt).then_inc(s["o_root"], 1)

                def step(b, first, last):
                    if first:
                        o_squared(b)
                        o_rooted(b)
                    norm.act_square(act, b.g, s["centred"], s["square"])
                    if not last:
                        act.wait_ge(s["o_sum_sq"], b.g + 1)
                        o_squared(b.next())
                    norm.act_root(act, b.g, s["var"], s["std"])
                    if not last:
                        o_rooted(b.next())

                pipeline(act, step)

            @block.vector
            def _(dve):
                links = Links(dve, s["link"], 2 * 8)
                link = links.link

                def root_of(b):
                    dve.wait_ge(s["o_square"], b.g + 1)
                    nc.vector.tensor_reduce(o_sum_sq[:], o_square[:], AX.X, ALU.add).then_inc(s["o_sum_sq"], 1)

                def step(b, first, last):
                    if first:
                        root_of(b)
                    dve.wait_ge(s["o_root"], b.g + 1)
                    link(nc.vector.tensor_scalar(guarded[:], o_root[:], NORM_EPS, None, ALU.max))
                    link(nc.vector.reciprocal(o_scale[:], guarded[:]))
                    link(nc.vector.tensor_tensor(unit[:], o[b.h][:], per_row(o_scale[:]), ALU.mult))
                    link(nc.vector.tensor_tensor(v[:], unit[:], x_all[:, b.tiles, :], ALU.add))
                    norm.centre(link, v[:], s["centred"])
                    if not last:
                        root_of(b.next())
                    norm.variance(dve, link, b.g, s["square"], s["var"])
                    dve.wait_ge(stored[b.h], b.round * 16 + stored_at[b.h])
                    norm.scale(dve, link, y[b.h][:], b.g, s["std"], s["y"])

                pipeline(dve, step, links)


def kernel(x, src, dst, edge_attr_16, edge_attr_64, edge_type_3, edge_weight, node_type_2, **weights):
    import numpy as np
    import concourse.bacc as bacc
    from concourse.bass_utils import run_bass_kernel_spmd

    def padded(a, value=0):
        a = np.asarray(a)
        return np.pad(a, [(0, ROWS - N)] + [(0, 0)] * (a.ndim - 1), constant_values=value)

    def columns(a, tiles=TILES):
        return np.ascontiguousarray(padded(a).reshape(-1, P, tiles).transpose(1, 0, 2).reshape(P, GROUPS * TILES))

    def in_order(a, pads):
        return np.concatenate([np.asarray(a), pads[:ROWS + WINDOW - N]])

    dst_lin = in_order(dst, np.arange(N, ROWS + WINDOW, dtype=np.int32))
    ends = [a.reshape(ROWS // TILES, TILES) for a in (padded(src, N), dst_lin[:ROWS])]
    named = {
        "x": padded(x), "edge64": padded(edge_attr_64), "edge16": padded(edge_attr_16),
        "idx": np.concatenate(ends, axis=1),
        "dst_lin": dst_lin, "dst_firsts": dst_lin[:ROWS:P],
        "edge16_T": np.concatenate([in_order(edge_attr_16, np.zeros((ROWS, F_EDGE), np.float32)).T] * EDGE_TYPES
                                   + [np.ones((EDGE_TYPES, ROWS + WINDOW), np.float32)]),
        "etype_lin": in_order(edge_type_3, np.zeros(ROWS, np.int32)),
        "src_lin": in_order(src, np.full(ROWS, N, np.int32)), "ew_lin": in_order(edge_weight, np.zeros(ROWS, np.float32)),
        "ew_cols": columns(edge_weight), "etype_cols": columns(edge_type_3), "ntype_cols": columns(node_type_2, WIDE),
    }
    for short in ("We1", "be1", "We2", "be2", "Wn1", "bn1", "Wn2", "bn2"):
        named[short] = weights["L0_gnn_" + short]
    named["W_conv"], named["b_conv"] = weights["L1_gnn_W"], weights["L1_gnn_b"]
    for k in range(1, 6):
        named[f"W{k}"], named[f"b{k}"] = weights[f"L2_gnn_W{k}"], weights[f"L2_gnn_b{k}"]
    named["W_sign"], named["b_sign"] = weights["L3_gnn_W"], weights["L3_gnn_b"]

    nc = bacc.Bacc("TRN2", target_bir_lowering=False, num_devices=1)
    arrays, io = {}, {}
    for name, a in named.items():
        a = np.ascontiguousarray(a)
        arrays["in_" + name] = a
        io[name] = nc.dram_tensor("in_" + name, a.shape, mybir.dt.from_np(a.dtype), kind="ExternalInput").ap()
    io["out"] = nc.dram_tensor("out", (ROWS, D), f32, kind="ExternalOutput").ap()
    build(nc, io)
    result = run_bass_kernel_spmd(nc, [arrays], core_ids=[0]).results[0]["out"]
    return result[:N]
```

```python
from contextlib import ExitStack, contextmanager

import concourse.bass as bass
from concourse import mybir

P = 128
N = 50000
D = 64
HID = 128
F_EDGE = 16
NODE_TYPES = 2
EDGE_TYPES = 3
TILES = 4
GROUP = TILES * P
GROUPS = 2 * -(-N // (2 * GROUP))
WIDE = 8
WIDE_GROUPS = GROUPS * TILES // WIDE
IN_SLOT = [-(-WIDE_GROUPS // 2), WIDE_GROUPS // 2]
assert WIDE_GROUPS % 2 == 1
STEPS = GROUPS // 2
ROWS = GROUPS * GROUP
DUMP = ROWS
TABLE = ROWS + P
EW_COL, ONE_COL = D, D + 1
EDGE_TILES = ROWS // P
WINDOW_TILES = WIDE + 1
WINDOW = WINDOW_TILES * P
PART_ROWS = 3 * 32
D_RECV = D + 2
LN_EPS = 1e-5
NORM_EPS = 1e-12
ALPHA = 0.1
HEAD_DIM = 16.0

f32 = mybir.dt.float32
bf16 = mybir.dt.bfloat16
i32 = mybir.dt.int32
ALU = mybir.AluOpType
ACT = mybir.ActivationFunctionType
AX = mybir.AxisListType


def linker(engine, sem, it, per_step):
    made = [0]

    def link(ins):
        made[0] += 1
        ins.then_inc(sem, 1)
        engine.wait_ge(sem, it * per_step + made[0])

    def end():
        assert made[0] == per_step, made[0]

    return link, end


class Group:

    def __init__(self, it, k, ahead=2):
        self.it, self.k, self.ahead = it, k, ahead
        self.g, self.h, self.round = it * 2 + k, k % 2, it + k // 2
        self.tiles = bass.ds(self.g * WIDE, WIDE)

    def next(self):
        return Group(self.it, self.k + 1)

    def last(self):
        return Group(self.it, self.k - 1)


def pipeline(engine, step, links=None):
    step(Group(0, 0), True, False)
    rounds = (WIDE_GROUPS - 3) // 2
    with engine.Fori(0, rounds, 1) as it:
        if links:
            links.enter(it)
        step(Group(it, 1), False, False)
        step(Group(it, 2), False, False)
        if links:
            links.leave(rounds)
    step(Group(0, WIDE_GROUPS - 2, 1), False, False)
    step(Group(0, WIDE_GROUPS - 1, 0), False, True)


class Links:

    def __init__(self, engine, sem, per_round, passed=None):
        self.engine, self.sem, self.per_round, self.passed = engine, sem, per_round, passed
        self.it, self.made, self.base = 0, 0, 0

    def link(self, ins):
        ins.then_inc(self.sem, 1)
        self.made += 1
        self.engine.wait_ge(self.sem, self.it * self.per_round + (self.base + self.made))
        if self.passed is not None:
            self.engine.sem_inc(self.passed, 1)

    def enter(self, it):
        self.it, self.base, self.made = it, self.base + self.made, 0

    def leave(self, rounds):
        assert self.made == self.per_round, self.made
        self.it, self.base, self.made = 0, self.base + rounds * self.made, 0


@contextmanager
def phase_semaphores(nc, tag, names):
    sems = {n: nc.alloc_semaphore(name=tag + n) for n in names}
    yield sems
    nc.all_engine_barrier()
    nc.clear_and_free_semaphores(list(sems.values()))
    nc.all_engine_barrier()


def over_features(columns):
    return columns.unsqueeze(2).to_broadcast([P, TILES, D])


def build(nc, io):
    with ExitStack() as whole:
        def sb(name, shape, dt=f32):
            return whole.enter_context(nc.sbuf_tensor(name, shape, dt))

        def ps(name, shape):
            return whole.enter_context(nc.psum_tensor(name, shape, f32))

        def sem(name):
            return whole.enter_context(nc.semaphore(name))

        def table(name, width, n=ROWS):
            return nc.dram_tensor(name, (n, width), f32).ap()

        sent_sum = [table(f"sent_sum{k}", D, TABLE) for k in range(2)]
        messages_t = table("messages_t", D_RECV, ROWS + WINDOW)
        recv_sum = table("recv_sum", D_RECV, TABLE)
        conv_sum = [table(f"conv_sum{k}", D, TABLE) for k in range(2)]
        attn_sum = [table(f"attn_sum{k}", D, TABLE) for k in range(2)]
        sign_sum = [table(f"sign_sum{k}", D, TABLE) for k in range(2)]
        y1_t = table("y1_t", D)
        h24_t = table("h24_t", 2 * D)
        h3_t = table("h3_t", D)
        z3_t = table("z3_t", 2 * D)
        f3_t = table("f3_t", D)
        z3_halves = z3_t.rearrange("r (s d) -> (r s) d", s=2)

        def group_of(tab, g, width=D):
            return tab.rearrange("(q t) d -> q t d", t=TILES)[bass.ds(g * P, P), :, 0:width]

        def wide_group_of(tab, g, width=D):
            return tab.rearrange("(q t) d -> q t d", t=WIDE)[bass.ds(g * P, P), :, 0:width]

        x_all = sb("x_all", [P, WIDE_GROUPS * WIDE, D])
        ident = sb("ident", [P, P])
        earlier = sb("earlier", [P, P])
        dump_row_i, dump_row = sb("dump_row_i", [P, 1], i32), sb("dump_row", [P, 1])
        ew_all = sb("ew_all", [P, GROUPS * TILES])
        etype_all = sb("etype_all", [P, GROUPS * TILES], i32)
        ntype_all = sb("ntype_all", [P, GROUPS * TILES], i32)
        recv_all = sb("recv_all", [P, GROUPS * TILES], i32)
        dis_all = sb("dis_all", [P, GROUPS * TILES])
        rcount_all = sb("rcount_all", [P, GROUPS * TILES])
        We1a, We1b, We2 = sb("We1a", [P, HID]), sb("We1b", [D, HID]), sb("We2", [HID, D])
        Wn1a, Wn1b, Wn2 = sb("Wn1a", [P, HID]), sb("Wn1b", [P, HID]), sb("Wn2", [HID, D])
        be1, bn1 = sb("be1", [HID, 1]), sb("bn1", [HID, 1])
        be2, bn2 = sb("be2", [P, D]), sb("bn2", [P, D])
        Wconv = sb("Wconv", [D + 1, D])
        W1234 = sb("W1234", [P, 4 * D])
        b1234_parts = sb("b1234_parts", [PART_ROWS, WIDE, 4 * D], bf16)
        W5 = sb("W5", [EDGE_TYPES * (F_EDGE + 1), 2, D])
        Wsign = sb("Wsign", [D + 1, 3 * D])
        Wsign_rows = sb("Wsign_rows", [D, 3 * D])

        starts_t = nc.dram_tensor("starts_t", (4 * P,), i32).ap()
        windows_dst, windows_src = [nc.dram_tensor(f"windows_{n}", (WIDE_GROUPS * WINDOW,), i32).ap() for n in ("dst", "src")]
        windows_ew = nc.dram_tensor("windows_ew", (WIDE_GROUPS * WINDOW,), f32).ap()
        numbers_all = sb("numbers_all", [P, WIDE_GROUPS, 2, WINDOW_TILES])
        index_all = sb("index_all", [P, WIDE_GROUPS, 3, WINDOW_TILES], i32)
        starts = sb("starts", [1, 4 * P], i32)
        sorted_flag = sb("sorted_flag", [1, 1], i32)
        band = sb("band", [P, 3 * P])

        wide_bank = [ps(f"bank{2 * n}_{2 * n + 1}", [P, 2 * GROUP]) for n in range(4)]
        bank = [wide_bank[n // 2][:, n % 2 * GROUP:(n % 2 + 1) * GROUP] for n in range(8)]

        gath_a = [[sem(f"gath_a{h}{t}") for t in range(TILES)] for h in range(2)]
        gath_b = [[sem(f"gath_b{h}{t}") for t in range(TILES)] for h in range(2)]
        passed = sem("passed")
        sent_done, recv_done = [sem(f"sent_done{k}") for k in range(2)], sem("recv_done")
        idx_loaded = [sem(f"idx_loaded{h}") for h in range(2)]
        loaded = [sem(f"loaded{h}") for h in range(2)]
        feat_loaded = [sem(f"feat_loaded{h}") for h in range(2)]
        in_free = [sem(f"in_free{h}") for h in range(2)]
        stored = [sem(f"stored{h}") for h in range(2)]
        added = [sem(f"added{k}") for k in range(2)]
        pe_passed = sem("pe_passed")
        ready = sem("ready")
        setup_load = sem("setup_load")
        late_load = sem("late_load")
        cleared = sem("cleared")
        cleared_later = sem("cleared_later")

        def fill(tab):
            return tab.rearrange("(p r) d -> p (r d)", p=P)

        ZEROS = TABLE * D_RECV // P // 6 + 1
        zeros = x_all[:].rearrange("p t d -> p (t d)")[:, 0:ZEROS]

        def clear(eng, tab, done):
            flat = fill(tab)
            part = flat.shape[1] // 6
            assert part * 6 == flat.shape[1] and part <= ZEROS
            for n in range(6):
                eng.dma_start(flat[:, n * part:(n + 1) * part], zeros[:, 0:part]).then_inc(done, 16)
            return 96

        def edge_buffers(c, tag):
            def eb(name, shape, dt=f32):
                return c.enter_context(nc.sbuf_tensor(tag + name, shape, dt))

            idx = [eb(f"idx{h}", [P, 2 * TILES], i32) for h in range(2)]
            cat = [eb(f"cat{h}", [P, TILES, 2 * D]) for h in range(2)]
            side = [eb(f"side{h}", [P, TILES, D_RECV]) for h in range(2)]
            extra = [eb(f"extra{h}", [P, TILES, D]) for h in range(2)]
            feat = [eb(f"feat{h}", [P, TILES, F_EDGE]) for h in range(2)]
            scat_idx = [eb(f"scat_idx{h}", [P, 2 * TILES], i32) for h in range(2)]
            rows_a = [eb(f"rows_a{h}", [P, TILES, D_RECV]) for h in range(2)]
            rows_b = [eb(f"rows_b{h}", [P, TILES, D]) for h in range(2)]
            idx_f = eb("idx_f", [P, 2 * TILES])
            gidx = [eb(f"gidx{h}", [P, TILES], i32) for h in range(2)]
            same = eb("same", [P, 2 * TILES, P])
            masked = eb("masked", [P, 2 * TILES, P])
            small = [eb(f"small{n}", [P, 2 * TILES]) for n in range(8)]
            msg = eb("msg", [P, TILES, D_RECV])
            typed = eb("typed", [P, TILES, EDGE_TYPES * (F_EDGE + 1)])
            catT = eb("catT", [P, GROUP])
            sideT = eb("sideT", [D, GROUP])
            hiddenT = eb("hiddenT", [HID, GROUP])
            work = [eb(f"work{n}", [P, TILES, D]) for n in range(1)]
            hw = eb("hw", [P, TILES, 2 * D])
            return (idx, cat, side, extra, feat, scat_idx, rows_a, rows_b, idx_f, gidx,
                    same, masked, small, msg, typed, catT, sideT, hiddenT, work, hw)

        with ExitStack() as c:
            zeroed, wsign_ready, wsign_t, biases, bias_link = c.enter_context(phase_semaphores(
                nc, "setup_", ("zeroed", "wsign_ready", "wsign_t", "biases", "bias_link"))).values()
            b1234, rest, top = [c.enter_context(nc.sbuf_tensor(f"setup_{n}", [PART_ROWS, WIDE, 4 * D], dt))
                                for n, dt in (("b1234", f32), ("rest", f32), ("top", bf16))]
            block = c.enter_context(nc.Block())
            loads = [
                (ew_all, io["ew_cols"]), (etype_all, io["etype_cols"]), (ntype_all, io["ntype_cols"]),
                (We1a, io["We1"][0:P]), (We1b, io["We1"][P:P + D]), (We2, io["We2"]),
                (Wn1a, io["Wn1"][0:P]), (Wn1b[0:D, :], io["Wn1"][D:2 * D]), (Wn1b[D:2 * D, :], io["Wn1"][P:P + D]), (Wn2, io["Wn2"]),
                (be1, io["be1"].unsqueeze(1)), (bn1, io["bn1"].unsqueeze(1)),
                (be2, io["be2"].unsqueeze(0).to_broadcast([P, D])),
                (bn2, io["bn2"].unsqueeze(0).to_broadcast([P, D])),
                (Wconv[0:D, :], io["W_conv"]), (Wconv[D:D + 1, :], io["b_conv"].unsqueeze(0)),
                (Wsign_rows, io["W_sign"]),
            ]
            late = []
            for m, k in enumerate((2, 4, 3, 1)):
                cols = slice(m * D, (m + 1) * D)
                late.append((W1234[:, cols], io[f"W{k}"].rearrange("a f h -> (a f) h")))
                for t in range(WIDE):
                    late.append((b1234[2 * t:2 * t + 2, t, cols], io[f"b{k}"]))
            for m in range(2):
                late.append((W5[0:EDGE_TYPES * F_EDGE, m, :], io["W5"].rearrange("a f h -> (a f) h")))
                late.append((W5[EDGE_TYPES * F_EDGE:EDGE_TYPES * (F_EDGE + 1), m, :], io["b5"]))
            late.append((Wsign[D:D + 1, 2 * D:3 * D], io["b_sign"].unsqueeze(0)))

            @block.sync
            def _(sp):
                for dst, src in loads:
                    sp.dma_start(dst[:] if not isinstance(dst, bass.AP) else dst, src).then_inc(setup_load, 16)
                sp.wait_ge(zeroed, 4)
                for dst, src in late:
                    sp.dma_start(dst, src).then_inc(late_load, 16)
                sp.wait_ge(setup_load, 16 * len(loads))
                sp.wait_ge(late_load, 16 * len(late))
                for part in (1, 2):
                    sp.dma_start(b1234[32 * part:32 * part + WIDE * NODE_TYPES, :, :], b1234[0:WIDE * NODE_TYPES, :, :]).then_inc(biases, 16)
                sp.wait_ge(biases, 32)

            @block.gpsimd
            def _(pool):
                pool.memset(ident[:], 0.0).then_inc(ready, 1)
                pool.memset(earlier[:], 1.0).then_inc(ready, 1)
                pool.iota(dump_row_i[:], [[0, 1]], base=DUMP, channel_multiplier=1).then_inc(ready, 1)
                pool.wait_ge(ready, 3)
                pool.affine_select(out=ident[:], in_=ident[:], compare_op=ALU.not_equal, fill=1.0,
                                   base=0, pattern=[[-1, P]], channel_multiplier=1).then_inc(ready, 1)
                pool.affine_select(out=earlier[:], in_=earlier[:], compare_op=ALU.is_gt, fill=0.0,
                                   base=0, pattern=[[-1, P]], channel_multiplier=1).then_inc(ready, 1)
                pool.tensor_copy(dump_row[:], dump_row_i[:]).then_inc(ready, 1)

            @block.scalar
            def _(act):
                act.wait_ge(zeroed, 4)
                for tab in sent_sum:
                    clear(act, tab, cleared)

            @block.vector
            def _(dve):
                dve.memset(zeros, 0.0).then_inc(zeroed, 1)
                dve.memset(b1234[:], 0.0).then_inc(zeroed, 1)
                dve.memset(Wsign[D:D + 1, :], 0.0).then_inc(zeroed, 1)
                dve.memset(W5[:], 0.0).then_inc(zeroed, 1)
                links = Links(dve, bias_link, 0)
                dve.wait_ge(late_load, 16 * len(late))
                dve.wait_ge(biases, 32)
                links.link(dve.tensor_copy(top[:], b1234[:]))
                links.link(dve.tensor_copy(b1234_parts[0:32], top[0:32]))
                links.link(dve.tensor_tensor(rest[:], b1234[:], top[:], ALU.subtract))
                links.link(dve.tensor_copy(top[:], rest[:]))
                links.link(dve.tensor_copy(b1234_parts[32:64], top[32:64]))
                links.link(dve.tensor_tensor(b1234_parts[64:96], rest[64:96], top[64:96], ALU.subtract))
                dve.wait_ge(setup_load, 16 * len(loads))
                dve.tensor_scalar(Wconv[:], Wconv[:], 1.0 - ALPHA, None, ALU.mult).then_inc(wsign_ready, 1)
                dve.wait_ge(wsign_t, 3)
                dve.tensor_copy(Wsign[0:D, :], bank[0][0:D, 0:3 * D]).then_inc(wsign_ready, 1)

            @block.tensor
            def _(pe):
                pe.wait_ge(ready, 6)
                pe.wait_ge(setup_load, 16 * len(loads))
                for m in range(3):
                    pe.transpose(bank[0][0:D, m * D:(m + 1) * D], Wsign_rows[:, m * D:(m + 1) * D],
                                 ident[0:D, 0:D]).then_inc(wsign_t, 1)

        gathers_a = gathers_b = adds = idx_at = free_at = 0

        loaded_at, stored_at = [0, 0], [0, 0]

        with ExitStack() as c:
            s = c.enter_context(phase_semaphores(nc, "fi_", (
                "loaded", "iota", "tile", "gathered", "start", "stored", "back", "link", "bad", "total", "flag")))
            COLS = 4
            STARTS = COLS * P

            def buf(name, shape, dt=f32):
                return c.enter_context(nc.sbuf_tensor("fi_" + name, shape, dt))

            firsts_i, firsts = buf("firsts_i", [P, EDGE_TILES], i32), buf("firsts", [P, EDGE_TILES])
            here_i, next_i = buf("here_i", [P, EDGE_TILES], i32), buf("next_i", [P, EDGE_TILES], i32)
            compare = buf("compare", [P, EDGE_TILES])
            limit_i, limit = buf("limit_i", [P, COLS], i32), buf("limit", [P, COLS])
            before_n, tile_i = buf("before_n", [P, COLS]), buf("tile_i", [P, COLS], i32)
            tile_dst_i, tile_dst = buf("tile_dst_i", [P, COLS, P], i32), buf("tile_dst", [P, COLS, P])
            inside, start_i = buf("inside", [P, COLS]), buf("start_i", [P, COLS], i32)
            own_i, after_i, own = buf("own_i", [WIDE_GROUPS, WIDE], i32), buf("after_i", [WIDE_GROUPS, WIDE], i32), buf("own", [WIDE_GROUPS, WIDE + 1])
            low_i, low = buf("low_i", [WIDE_GROUPS, WIDE + 1], i32), buf("low", [WIDE_GROUPS, WIDE + 1])
            high = buf("high", [WIDE_GROUPS, WIDE + 1])
            bad = buf("bad", [P, 4])
            ones = buf("ones", [P, 1])
            flag = buf("flag", [1, 2])
            band_i = buf("band_i", [P, 3 * P], i32)
            block = c.enter_context(nc.Block())

            @block.sync
            def _(sp):
                sp.dma_start(firsts_i[:], io["dst_firsts"].unsqueeze(0).to_broadcast([P, EDGE_TILES])).then_inc(s["loaded"], 16)
                sp.dma_start(here_i[:], io["dst_lin"][0:ROWS].rearrange("(p n) -> p n", p=P)).then_inc(s["loaded"], 16)
                sp.dma_start(next_i[:], io["dst_lin"][1:ROWS + 1].rearrange("(p n) -> p n", p=P)).then_inc(s["loaded"], 16)
                sp.wait_ge(s["start"], 1)
                sp.dma_start(starts_t.rearrange("(p c) -> p c", p=P), start_i[:]).then_inc(s["stored"], 16)
                sp.wait_ge(s["stored"], 16)
                sp.dma_start(starts[:], starts_t.unsqueeze(0)).then_inc(s["back"], 16)
                sp.dma_start(own_i[:], starts_t[0:WIDE_GROUPS * WIDE].rearrange("(g k) -> g k", k=WIDE)).then_inc(s["back"], 16)
                sp.dma_start(after_i[:], starts_t[WIDE:(WIDE_GROUPS + 1) * WIDE].rearrange("(g k) -> g k", k=WIDE)
                             ).then_inc(s["back"], 16)
                sp.wait_ge(s["back"], 48)
                sp.wait_ge(s["flag"], 1)

            @block.gpsimd
            def _(pool):
                pool.iota(limit_i[:], [[P, COLS]], base=0, channel_multiplier=COLS * P).then_inc(s["iota"], 1)
                pool.iota(low_i[:], [[P, WIDE + 1]], base=-P, channel_multiplier=0).then_inc(s["iota"], 1)
                pool.iota(band_i[:], [[1, 3 * P]], base=0, channel_multiplier=0).then_inc(s["iota"], 1)
                pool.wait_ge(s["tile"], 1)
                for k in range(COLS):
                    pool.indirect_dma_start(tile_dst_i[:, k, :], None, io["dst_lin"].rearrange("(m q) -> m q", q=P),
                                            bass.IndirectOffsetOnAxis(ap=tile_i[:, k:k + 1], axis=0)
                                            ).then_inc(s["gathered"], 16)

            @block.vector
            def _(dve):
                links = Links(dve, s["link"], 0)
                link = links.link
                dve.wait_ge(s["iota"], 3)
                link(dve.tensor_copy(band[:], band_i[:]))
                link(dve.memset(bad[:], 0.0))
                link(dve.memset(ones[:], 1.0))
                link(dve.tensor_copy(limit[:], limit_i[:]))
                link(dve.tensor_copy(low[:], low_i[:]))
                dve.wait_ge(s["loaded"], 48)
                link(dve.tensor_copy(firsts[:], firsts_i[:]))
                for k in range(COLS):
                    link(dve.tensor_scalar(compare[:], firsts[:], limit[:, k:k + 1], None, ALU.is_lt))
                    link(dve.tensor_reduce(before_n[:, k:k + 1], compare[:], AX.X, ALU.add))
                link(dve.tensor_scalar(before_n[:], before_n[:], -1.0, 0.0, ALU.add, ALU.max))
                dve.tensor_copy(tile_i[:], before_n[:]).then_inc(s["tile"], 1)
                link(dve.tensor_tensor(compare[:], here_i[:], next_i[:], ALU.is_gt))
                link(dve.tensor_reduce(bad[:, 0:1], compare[:], AX.X, ALU.add))
                dve.wait_ge(s["gathered"], 16 * COLS)
                link(dve.tensor_copy(tile_dst[:], tile_dst_i[:]))
                for k in range(COLS):
                    link(dve.tensor_scalar(compare[:, 0:P], tile_dst[:, k, :], limit[:, k:k + 1], None, ALU.is_lt))
                    link(dve.tensor_reduce(inside[:, k:k + 1], compare[:, 0:P], AX.X, ALU.add))
                dve.scalar_tensor_tensor(start_i[:], before_n[:], float(P), inside[:], ALU.mult, ALU.add).then_inc(s["start"], 1)
                dve.wait_ge(s["back"], 48)
                link(dve.tensor_copy(own[:, 0:WIDE], own_i[:]))
                link(dve.tensor_copy(own[:, WIDE:WIDE + 1], after_i[:, 0:1]))
                link(dve.tensor_scalar(high[:], own[:], own[:, 0:1], None, ALU.subtract))
                link(dve.tensor_tensor(own[:], high[:], low[:], ALU.is_lt))
                link(dve.tensor_reduce(bad[0:WIDE_GROUPS, 1:2], own[:, 1:WIDE], AX.X, ALU.add))
                link(dve.tensor_scalar(low[:], low[:], 2.0 * P, None, ALU.add))
                link(dve.tensor_tensor(own[:], high[:], low[:], ALU.is_gt))
                link(dve.tensor_reduce(bad[0:WIDE_GROUPS, 2:3], own[:, 1:WIDE + 1], AX.X, ALU.add))
                dve.tensor_reduce(bad[:, 3:4], bad[:, 0:3], AX.X, ALU.add).then_inc(s["bad"], 1)
                dve.wait_ge(s["total"], 1)
                link(dve.tensor_scalar(flag[:, 0:1], bank[0][0:1, 0:1], 0.5, None, ALU.is_lt))
                dve.tensor_copy(sorted_flag[:], flag[:, 0:1]).then_inc(s["flag"], 1)

            @block.tensor
            def _(pe):
                pe.wait_ge(s["bad"], 1)
                nc.tensor.matmul(bank[0][0:1, 0:1], bad[:, 3:4], ones[:], start=True, stop=True).then_inc(s["total"], 1)

        is_sorted = nc.values_load(sorted_flag[0:1, 0:1], min_val=0, max_val=1)

        MEETINGS = [(k, t) for k in range(WINDOW_TILES) for t in (k - 1, k, k + 1) if 0 <= t < WIDE]

        def band_block(S, k, t):
            return S[:, k, (t - k + 1) * P:(t - k + 2) * P]

        def compare_bands(S, numbers):
            for k in range(WINDOW_TILES):
                met = [t for kk, t in MEETINGS if kk == k]
                low, high = (met[0] - k + 1) * P, (met[-1] - k + 2) * P
                ins = nc.vector.tensor_scalar(S[:, k, low:high], band[:, low:high], numbers[:, 0, k:k + 1], None, ALU.is_equal)
            return ins

        def sum_bands(S, rows_of_tile, sums_of_tile):
            for t in range(WIDE):
                met = [k for k, tt in MEETINGS if tt == t]
                for k in met:
                    ins = nc.tensor.matmul(sums_of_tile(t), band_block(S, k, t), rows_of_tile(k), start=(k == met[0]), stop=(k == met[-1]))
            return ins

        def window_columns():
            COLS = WIDE_GROUPS * WINDOW_TILES
            ROWS_OF_CHUNK = 14 * WINDOW_TILES
            CHUNKS = COLS // ROWS_OF_CHUNK
            REST = COLS - CHUNKS * ROWS_OF_CHUNK
            assert 0 < REST < ROWS_OF_CHUNK <= P and COLS <= GROUP
            with ExitStack() as c:
                s = c.enter_context(phase_semaphores(nc, "wc_", ("loaded", "iota", "floats", "columns", "link", "done")))
                numbers_i = c.enter_context(nc.sbuf_tensor("wc_numbers_i", [P, 2, CHUNKS + 1, P], i32))
                numbers_f = c.enter_context(nc.sbuf_tensor("wc_numbers_f", [P, 3, CHUNKS + 1, P], f32))
                first_i = c.enter_context(nc.sbuf_tensor("wc_first_i", [P, WIDE_GROUPS, WINDOW_TILES], i32))
                first = c.enter_context(nc.sbuf_tensor("wc_first", [P, WIDE_GROUPS, WINDOW_TILES], f32))
                negative = c.enter_context(nc.sbuf_tensor("wc_negative", [P, WIDE_GROUPS, WINDOW_TILES], f32))
                block = c.enter_context(nc.Block())

                def parts(flat, tile):
                    whole_rows = flat[0:CHUNKS * ROWS_OF_CHUNK * P].rearrange("(c q p) -> q c p", q=ROWS_OF_CHUNK, p=P)
                    rest = flat[CHUNKS * ROWS_OF_CHUNK * P:COLS * P].rearrange("(q p) -> q p", p=P)
                    return (tile[0:ROWS_OF_CHUNK, 0:CHUNKS, :], whole_rows), (tile[0:REST, CHUNKS, :], rest)

                def by_group(flat):
                    return flat[:, 0:COLS].rearrange("p (g k) -> p g k", k=WINDOW_TILES)

                @block.sync
                def _(sp):
                    for flat, tile in ((windows_dst, numbers_i[:, 0]), (windows_src, numbers_i[:, 1]), (windows_ew, numbers_f[:, 2])):
                        for to, source in parts(flat, tile):
                            sp.dma_start(to, source).then_inc(s["loaded"], 16)

                @block.gpsimd
                def _(pool):
                    pool.iota(first_i[:], [[WIDE * P, WIDE_GROUPS], [P, WINDOW_TILES]], base=-P, channel_multiplier=0).then_inc(s["iota"], 1)

                @block.tensor
                def _(pe):
                    pe.wait_ge(s["loaded"], 96)
                    pe.wait_ge(s["floats"], 2)
                    for n in range(3):
                        for chunk in range(CHUNKS + 1):
                            q = ROWS_OF_CHUNK if chunk < CHUNKS else REST
                            at = chunk * ROWS_OF_CHUNK
                            ins = nc.tensor.transpose(bank[n][:, at:at + q], numbers_f[0:q, n, chunk, :], ident[0:q, 0:q])
                    ins.then_inc(s["columns"], 1)

                @block.vector
                def _(dve):
                    links = Links(dve, s["link"], 0)
                    link = links.link
                    dve.wait_ge(s["iota"], 1)
                    link(dve.tensor_copy(first[:], first_i[:]))
                    dve.wait_ge(s["loaded"], 96)
                    dve.tensor_copy(numbers_f[0:ROWS_OF_CHUNK, 0:2, 0:CHUNKS, :], numbers_i[0:ROWS_OF_CHUNK, :, 0:CHUNKS, :]).then_inc(s["floats"], 1)
                    dve.tensor_copy(numbers_f[0:REST, 0:2, CHUNKS, :], numbers_i[0:REST, :, CHUNKS, :]).then_inc(s["floats"], 1)
                    dve.wait_ge(s["columns"], 1)
                    link(dve.tensor_tensor(numbers_all[:, :, 0, :], by_group(bank[0]), first[:], ALU.subtract))
                    link(dve.tensor_copy(numbers_all[:, :, 1, :], by_group(bank[2])))
                    link(dve.tensor_copy(index_all[:, :, 0, :], by_group(bank[1])))
                    link(dve.tensor_scalar(negative[:], numbers_all[:, :, 1, :], 0.0, None, ALU.is_lt))
                    link(dve.tensor_scalar(index_all[:, :, 2, :], by_group(bank[0]), float(ROWS - 1), None, ALU.min))
                    dve.scalar_tensor_tensor(index_all[:, :, 1, :], by_group(bank[1]), 2.0, negative[:], ALU.mult, ALU.add).then_inc(s["done"], 1)

        class Parts:

            def __init__(self, parts, first, remainder, second, split):
                self.parts = parts
                self.first, self.remainder, self.second, self.split = first, remainder, second, split

            def act_first(self, act, g, h, rows):
                nc.scalar.activation(self.parts[h][:, :, 0, :], rows, ACT.Copy).then_inc(self.first, 1)

            def dve_remainder(self, dve, g, h, rows):
                dve.wait_ge(self.first, g + 1)
                nc.vector.tensor_tensor(rows, rows, self.parts[h][:, :, 0, :], ALU.subtract).then_inc(self.remainder, 1)

            def act_second(self, act, g, h, rows):
                act.wait_ge(self.remainder, g + 1)
                nc.scalar.activation(self.parts[h][:, :, 1, :], rows, ACT.Copy).then_inc(self.second, 1)

            def dve_third(self, dve, g, h, rows):
                dve.wait_ge(self.second, g + 1)
                nc.vector.tensor_tensor(self.parts[h][:, :, 2, :], rows, self.parts[h][:, :, 1, :], ALU.subtract).then_inc(self.split, 1)

        def node_tile_sums(pair, width):
            return lambda t: pair[t // 4][:, (t % 4) // 2 * GROUP + t % 2 * 3 * width:(t % 4) // 2 * GROUP + (t % 2 + 1) * 3 * width]

        def add_parts(pair, width, out):
            for half in range(2):
                parts = pair[half][:].rearrange("p (b n) -> p b n", b=2)[:, :, 0:6 * width].rearrange("p b (t m d) -> p b t d m", t=2, m=3)
                ins = nc.vector.tensor_reduce(out[:, half * 4:half * 4 + 4, :].rearrange("p (b t) d -> p b t d", b=2), parts, AX.X, ALU.add)
            return ins

        def window_sums(tag, table_rows, sums, width, gathered_from=None, signed=False):
            gathers = gathered_from is not None
            weighed = gathers and not signed
            with ExitStack() as c:
                s = c.enter_context(phase_semaphores(nc, tag, (
                    "numbers", "index", "S", "weighed", "first", "remainder", "second", "split", "agg", "out",
                    "rows_loaded0", "rows_loaded1", "out_stored0", "out_stored1", "sp_passed")))
                rows_loaded = [s[f"rows_loaded{h}"] for h in range(2)]
                out_stored = [s[f"out_stored{h}"] for h in range(2)]

                def buf(name, shape, dt=f32):
                    return [c.enter_context(nc.sbuf_tensor(f"{tag}{name}{h}", shape, dt)) for h in range(2)]

                K = WINDOW_TILES
                numbers, index = buf("numbers", [P, 2, K]), buf("index", [P, K], i32)
                in_rows, S, out = buf("rows", [P, K, width]), buf("S", [P, K, 3 * P], bf16), buf("out", [P, WIDE, width])
                parts = Parts(buf("parts", [P, K, 3, width], bf16), s["first"], s["remainder"], s["second"], s["split"])
                sums_psum = [wide_bank[0:2], wide_bank[2:4]]
                block = c.enter_context(nc.Block())

                if not gathers:
                    @block.sync
                    def _(sp):
                        def step(b, first, last):
                            if not first:
                                sp.wait_ge(s["split"], b.g - 1)
                            sp.sem_inc(s["sp_passed"], 1)
                            start = sp.value_load(starts[0:1, bass.ds(b.g * WIDE, 1)], min_val=0, max_val=ROWS)
                            sp.dma_start(in_rows[b.h][:], table_rows[bass.ds(start, WINDOW), :].rearrange("(k p) d -> p k d", p=P)
                                         ).then_inc(rows_loaded[b.h], 16)

                        pipeline(sp, step)
                else:
                    @block.gpsimd
                    def _(pool):
                        def step(b, first, last):
                            pool.wait_ge(s["index"], b.g + 1)
                            if not first:
                                pool.wait_ge(s["split"], b.g - 1)
                            pool.sem_inc(passed, 1)
                            for k in range(K):
                                pool.indirect_dma_start(in_rows[b.h][:, k, :], None, gathered_from,
                                                        bass.IndirectOffsetOnAxis(ap=index[b.h][:, k:k + 1], axis=0)
                                                        ).then_inc(rows_loaded[b.h], 16)

                        pipeline(pool, step)

                @block.tensor
                def _(pe):
                    def step(b, first, last):
                        if not first:
                            pe.wait_ge(s["out"], b.g - 1)
                        pe.wait_ge(s["S"], b.g + 1)
                        pe.wait_ge(s["split"], b.g + 1)
                        pe.sem_inc(pe_passed, 1)
                        sum_bands(S[b.h], lambda k: parts.parts[b.h][:, k, :, :].rearrange("p m d -> p (m d)"),
                                  node_tile_sums(sums_psum[b.h], width)).then_inc(s["agg"], 1)

                    pipeline(pe, step)

                @block.scalar
                def _(act):
                    def store(b):
                        act.wait_ge(s["out"], b.g + 1)
                        act.dma_start(sums[bass.ds(b.g * WIDE * P, WIDE * P), :].rearrange("(t p) d -> p t d", p=P), out[b.h][:]
                                      ).then_inc(out_stored[b.h], 16)

                    def step(b, first, last):
                        if not first:
                            act.wait_ge(s["agg"], b.g - 1)
                        if weighed:
                            act.wait_ge(s["weighed"], b.g + 1)
                        else:
                            act.wait_ge(rows_loaded[b.h], (b.round + 1) * (16 * K if gathers else 16))
                        parts.act_first(act, b.g, b.h, in_rows[b.h][:])
                        parts.act_second(act, b.g, b.h, in_rows[b.h][:])
                        if not first:
                            store(b.last())
                        if last:
                            store(b)

                    pipeline(act, step)
                    for h in range(2):
                        act.wait_ge(out_stored[h], 16 * IN_SLOT[h])

                @block.vector
                def _(dve):
                    def take_index(b, early):
                        if not early:
                            dve.wait_ge(rows_loaded[b.h], b.round * 16 * K)
                        nc.vector.tensor_scalar(index[b.h][:], index_all[:, bass.ds(b.g, 1), int(signed), :].rearrange("p g k -> p (g k)"),
                                                1.0, None, ALU.mult).then_inc(s["index"], 1)

                    def bands(b, early):
                        if not early:
                            dve.wait_ge(s["agg"], b.g - 1)
                        nc.vector.tensor_scalar(numbers[b.h][:], numbers_all[:, bass.ds(b.g, 1), :, :].rearrange("p g n k -> p (g n) k"),
                                                1.0, None, ALU.mult).then_inc(s["numbers"], 1)
                        dve.wait_ge(s["numbers"], b.g + 1)
                        compare_bands(S[b.h], numbers[b.h]).then_inc(s["S"], 1)

                    def take_sums(b):
                        dve.wait_ge(out_stored[b.h], b.round * 16)
                        dve.wait_ge(s["agg"], b.g + 1)
                        add_parts(sums_psum[b.h], width, out[b.h]).then_inc(s["out"], 1)

                    def step(b, first, last):
                        if first:
                            if gathers:
                                take_index(b, True)
                                take_index(b.next(), True)
                            bands(b, True)
                        dve.wait_ge(rows_loaded[b.h], (b.round + 1) * (16 * K if gathers else 16))
                        if weighed:
                            dve.wait_ge(s["S"], b.g + 1)
                            nc.vector.tensor_tensor(in_rows[b.h][:], in_rows[b.h][:], numbers[b.h][:, 1, :].unsqueeze(2).to_broadcast([P, K, width]),
                                                    ALU.mult).then_inc(s["weighed"], 1)
                        if gathers and b.ahead > 1:
                            take_index(b.next().next(), False)
                        if not first:
                            take_sums(b.last())
                        parts.dve_remainder(dve, b.g, b.h, in_rows[b.h][:])
                        parts.dve_third(dve, b.g, b.h, in_rows[b.h][:])
                        if not last:
                            bands(b.next(), first)
                        if last:
                            take_sums(b)

                    pipeline(dve, step)

        def window_attention(tag, sums):
            with ExitStack() as c:
                s = c.enter_context(phase_semaphores(nc, tag, (
                    "numbers", "index", "S", "agg", "out", "typed", "w", "score", "exp", "hw", "product",
                    "msg", "first", "remainder", "second", "split", "type_ids", "link", "feat_loaded0", "feat_loaded1",
                    "rows_loaded0", "rows_loaded1", "out_stored0", "out_stored1", "sp_passed")))
                feat_loaded = [s[f"feat_loaded{h}"] for h in range(2)]
                rows_loaded = [s[f"rows_loaded{h}"] for h in range(2)]
                out_stored = [s[f"out_stored{h}"] for h in range(2)]

                def buf(name, shape, dt=f32, slots=2):
                    return [c.enter_context(nc.sbuf_tensor(f"{tag}{name}{h}", shape, dt)) for h in range(slots)]

                K = WINDOW_TILES
                TW = EDGE_TYPES * (F_EDGE + 1)
                numbers, src_index, dst_index = buf("numbers", [P, 2, K], slots=1)[0], buf("src_index", [P, K], i32), buf("dst_index", [P, K], i32)
                h24_rows, h3_rows = buf("h24_rows", [P, K, 2 * D]), buf("h3_rows", [P, K, D])
                feat, types = buf("feat", [TW, WINDOW], slots=1)[0], buf("types", [TW, WINDOW], i32, slots=1)[0]
                typedT = buf("typedT", [TW, WINDOW], slots=1)[0]
                type_id_i, type_id = buf("type_id_i", [TW, 1], i32, slots=1)[0], buf("type_id", [TW, 1], slots=1)[0]
                type_step = buf("type_step", [TW, 5], slots=1)[0]
                S = buf("S", [P, K, 3 * P], bf16)
                parts = Parts(buf("parts", [P, K, 3, D], bf16), s["first"], s["remainder"], s["second"], s["split"])
                product, msg = buf("product", [P, K, D], slots=1)[0], buf("msg", [P, K, D], slots=1)[0]
                score, top, below, exped, total, quotient, weight = [buf(f"number{n}_", [P, K], slots=1)[0] for n in range(7)]
                out = buf("out", [P, WIDE, D])
                w_psum, last_psum = wide_bank[0], bank[2]
                sums_psum = wide_bank[2:4]
                block = c.enter_context(nc.Block())

                @block.sync
                def _(sp):
                    def load(b, first):
                        if not first:
                            sp.wait_ge(s["typed"], b.g)
                        sp.sem_inc(s["sp_passed"], 1)
                        start = sp.value_load(starts[0:1, bass.ds(b.g * WIDE, 1)], min_val=0, max_val=ROWS)
                        window = bass.ds(start, WINDOW)
                        sp.dma_start(feat[:], io["edge16_T"][:, window]).then_inc(feat_loaded[b.h], 16)
                        sp.dma_start(types[:], io["etype_lin"].unsqueeze(0)[:, window].to_broadcast([TW, WINDOW])).then_inc(feat_loaded[b.h], 16)

                    def step(b, first, last):
                        load(b, first)

                    pipeline(sp, step)

                @block.gpsimd
                def _(pool):
                    pool.iota(type_id_i[:], [[0, 1]], base=0, channel_multiplier=1).then_inc(s["type_ids"], 1)

                    def step(b, first, last):
                        pool.wait_ge(s["index"], b.g + 1)
                        if not first:
                            pool.wait_ge(s["msg"], b.g - 1)
                        pool.sem_inc(passed, 1)
                        for k in range(K):
                            pool.indirect_dma_start(h24_rows[b.h][:, k, :], None, h24_t,
                                                    bass.IndirectOffsetOnAxis(ap=src_index[b.h][:, k:k + 1], axis=0)
                                                    ).then_inc(rows_loaded[b.h], 16)
                            pool.indirect_dma_start(h3_rows[b.h][:, k, :], None, h3_t,
                                                    bass.IndirectOffsetOnAxis(ap=dst_index[b.h][:, k:k + 1], axis=0)
                                                    ).then_inc(rows_loaded[b.h], 16)

                    pipeline(pool, step)

                @block.tensor
                def _(pe):
                    def features(b, first):
                        if not first:
                            pe.wait_ge(s["hw"], b.g)
                        pe.wait_ge(s["typed"], b.g + 1)
                        pe.sem_inc(pe_passed, 1)
                        for k in range(K):
                            to = w_psum[:, k * 2 * D:(k + 1) * 2 * D] if k < WIDE else last_psum[:, 0:2 * D]
                            ins = nc.tensor.matmul(to, typedT[:, k * P:(k + 1) * P], W5[:].rearrange("p a d -> p (a d)"), start=True, stop=True)
                        ins.then_inc(s["w"], 1)

                    def step(b, first, last):
                        if first:
                            features(b, True)
                        if not last:
                            features(b.next(), False)
                        if not first:
                            pe.wait_ge(s["out"], b.g)
                        pe.wait_ge(s["split"], b.g + 1)
                        pe.wait_ge(s["S"], b.g + 1)
                        pe.sem_inc(pe_passed, 1)
                        sum_bands(S[b.h], lambda k: parts.parts[b.h][:, k, :, :].rearrange("p m d -> p (m d)"),
                                  node_tile_sums(sums_psum, D)).then_inc(s["agg"], 1)

                    pipeline(pe, step)

                @block.scalar
                def _(act):
                    def store(b):
                        act.wait_ge(s["out"], b.g + 1)
                        act.dma_start(sums[bass.ds(b.g * WIDE * P, WIDE * P), :].rearrange("(t p) d -> p t d", p=P), out[b.h][:]
                                      ).then_inc(out_stored[b.h], 16)

                    def step(b, first, last):
                        act.wait_ge(s["score"], b.g + 1)
                        nc.scalar.activation(exped[:], below[:], ACT.Exp).then_inc(s["exp"], 1)
                        if not first:
                            act.wait_ge(s["agg"], b.g - 1)
                        act.wait_ge(s["msg"], b.g + 1)
                        parts.act_first(act, b.g, b.h, msg[:])
                        parts.act_second(act, b.g, b.h, msg[:])
                        if not first:
                            store(b.last())
                        if last:
                            store(b)

                    pipeline(act, step)
                    for h in range(2):
                        act.wait_ge(out_stored[h], 16 * IN_SLOT[h])

                @block.vector
                def _(dve):
                    links = Links(dve, s["link"], 2 * 6)
                    link = links.link
                    dve.wait_ge(s["type_ids"], 1)
                    link(dve.tensor_copy(type_id[:], type_id_i[:]))
                    for a in range(1, EDGE_TYPES + 1):
                        link(dve.tensor_scalar(type_step[:, a:a + 1], type_id[:], float(a * F_EDGE), None, ALU.is_ge))
                    link(dve.tensor_scalar(type_id[:], type_id[:], -float(EDGE_TYPES * F_EDGE) - (EDGE_TYPES - 1), None, ALU.add))
                    link(dve.tensor_tensor(type_id[:], type_id[:], type_step[:, EDGE_TYPES:EDGE_TYPES + 1], ALU.mult))
                    for a in range(1, EDGE_TYPES):
                        link(dve.tensor_tensor(type_id[:], type_id[:], type_step[:, a:a + 1], ALU.add))

                    def take_index(b, early):
                        if not early:
                            dve.wait_ge(rows_loaded[b.h], b.round * 32 * K)
                        nc.vector.tensor_scalar(dst_index[b.h][:], index_all[:, bass.ds(b.g, 1), 2, :].rearrange("p g k -> p (g k)"),
                                                1.0, None, ALU.mult)
                        nc.vector.tensor_scalar(src_index[b.h][:], index_all[:, bass.ds(b.g, 1), 0, :].rearrange("p g k -> p (g k)"),
                                                1.0, None, ALU.mult).then_inc(s["index"], 1)

                    def bands(b, early):
                        if not early:
                            dve.wait_ge(s["agg"], b.g - 1)
                        dve.wait_ge(s["S"], b.g)
                        nc.vector.tensor_scalar(numbers[:], numbers_all[:, bass.ds(b.g, 1), :, :].rearrange("p g n k -> p (g n) k"),
                                                1.0, None, ALU.mult).then_inc(s["numbers"], 1)
                        dve.wait_ge(s["numbers"], b.g + 1)
                        compare_bands(S[b.h], numbers).then_inc(s["S"], 1)

                    def by_type(b, first):
                        if not first:
                            dve.wait_ge(s["w"], b.g)
                        dve.wait_ge(feat_loaded[b.h], (b.round + 1) * 32)
                        nc.vector.scalar_tensor_tensor(typedT[:], types[:], type_id[:, 0:1], feat[:], ALU.is_equal, ALU.mult).then_inc(s["typed"], 1)

                    def take_sums(b):
                        dve.wait_ge(out_stored[b.h], b.round * 16)
                        dve.wait_ge(s["agg"], b.g + 1)
                        add_parts(sums_psum, D, out[b.h]).then_inc(s["out"], 1)

                    def step(b, first, last):
                        if first:
                            take_index(b, True)
                            take_index(b.next(), True)
                            bands(b, True)
                            by_type(b, True)
                        dve.wait_ge(rows_loaded[b.h], (b.round + 1) * 32 * K)
                        dve.wait_ge(s["w"], b.g + 1)
                        h24 = h24_rows[b.h]
                        nc.vector.tensor_tensor(h24[:, 0:WIDE, :], h24[:, 0:WIDE, :], wide_rows(w_psum, 2 * D), ALU.add)
                        nc.vector.tensor_tensor(h24[:, WIDE, :], h24[:, WIDE, :], last_psum[:, 0:2 * D], ALU.add).then_inc(s["hw"], 1)
                        dve.wait_ge(s["hw"], b.g + 1)
                        nc.vector.tensor_tensor(product[:], h24[:, :, D:2 * D], h3_rows[b.h][:], ALU.mult).then_inc(s["product"], 1)
                        dve.wait_ge(s["product"], b.g + 1)
                        link(nc.vector.tensor_reduce(score[:], product[:], AX.X, ALU.add))
                        link(nc.vector.tensor_scalar(weight[:], score[:], HEAD_DIM ** -0.5, None, ALU.mult))
                        link(nc.vector.tensor_reduce(top[:], weight[:].unsqueeze(2), AX.X, ALU.max))
                        nc.vector.tensor_tensor(below[:], weight[:], top[:], ALU.subtract).then_inc(s["score"], 1)
                        if not last:
                            by_type(b.next(), False)
                        if b.ahead > 1:
                            take_index(b.next().next(), False)
                        if not first:
                            take_sums(b.last())
                            dve.wait_ge(s["split"], b.g)
                        dve.wait_ge(s["exp"], b.g + 1)
                        link(nc.vector.tensor_reduce(total[:], exped[:].unsqueeze(2), AX.X, ALU.add))
                        link(nc.vector.reciprocal(quotient[:], total[:]))
                        link(nc.vector.tensor_tensor(weight[:], exped[:], quotient[:], ALU.mult))
                        nc.vector.tensor_tensor(msg[:], h24[:, :, 0:D], weight[:].unsqueeze(2).to_broadcast([P, K, D]), ALU.mult).then_inc(s["msg"], 1)
                        if not last:
                            bands(b.next(), first)
                        parts.dve_remainder(dve, b.g, b.h, msg[:])
                        parts.dve_third(dve, b.g, b.h, msg[:])
                        if last:
                            take_sums(b)

                    pipeline(dve, step, links)

        def by_order(in_order, in_any_order):
            with nc.If(is_sorted == 1):
                nc.all_engine_barrier()
                in_order()
                nc.all_engine_barrier()
            with nc.Else():
                nc.all_engine_barrier()
                in_any_order()
                nc.all_engine_barrier()

        def edge_messages(tag, in_order):
            indices = TILES if in_order else 2 * TILES
            with ExitStack() as c:
                s = c.enter_context(phase_semaphores(nc, tag, (
                    "idx_f", "wide", "same", "scat_idx", "transposed", "in_T", "hidden", "hidden_T",
                    "out", "msg", "sums", "rows", "rows_free", "link", "ones_set", "msg_stored0", "msg_stored1",
                    "windows", "sp_passed")))
                msg_stored = [s["msg_stored0"], s["msg_stored1"]]
                (idx, cat, side, extra, feat, scat_idx, rows_a, rows_b, idx_f, gidx,
                 same, masked, small, msg, typed, catT, sideT, hiddenT, work, hw) = edge_buffers(c, tag)
                msg = [c.enter_context(nc.sbuf_tensor(f"{tag}messages{h}", [P, TILES, D_RECV], f32)) for h in range(2)]
                block = c.enter_context(nc.Block())

                @block.sync
                def _(sp):
                    def load(h, it):
                        sp.wait_ge(in_free[h], it + free_at)
                        sp.dma_start(idx[h][:], io["idx"][bass.ds((it * 2 + h) * P, P), :]).then_inc(idx_loaded[h], 16)
                        sp.dma_start(cat[h][:, :, 0:D], group_of(io["edge64"], it * 2 + h)).then_inc(loaded[h], 16)

                    def copy_window(group):
                        sp.sem_inc(s["sp_passed"], 1)
                        start = sp.value_load(starts[0:1, bass.ds(group * WIDE, 1)], min_val=0, max_val=ROWS)
                        for tab, name in ((windows_dst, "dst_lin"), (windows_src, "src_lin"), (windows_ew, "ew_lin")):
                            sp.dma_start(tab[bass.ds(group * WINDOW, WINDOW)], io[name][bass.ds(start, WINDOW)]).then_inc(s["windows"], 16)

                    def store(h, it):
                        if in_order:
                            sp.wait_ge(s["msg"], (it * 2 + h) * 2 + 2)
                            sp.dma_start(group_of(messages_t, it * 2 + h, D_RECV), msg[h][:]).then_inc(msg_stored[h], 16)

                    for h in range(2):
                        load(h, 0)
                    with sp.Fori(0, STEPS - 1, 1) as it:
                        for h in range(2):
                            load(h, it + 1)
                            store(h, it)
                        if in_order:
                            copy_window(it)
                    for h in range(2):
                        store(h, STEPS - 1)
                    if in_order:
                        copy_window(WIDE_GROUPS - 1)
                        sp.wait_ge(s["windows"], 48 * WIDE_GROUPS)
                        for h in range(2):
                            sp.wait_ge(msg_stored[h], STEPS * 16)

                @block.gpsimd
                def _(pool):
                    def gather(t, h, it):
                        pool.wait_ge(idx_loaded[h], it * 16 + 16 + idx_at)
                        pool.sem_inc(passed, 1)
                        pool.indirect_dma_start(cat[h][:, t, D:2 * D], None, io["x"],
                                                bass.IndirectOffsetOnAxis(ap=idx[h][:, t:t + 1], axis=0)
                                                ).then_inc(gath_a[h][t], 16)
                        pool.indirect_dma_start(side[h][:, t, 0:D], None, io["x"],
                                                bass.IndirectOffsetOnAxis(ap=idx[h][:, TILES + t:TILES + t + 1], axis=0)
                                                ).then_inc(gath_b[h][t], 16)

                    def scatter(t, h, g):
                        k = t % 2
                        pool.wait_ge(sent_done[k], g * (16 * TILES // 2) + 16 * (t // 2))
                        if t == 0:
                            pool.wait_ge(s["scat_idx"], g + 1)
                            pool.wait_ge(s["rows"], g + 1)
                        if not in_order:
                            pool.wait_ge(recv_done, g * (16 * TILES) + 16 * t)
                        if t == 1:
                            pool.sem_inc(s["rows_free"], 1)
                        pool.sem_inc(passed, 1)
                        pool.indirect_dma_start(sent_sum[k], bass.IndirectOffsetOnAxis(ap=scat_idx[h][:, t:t + 1], axis=0),
                                                rows_b[h][:, t, :], None, compute_op=ALU.add
                                                ).then_inc(sent_done[k], 16)
                        if not in_order:
                            pool.indirect_dma_start(recv_sum, bass.IndirectOffsetOnAxis(ap=scat_idx[h][:, TILES + t:TILES + t + 1], axis=0),
                                                    rows_a[h][:, t, :], None, compute_op=ALU.add
                                                    ).then_inc(recv_done, 16)

                    for t in range(TILES):
                        gather(t, 0, 0)
                    for t in range(TILES):
                        gather(t, 1, 0)
                    pool.wait_ge(cleared, 2 * 96 + (16 if in_order else 96))
                    with pool.Fori(0, STEPS - 1, 1) as it:
                        for h in range(2):
                            for t in range(TILES):
                                gather(t, h, it + 1)
                                scatter(t, h, it * 2 + h)
                    for h in range(2):
                        for t in range(TILES):
                            scatter(t, h, GROUPS - 2 + h)
                    for k in range(2):
                        pool.wait_ge(sent_done[k], GROUPS * TILES // 2 * 16)
                    if not in_order:
                        pool.wait_ge(recv_done, GROUPS * TILES * 16)
                    pool.wait_ge(cleared_later, (3 if in_order else 6) * 96)

                @block.vector
                def _(dve):
                    n = indices
                    for h in range(2):
                        dve.memset(msg[h][:, :, ONE_COL:ONE_COL + 1], 1.0).then_inc(s["ones_set"], 1)
                    dve.wait_ge(ready, 6)
                    with dve.Fori(0, STEPS, 1) as it:
                        link, end = linker(dve, s["link"], it, 10 if in_order else 12)
                        for h in range(2):
                            g = it * 2 + h
                            dve.wait_ge(s["wide"], g)
                            dve.wait_ge(s["scat_idx"], g)
                            dve.wait_ge(idx_loaded[h], it * 16 + 16 + idx_at)
                            nc.vector.tensor_copy(idx_f[:], idx[h][:]).then_inc(s["idx_f"], 1)
                            dve.wait_ge(s["sums"], g)
                            if in_order:
                                dve.wait_ge(msg_stored[h], it * 16)
                            nc.vector.tensor_scalar(msg[h][:, :, EW_COL], ew_all[:, bass.ds(g * TILES, TILES)], 1.0, None, ALU.mult
                                                    ).then_inc(s["msg"], 1)
                            dve.wait_ge(s["idx_f"], g + 1)
                            dve.wait_ge(s["wide"], g + 1)
                            link(nc.vector.tensor_tensor(
                                same[:, 0:n, :], wide_bank[0][:, 0:n * P].rearrange("p (t j) -> p t j", t=n),
                                idx_f[:, 0:n].unsqueeze(2).to_broadcast([P, n, P]), ALU.is_equal))
                            dve.sem_inc(s["same"], 1)
                            link(nc.vector.tensor_tensor(masked[:, 0:n, :], same[:, 0:n, :], earlier[:].unsqueeze(1).to_broadcast([P, n, P]), ALU.mult))
                            link(nc.vector.tensor_reduce(small[0][:, 0:n], masked[:, 0:n, :], AX.X, ALU.add))
                            link(nc.vector.tensor_scalar(small[1][:, 0:n], idx_f[:, 0:n], dump_row[:, 0:1], -1.0, ALU.subtract, ALU.mult))
                            link(nc.vector.scalar_tensor_tensor(small[2][:, 0:n], small[0][:, 0:n], 1.0, small[1][:, 0:n], ALU.min, ALU.mult))
                            dve.wait_ge(s["out"], g + 1)
                            nc.vector.tensor_tensor(msg[h][:, :, 0:D], bank[5][:, 0:TILES * D].rearrange("p (t d) -> p t d", t=TILES),
                                                    be2[:].unsqueeze(1).to_broadcast([P, TILES, D]), ALU.add).then_inc(s["msg"], 1)
                            dve.wait_ge(s["rows_free"], g)
                            if not in_order:
                                link(nc.vector.tensor_tensor(recv_all[:, bass.ds(g * TILES, TILES)], small[2][:, TILES:2 * TILES],
                                                             idx_f[:, TILES:2 * TILES], ALU.add))
                            nc.vector.tensor_tensor(scat_idx[h][:, 0:n], small[2][:, 0:n], idx_f[:, 0:n], ALU.add).then_inc(s["scat_idx"], 1)
                        end()

                @block.tensor
                def _(pe):
                    pe.wait_ge(ready, 6)
                    pe.wait_ge(s["ones_set"], 2)
                    with pe.Fori(0, STEPS, 1) as it:
                        for h in range(2):
                            g = it * 2 + h
                            pe.wait_ge(s["same"], g)
                            pe.wait_ge(s["idx_f"], g + 1)
                            for k in range(indices):
                                last = nc.tensor.transpose(wide_bank[0][:, k * P:(k + 1) * P], idx_f[:, k:k + 1].to_broadcast([P, P]), ident[:])
                            last.then_inc(s["wide"], 1)
                            pe.wait_ge(s["in_T"], g)
                            pe.wait_ge(loaded[h], it * 16 + 16 + loaded_at[h])
                            for t in range(TILES):
                                pe.wait_ge(gath_a[h][t], it * 16 + 16)
                                pe.wait_ge(gath_b[h][t], it * 16 + 16)
                                pe.wait_ge(ready, 6)
                                nc.tensor.transpose(bank[2][:, t * P:(t + 1) * P], cat[h][:, t, :], ident[:])
                                last = nc.tensor.transpose(bank[3][0:D, t * P:(t + 1) * P], side[h][:, t, 0:D], ident[:])
                            last.then_inc(s["transposed"], 1)
                            pe.wait_ge(s["transposed"], g + 1)
                            pe.sem_inc(in_free[h], 1)
                            pe.wait_ge(s["in_T"], g + 1)
                            nc.tensor.matmul(bank[4][:], We1a[:], catT[:], start=True, stop=False)
                            nc.tensor.matmul(bank[4][:], We1b[:], sideT[0:D, :], start=False, stop=True).then_inc(s["hidden"], 1)
                            pe.wait_ge(s["hidden_T"], g + 1)
                            for t in range(TILES):
                                last = nc.tensor.matmul(bank[5][:, t * D:(t + 1) * D], hiddenT[:, t * P:(t + 1) * P], We2[:], start=True, stop=True)
                            last.then_inc(s["out"], 1)
                            pe.wait_ge(s["rows"], g)
                            pe.wait_ge(s["same"], g + 1)
                            pe.wait_ge(s["msg"], g * 2 + 2)
                            for t in range(TILES):
                                last = nc.tensor.matmul(bank[6][:, t * D:(t + 1) * D], same[:, t, :], msg[h][:, t, 0:D], start=True, stop=True)
                                if not in_order:
                                    last = nc.tensor.matmul(bank[7][:, t * D_RECV:(t + 1) * D_RECV], same[:, TILES + t, :], msg[h][:, t, :], start=True, stop=True)
                            last.then_inc(s["sums"], 1)

                @block.scalar
                def _(act):
                    if in_order:
                        act.dma_start(messages_t[ROWS:ROWS + WINDOW, :].rearrange("(p r) d -> p (r d)", p=P), zeros[:, 0:WINDOW_TILES * D_RECV]
                                      ).then_inc(cleared, 16)
                        for tab in (conv_sum[1], attn_sum[1], sign_sum[1]):
                            clear(act, tab, cleared_later)
                    else:
                        clear(act, recv_sum, cleared)
                        for tab in conv_sum + attn_sum + sign_sum:
                            clear(act, tab, cleared_later)
                    with act.Fori(0, STEPS, 1) as it:
                        for h in range(2):
                            g = it * 2 + h
                            act.wait_ge(s["hidden"], g)
                            act.wait_ge(s["transposed"], g + 1)
                            nc.scalar.activation(catT[:], bank[2][:], ACT.Copy)
                            nc.scalar.activation(sideT[0:D, :], bank[3][0:D, :], ACT.Copy).then_inc(s["in_T"], 1)
                            act.wait_ge(s["out"], g)
                            act.wait_ge(s["hidden"], g + 1)
                            nc.scalar.activation(hiddenT[:], bank[4][:], ACT.Relu, bias=be1[:, 0:1]).then_inc(s["hidden_T"], 1)
                            act.wait_ge(s["rows_free"], g)
                            act.wait_ge(s["sums"], g + 1)
                            if not in_order:
                                nc.scalar.activation(rows_a[h][:], bank[7][:, 0:TILES * D_RECV].rearrange("p (t d) -> p t d", t=TILES), ACT.Copy)
                            nc.scalar.activation(rows_b[h][:], bank[6][:, 0:TILES * D].rearrange("p (t d) -> p t d", t=TILES), ACT.Copy
                                                 ).then_inc(s["rows"], 1)

        def layer_0_in_order():
            edge_messages("m0_", in_order=True)
            window_columns()
            window_sums("w0_", messages_t, recv_sum, D_RECV)

        by_order(layer_0_in_order, lambda: edge_messages("e0_", in_order=False))
        gathers_a += STEPS * 16
        gathers_b += STEPS * 16
        idx_at += STEPS * 16
        loaded_at = [at + STEPS * 16 for at in loaded_at]
        free_at += STEPS

        def wide_buffers(c, tag):
            def rows(name, width=D, slots=None):
                def one(n):
                    return c.enter_context(nc.sbuf_tensor(tag + n, [P, WIDE, width], f32))
                return one(name) if slots is None else [one(f"{name}{h}") for h in range(slots)]

            def numbers(*names):
                return [c.enter_context(nc.sbuf_tensor(tag + n, [P, WIDE], f32)) for n in names]
            return rows, numbers

        def per_row(numbers):
            return numbers.unsqueeze(2).to_broadcast([P, WIDE, D])

        def wide_rows(flat, width=D):
            return flat[:, 0:WIDE * width].rearrange("p (t d) -> p t d", t=WIDE)

        class Norm:

            def __init__(self, rows, numbers):
                self.centred, self.square = rows("centred"), rows("square")
                self.total, self.mean, self.sum_sq, self.var, self.std, self.rstd = numbers(
                    "total", "mean", "sum_sq", "var", "std", "rstd")

            def centre(self, link, v, centred):
                link(nc.vector.tensor_reduce(self.total[:], v, AX.X, ALU.add))
                link(nc.vector.tensor_scalar(self.mean[:], self.total[:], 1.0 / D, None, ALU.mult))
                nc.vector.tensor_tensor(self.centred[:], v, per_row(self.mean[:]), ALU.subtract).then_inc(centred, 1)

            def variance(self, dve, link, g, square, var):
                dve.wait_ge(square, g + 1)
                link(nc.vector.tensor_reduce(self.sum_sq[:], self.square[:], AX.X, ALU.add))
                nc.vector.tensor_scalar(self.var[:], self.sum_sq[:], 1.0 / D, LN_EPS, ALU.mult, ALU.add).then_inc(var, 1)

            def scale(self, dve, link, out, g, std, done):
                dve.wait_ge(std, g + 1)
                link(nc.vector.reciprocal(self.rstd[:], self.std[:]))
                nc.vector.tensor_tensor(out, self.centred[:], per_row(self.rstd[:]), ALU.mult).then_inc(done, 1)

            def act_square(self, act, g, centred, square):
                act.wait_ge(centred, g + 1)
                nc.scalar.activation(self.square[:], self.centred[:], ACT.Square).then_inc(square, 1)

            def act_root(self, act, g, var, std):
                act.wait_ge(var, g + 1)
                nc.scalar.activation(self.std[:], self.var[:], ACT.Sqrt).then_inc(std, 1)

        with ExitStack() as c:
            s = c.enter_context(phase_semaphores(nc, "n0_", (
                "transposed", "in_T", "hidden", "hidden_T", "out", "x1", "y1", "biased", "deg", "root_deg",
                "dis", "centred", "square", "var", "std", "link", "pool_link")))
            rows, numbers = wide_buffers(c, "n0_")
            norm = Norm(rows, numbers)
            inp = rows("in", 2 * D, 2)
            received = rows("received", D + D_RECV, 2)
            biased, x1, y1 = rows("biased", D, 2), rows("x1_", D, 2), rows("y1_", D, 2)
            v = rows("v")
            degree, kept, not_positive, safe, root, rroot, at_least_1, positive = numbers(
                "degree", "kept", "not_positive", "safe", "root", "rroot", "at_least_1", "positive")
            dis = numbers("dis0", "dis1")
            inT = c.enter_context(nc.sbuf_tensor("n0_inT", [P, WIDE * P], f32))
            receivedT = c.enter_context(nc.sbuf_tensor("n0_receivedT", [P, WIDE * P], f32))
            hidT = c.enter_context(nc.sbuf_tensor("n0_hidT", [HID, WIDE * P], f32))
            in_psum, received_psum, hid_psum, out_psum = wide_bank[0], wide_bank[1], wide_bank[2], bank[6]
            block = c.enter_context(nc.Block())

            @block.sync
            def _(sp):
                def load(b, early):
                    if not early:
                        sp.wait_ge(s["biased"], b.g - 1)
                        sp.wait_ge(s["transposed"], b.g - 1)
                        sp.wait_ge(s["dis"], b.g - 1)
                    sp.dma_start(inp[b.h][:, :, 0:D], wide_group_of(io["x"], b.g)).then_inc(loaded[b.h], 16)
                    sp.dma_start(inp[b.h][:, :, D:2 * D], wide_group_of(sent_sum[0], b.g)).then_inc(loaded[b.h], 16)
                    sp.dma_start(received[b.h][:, :, 0:D], wide_group_of(sent_sum[1], b.g)).then_inc(loaded[b.h], 16)
                    sp.dma_start(received[b.h][:, :, D:D + D_RECV], wide_group_of(recv_sum, b.g, D_RECV)).then_inc(loaded[b.h], 16)

                def step(b, first, last):
                    if first:
                        load(b, True)
                    if not last:
                        load(b.next(), first)

                pipeline(sp, step)

            @block.tensor
            def _(pe):
                def transposes(b, first):
                    if not first:
                        pe.wait_ge(s["in_T"], b.g)
                    pe.wait_ge(loaded[b.h], b.round * 64 + 64 + loaded_at[b.h])
                    pe.sem_inc(pe_passed, 1)
                    for t in range(WIDE):
                        nc.tensor.transpose(in_psum[:, t * P:(t + 1) * P], inp[b.h][:, t, :], ident[:])
                        last = nc.tensor.transpose(received_psum[:, t * P:(t + 1) * P], received[b.h][:, t, 0:2 * D], ident[:])
                    last.then_inc(s["transposed"], 1)

                def hidden(b, first):
                    if not first:
                        pe.wait_ge(s["hidden_T"], b.g)
                    pe.wait_ge(s["in_T"], b.g + 1)
                    for half in range(2):
                        cols = slice(half * 4 * P, (half + 1) * 4 * P)
                        nc.tensor.matmul(hid_psum[:, cols], Wn1a[:], inT[:, cols], start=True, stop=False)
                        last = nc.tensor.matmul(hid_psum[:, cols], Wn1b[:], receivedT[:, cols], start=False, stop=True)
                    last.then_inc(s["hidden"], 1)

                def step(b, first, last):
                    if first:
                        transposes(b, True)
                        hidden(b, True)
                    if not last:
                        transposes(b.next(), False)
                    if not first:
                        pe.wait_ge(s["centred"], b.g)
                    pe.wait_ge(s["hidden_T"], b.g + 1)
                    for t in range(WIDE):
                        out = nc.tensor.matmul(out_psum[:, t * D:(t + 1) * D], hidT[:, t * P:(t + 1) * P], Wn2[:], start=True, stop=True)
                    out.then_inc(s["out"], 1)
                    if not last:
                        hidden(b.next(), False)

                pipeline(pe, step)

            @block.scalar
            def _(act):
                def inputs(b, first):
                    if not first:
                        act.wait_ge(s["hidden"], b.g)
                    act.wait_ge(s["transposed"], b.g + 1)
                    nc.scalar.activation(inT[:], in_psum[:], ACT.Copy)
                    nc.scalar.activation(receivedT[:], received_psum[:], ACT.Copy).then_inc(s["in_T"], 1)

                def degree_root(b):
                    act.wait_ge(s["deg"], b.g + 1)
                    nc.scalar.activation(root[:], safe[:], ACT.Sqrt).then_inc(s["root_deg"], 1)

                def store(b):
                    act.wait_ge(s["y1"], b.g + 1)
                    act.dma_start(wide_group_of(y1_t, b.g), y1[b.h][:]).then_inc(stored[b.h], 16)

                def relu(b, first):
                    if not first:
                        act.wait_ge(s["out"], b.g)
                    act.wait_ge(s["hidden"], b.g + 1)
                    nc.scalar.activation(hidT[:], hid_psum[:], ACT.Relu, bias=bn1[:, 0:1]).then_inc(s["hidden_T"], 1)

                def step(b, first, last):
                    if first:
                        inputs(b, True)
                        degree_root(b)
                        relu(b, True)
                    if not last:
                        inputs(b.next(), False)
                    norm.act_square(act, b.g, s["centred"], s["square"])
                    if not last:
                        degree_root(b.next())
                    norm.act_root(act, b.g, s["var"], s["std"])
                    if not first:
                        store(b.last())
                    if not last:
                        relu(b.next(), False)
                    if last:
                        store(b)

                pipeline(act, step)
                for h in range(2):
                    act.wait_ge(stored[h], stored_at[h] + 16 * IN_SLOT[h])

            @block.gpsimd
            def _(pool):
                links = Links(pool, s["pool_link"], 2, passed)

                def double(b, first):
                    if not first:
                        pool.wait_ge(s["centred"], b.g - 1)
                    pool.wait_ge(loaded[b.h], b.round * 64 + 64 + loaded_at[b.h])
                    pool.sem_inc(passed, 1)
                    links.link(pool.tensor_scalar(biased[b.h][:], inp[b.h][:, :, 0:D], 2.0, None, ALU.mult))
                    pool.tensor_tensor(biased[b.h][:], biased[b.h][:], bn2[:].unsqueeze(1).to_broadcast([P, WIDE, D]), ALU.add
                                       ).then_inc(s["biased"], 1)

                def step(b, first, last):
                    if first:
                        double(b, True)
                    if not last:
                        double(b.next(), False)
                    pool.wait_ge(s["dis"], b.g + 1)
                    pool.wait_ge(s["x1"], b.g + 1)
                    pool.sem_inc(passed, 1)
                    pool.tensor_copy(x_all[:, b.tiles, :], x1[b.h][:])
                    pool.wait_ge(stored[b.h], b.round * 16 + stored_at[b.h])
                    pool.sem_inc(passed, 1)
                    pool.tensor_tensor(y1[b.h][:], x1[b.h][:], per_row(dis[b.h][:]), ALU.mult).then_inc(s["y1"], 1)

                pipeline(pool, step, links)

            @block.vector
            def _(dve):
                links = Links(dve, s["link"], 2 * 14)
                link = links.link

                def degrees(b):
                    deg, count = received[b.h][:, :, D + EW_COL], received[b.h][:, :, D + ONE_COL]
                    dve.wait_ge(loaded[b.h], b.round * 64 + 64 + loaded_at[b.h])
                    link(nc.vector.tensor_scalar(degree[:], deg, 1.0, None, ALU.add))
                    link(nc.vector.tensor_scalar(positive[:], degree[:], 0.0, None, ALU.is_gt))
                    link(nc.vector.tensor_tensor(kept[:], degree[:], positive[:], ALU.mult))
                    link(nc.vector.tensor_scalar(not_positive[:], positive[:], -1.0, 1.0, ALU.mult, ALU.add))
                    nc.vector.tensor_tensor(safe[:], kept[:], not_positive[:], ALU.add).then_inc(s["deg"], 1)
                    link(nc.vector.tensor_scalar(at_least_1[:], count, 1.0, None, ALU.max))
                    link(nc.vector.reciprocal(rcount_all[:, b.tiles], at_least_1[:]))

                def dis_of(b, first):
                    if not first:
                        dve.wait_ge(s["y1"], b.g - 1)
                    dve.wait_ge(s["root_deg"], b.g + 1)
                    link(nc.vector.reciprocal(rroot[:], root[:]))
                    link(nc.vector.tensor_tensor(dis[b.h][:], rroot[:], positive[:], ALU.mult))
                    link(nc.vector.tensor_copy(dis_all[:, b.tiles], dis[b.h][:]))
                    dve.sem_inc(s["dis"], 1)

                def step(b, first, last):
                    if first:
                        degrees(b)
                        dis_of(b, True)
                    dve.wait_ge(s["biased"], b.g + 1)
                    dve.wait_ge(s["out"], b.g + 1)
                    link(nc.vector.tensor_tensor(v[:], biased[b.h][:], wide_rows(out_psum), ALU.add))
                    norm.centre(link, v[:], s["centred"])
                    if not last:
                        degrees(b.next())
                    norm.variance(dve, link, b.g, s["square"], s["var"])
                    if not last:
                        dis_of(b.next(), False)
                    norm.scale(dve, link, x1[b.h][:], b.g, s["std"], s["x1"])

                pipeline(dve, step, links)
        loaded_at = [loaded_at[h] + IN_SLOT[h] * 64 for h in range(2)]
        stored_at = [stored_at[h] + IN_SLOT[h] * 16 for h in range(2)]

        def tiled(flat, width, tiles=TILES):
            return flat[:, 0:tiles * width].rearrange("p (t d) -> p t d", t=tiles)

        def edge_sums(tag, gathered_from, sums, signed):
            before, adds_before = gathers_a, adds
            with ExitStack() as c:
                s = c.enter_context(phase_semaphores(nc, tag, (
                    "idx_f", "wide", "same", "gidx", "scat_idx", "msg", "sums", "rows", "rows_free", "link")))
                (idx, cat, side, extra, feat, scat_idx, rows_a, rows_b, idx_f, gidx,
                 same, masked, small, msg, typed, catT, sideT, hiddenT, work, hw) = edge_buffers(c, tag)
                block = c.enter_context(nc.Block())

                @block.sync
                def _(sp):
                    with sp.Fori(0, STEPS, 1) as it:
                        for h in range(2):
                            g = it * 2 + h
                            sp.wait_ge(in_free[h], it + free_at)
                            sp.dma_start(idx[h][:], io["idx"][bass.ds(g * P, P), :]).then_inc(idx_loaded[h], 16)

                @block.gpsimd
                def _(pool):
                    def gather(t, h, it):
                        if t == 0 and signed:
                            pool.wait_ge(s["gidx"], it * 2 + h + 1)
                        pool.wait_ge(idx_loaded[h], it * 16 + 16 + idx_at)
                        pool.sem_inc(passed, 1)
                        index = gidx[h] if signed else idx[h]
                        pool.indirect_dma_start(cat[h][:, t, 0:D], None, gathered_from,
                                                bass.IndirectOffsetOnAxis(ap=index[:, t:t + 1], axis=0)
                                                ).then_inc(gath_a[h][t], 16)

                    def scatter(t, h, g):
                        k = t % 2
                        pool.wait_ge(added[k], g * (16 * TILES // 2) + 16 * (t // 2) + adds_before)
                        if t == 0:
                            pool.wait_ge(s["scat_idx"], g + 1)
                            pool.wait_ge(s["rows"], g + 1)
                        if t == 1:
                            pool.sem_inc(s["rows_free"], 1)
                        pool.sem_inc(passed, 1)
                        pool.indirect_dma_start(sums[k], bass.IndirectOffsetOnAxis(ap=scat_idx[h][:, t:t + 1], axis=0),
                                                rows_b[h][:, t, :], None, compute_op=ALU.add).then_inc(added[k], 16)

                    for t in range(TILES):
                        gather(t, 0, 0)
                    with pool.Fori(0, STEPS - 1, 1) as it:
                        for t in range(TILES):
                            gather(t, 1, it)
                            scatter(t, 0, it * 2)
                        for t in range(TILES):
                            gather(t, 0, it + 1)
                            scatter(t, 1, it * 2 + 1)
                    for t in range(TILES):
                        gather(t, 1, STEPS - 1)
                        scatter(t, 0, GROUPS - 2)
                    for t in range(TILES):
                        scatter(t, 1, GROUPS - 1)
                    for k in range(2):
                        pool.wait_ge(added[k], GROUPS * TILES * 8 + adds_before)

                @block.vector
                def _(dve):
                    with dve.Fori(0, STEPS, 1) as it:
                        link, end = linker(dve, s["link"], it, 2 if signed else 0)
                        for h in range(2):
                            g = it * 2 + h
                            cols = bass.ds(g * TILES, TILES)
                            dve.wait_ge(s["wide"], g)
                            dve.wait_ge(s["same"], g)
                            if signed:
                                dve.wait_ge(s["gidx"], g)
                            dve.wait_ge(idx_loaded[h], it * 16 + 16 + idx_at)
                            nc.vector.tensor_copy(idx_f[:], idx[h][:]).then_inc(s["idx_f"], 1)
                            if signed:
                                link(nc.vector.tensor_scalar(small[0][:, 0:TILES], ew_all[:, cols], 0.0, None, ALU.is_lt))
                                dve.wait_ge(s["idx_f"], g + 1)
                                nc.vector.scalar_tensor_tensor(gidx[h][:], idx_f[:, 0:TILES], 2.0, small[0][:, 0:TILES], ALU.mult, ALU.add
                                                               ).then_inc(s["gidx"], 1)
                            dve.wait_ge(s["idx_f"], g + 1)
                            dve.wait_ge(s["sums"], g)
                            dve.wait_ge(s["wide"], g + 1)
                            nc.vector.tensor_tensor(same[:, 0:TILES, :], tiled(bank[g_wide], P),
                                                    idx_f[:, TILES:2 * TILES].unsqueeze(2).to_broadcast([P, TILES, P]), ALU.is_equal
                                                    ).then_inc(s["same"], 1)
                            dve.wait_ge(s["rows_free"], g)
                            nc.vector.tensor_scalar(scat_idx[h][:, 0:TILES], recv_all[:, cols], 1.0, None, ALU.mult).then_inc(s["scat_idx"], 1)
                            if not signed:
                                for t in range(TILES):
                                    dve.wait_ge(gath_a[h][t], it * 16 + 16 + before)
                                nc.vector.tensor_tensor(msg[:, :, 0:D], cat[h][:, :, 0:D], over_features(ew_all[:, cols]), ALU.mult
                                                        ).then_inc(s["msg"], 1)
                        end()

                @block.tensor
                def _(pe):
                    with pe.Fori(0, STEPS, 1) as it:
                        for h in range(2):
                            g = it * 2 + h
                            pe.wait_ge(s["same"], g)
                            pe.wait_ge(s["idx_f"], g + 1)
                            for t in range(TILES):
                                last = nc.tensor.transpose(bank[g_wide][:, t * P:(t + 1) * P],
                                                           idx_f[:, TILES + t:TILES + t + 1].to_broadcast([P, P]), ident[:])
                            last.then_inc(s["wide"], 1)
                            pe.wait_ge(s["rows"], g)
                            if signed:
                                for t in range(TILES):
                                    pe.wait_ge(gath_a[h][t], it * 16 + 16 + before)
                            else:
                                pe.wait_ge(s["msg"], g + 1)
                            pe.wait_ge(s["same"], g + 1)
                            for t in range(TILES):
                                rows = cat[h][:, t, 0:D] if signed else msg[:, t, 0:D]
                                last = nc.tensor.matmul(bank[6][:, t * D:(t + 1) * D], same[:, t, :], rows, start=True, stop=True)
                            last.then_inc(s["sums"], 1)
                            pe.wait_ge(s["sums"], g + 1)
                            pe.sem_inc(in_free[h], 1)

                @block.scalar
                def _(act):
                    with act.Fori(0, STEPS, 1) as it:
                        for h in range(2):
                            g = it * 2 + h
                            act.wait_ge(s["rows_free"], g)
                            act.wait_ge(s["sums"], g + 1)
                            nc.scalar.activation(rows_b[h][:], tiled(bank[6], D), ACT.Copy).then_inc(s["rows"], 1)

        g_wide = 0
        by_order(lambda: window_sums("w1_", None, conv_sum[0], D, gathered_from=y1_t),
                 lambda: edge_sums("e1_", y1_t, conv_sum, signed=False))
        gathers_a += STEPS * 16
        idx_at += STEPS * 16
        free_at += STEPS
        adds += GROUPS * TILES * 8

        with ExitStack() as c:
            s = c.enter_context(phase_semaphores(nc, "n1_", (
                "t", "t_psum", "t_T", "conv", "o", "neg", "exp", "x2", "onehot", "typed", "typed_psum", "typed_T",
                "proj", "h", "u", "centred", "square", "var", "log", "std", "link", "pool_link", "ones_set", "onehot_zeroed")))
            rows, numbers = wide_buffers(c, "n1_")
            norm = Norm(rows, numbers)
            sum0, sum1 = rows("sum0", D, 2), rows("sum1", D, 2)
            y, t_in, o, neg, exped, v = rows("y"), rows("t"), rows("o"), rows("neg"), rows("exped"), rows("v")
            x2 = rows("x2_", D, 2)
            x_typed = rows("x_typed", 2 * D)
            h_out = rows("h_out", 4 * D)
            ntype, log = numbers("ntype", "log")
            onehot = c.enter_context(nc.sbuf_tensor("n1_onehot", [P, 3, 32], f32))
            onehotT = c.enter_context(nc.sbuf_tensor("n1_onehotT", [PART_ROWS, P], bf16))
            by_type = onehot[:, :, 0:WIDE * NODE_TYPES].rearrange("p n (t k) -> p n t k", k=NODE_TYPES)
            tT = c.enter_context(nc.sbuf_tensor("n1_tT", [D + 1, WIDE * P], f32))
            typedT = c.enter_context(nc.sbuf_tensor("n1_typedT", [P, WIDE * P], f32))
            t_psum, conv_psum, onehot_psum, typed_psum = wide_bank[0], bank[2], bank[3], wide_bank[2]
            pair_psum = bank[6:8]
            block = c.enter_context(nc.Block())

            @block.sync
            def _(sp):
                def load(b, early):
                    if not early:
                        sp.wait_ge(s["t"], b.g - 1)
                    sp.dma_start(sum0[b.h][:], wide_group_of(conv_sum[0], b.g)).then_inc(loaded[b.h], 16)
                    sp.dma_start(sum1[b.h][:], wide_group_of(conv_sum[1], b.g)).then_inc(loaded[b.h], 16)

                def step(b, first, last):
                    if first:
                        load(b, True)
                        load(b.next(), True)
                    if b.ahead > 1:
                        load(b.next().next(), False)

                pipeline(sp, step)

            @block.gpsimd
            def _(pool):
                links = Links(pool, s["pool_link"], 2 * 6, passed)
                link = links.link

                def summed(b, first):
                    if not first:
                        pool.wait_ge(s["t_psum"], b.g)
                    pool.wait_ge(loaded[b.h], b.round * 32 + 32 + loaded_at[b.h])
                    pool.sem_inc(passed, 1)
                    link(pool.tensor_tensor(sum0[b.h][:], sum0[b.h][:], sum1[b.h][:], ALU.add))
                    link(pool.tensor_tensor(y[:], x_all[:, b.tiles, :], per_row(dis_all[:, b.tiles]), ALU.mult))
                    link(pool.tensor_tensor(sum0[b.h][:], sum0[b.h][:], y[:], ALU.add))
                    pool.tensor_tensor(t_in[:], sum0[b.h][:], per_row(dis_all[:, b.tiles]), ALU.mult).then_inc(s["t"], 1)

                def step(b, first, last):
                    if first:
                        summed(b, True)
                        summed(b.next(), False)
                    if not first:
                        pool.wait_ge(s["typed_psum"], b.g)
                        pool.sem_inc(passed, 1)
                    link(pool.tensor_copy(ntype[:], ntype_all[:, b.tiles]))
                    link(pool.tensor_copy(by_type[:, :, :, 1], ntype[:].unsqueeze(1).to_broadcast([P, 3, WIDE])))
                    pool.tensor_scalar(by_type[:, :, :, 0], ntype[:].unsqueeze(1).to_broadcast([P, 3, WIDE]), -1.0, 1.0, ALU.mult, ALU.add).then_inc(s["onehot"], 1)
                    if b.ahead > 1:
                        summed(b.next().next(), False)
                    pool.wait_ge(s["x2"], b.g + 1)
                    pool.sem_inc(passed, 1)
                    link(pool.tensor_tensor(x_typed[:, :, D:2 * D], x2[b.h][:], per_row(ntype[:]), ALU.mult))
                    pool.tensor_tensor(x_typed[:, :, 0:D], x2[b.h][:], x_typed[:, :, D:2 * D], ALU.subtract).then_inc(s["typed"], 1)

                pool.wait_ge(s["onehot_zeroed"], 1)
                pipeline(pool, step, links)

            @block.tensor
            def _(pe):
                def transposes(b, first):
                    if not first:
                        pe.wait_ge(s["t_T"], b.g)
                    pe.wait_ge(s["t"], b.g + 1)
                    pe.sem_inc(pe_passed, 1)
                    for t in range(WIDE):
                        last = nc.tensor.transpose(t_psum[0:D, t * P:(t + 1) * P], t_in[:, t, :], ident[:])
                    last.then_inc(s["t_psum"], 1)

                def conv(b, first):
                    if not first:
                        pe.wait_ge(s["o"], b.g)
                    pe.wait_ge(s["t_T"], b.g + 1)
                    pe.sem_inc(pe_passed, 1)
                    for t in range(WIDE):
                        last = nc.tensor.matmul(conv_psum[:, t * D:(t + 1) * D], tT[:, t * P:(t + 1) * P], Wconv[:], start=True, stop=True)
                    last.then_inc(s["conv"], 1)

                def step(b, first, last):
                    if first:
                        transposes(b, True)
                        pe.wait_ge(s["ones_set"], 1)
                        conv(b, True)
                        transposes(b.next(), False)
                        conv(b.next(), False)
                    if b.ahead > 1:
                        transposes(b.next().next(), False)
                    if not first:
                        pe.wait_ge(s["typed_T"], b.g)
                    pe.wait_ge(s["onehot"], b.g + 1)
                    pe.wait_ge(s["typed"], b.g + 1)
                    pe.sem_inc(pe_passed, 1)
                    nc.tensor.transpose(onehot_psum[0:PART_ROWS, 0:P], onehot[:].rearrange("p n r -> p (n r)"), ident[:])
                    for t in range(WIDE):
                        ins = nc.tensor.transpose(typed_psum[:, t * P:(t + 1) * P], x_typed[:, t, :], ident[:])
                    ins.then_inc(s["typed_psum"], 1)
                    if b.ahead > 1:
                        conv(b.next().next(), False)
                    pe.wait_ge(s["typed_T"], b.g + 1)
                    pe.sem_inc(pe_passed, 1)
                    for pair in range(WIDE // 2):
                        if not (first and pair < 2):
                            pe.wait_ge(s["h"], b.g * 4 + pair - 1)
                            pe.sem_inc(pe_passed, 1)
                        for k in range(2):
                            t = 2 * pair + k
                            out = pair_psum[pair % 2][:, k * 4 * D:(k + 1) * 4 * D]
                            nc.tensor.matmul(out, typedT[:, t * P:(t + 1) * P], W1234[:], start=True, stop=False)
                            ins = nc.tensor.matmul(out, onehotT[:], b1234_parts[:, t, :], start=False, stop=True)
                        ins.then_inc(s["proj"], 1)

                pipeline(pe, step)

            @block.scalar
            def _(act):
                act.preload_act_table_set("natural_log_exp_and_others")

                def t_copied(b, first):
                    if not first:
                        act.wait_ge(s["conv"], b.g)
                    act.wait_ge(s["t_psum"], b.g + 1)
                    nc.scalar.activation(tT[0:D, :], t_psum[0:D, :], ACT.Copy).then_inc(s["t_T"], 1)

                def exponential(b):
                    act.wait_ge(s["o"], b.g + 1)
                    nc.scalar.activation(neg[:], o[:], ACT.Relu, scale=-1.0).then_inc(s["neg"], 1)
                    act.wait_ge(s["neg"], b.g + 1)
                    nc.scalar.activation(exped[:], neg[:], ACT.Exp, scale=-1.0).then_inc(s["exp"], 1)

                def root(b):
                    act.wait_ge(s["var"], b.g + 1)
                    nc.scalar.activation(log[:], norm.var[:], ACT.Ln).then_inc(s["log"], 1)
                    act.wait_ge(s["log"], b.g + 1)
                    nc.scalar.activation(norm.std[:], log[:], ACT.Exp, scale=0.5).then_inc(s["std"], 1)

                def pair_copied(b, pair):
                    act.wait_ge(s["proj"], b.g * 4 + pair + 1)
                    nc.scalar.activation(h_out[:, 2 * pair:2 * pair + 2, :], pair_psum[pair % 2][:, :].rearrange("p (t d) -> p t d", t=2), ACT.Copy
                                         ).then_inc(s["h"], 1)

                def store_half(b, half):
                    tiles = slice(half * 4, half * 4 + 4)
                    act.wait_ge(s["h"], b.g * 4 + half * 2 + 2)
                    act.dma_start(wide_group_of(h24_t, b.g, 2 * D)[:, tiles, :], h_out[:, tiles, 0:2 * D]).then_inc(stored[half], 16)
                    act.dma_start(wide_group_of(h3_t, b.g)[:, tiles, :], h_out[:, tiles, 2 * D:3 * D]).then_inc(stored[half], 16)

                def step(b, first, last):
                    if first:
                        t_copied(b, True)
                        exponential(b)
                        t_copied(b.next(), False)
                        norm.act_square(act, b.g, s["centred"], s["square"])
                        exponential(b.next())
                        root(b)
                    if b.ahead > 1:
                        t_copied(b.next().next(), False)
                    act.wait_ge(s["typed_psum"], b.g + 1)
                    if not first:
                        act.wait_ge(s["proj"], b.g * 4)
                    nc.scalar.activation(onehotT[:], onehot_psum[0:PART_ROWS, 0:P], ACT.Copy)
                    nc.scalar.activation(typedT[:], typed_psum[:], ACT.Copy).then_inc(s["typed_T"], 1)
                    if not last:
                        norm.act_square(act, b.next().g, s["centred"], s["square"])
                    if b.ahead > 1:
                        exponential(b.next().next())
                    if not last:
                        root(b.next())
                    if not first:
                        act.wait_ge(s["u"], b.g)
                    act.wait_ge(stored[0], b.g * 32 + stored_at[0])
                    pair_copied(b, 0)
                    pair_copied(b, 1)
                    store_half(b, 0)
                    act.wait_ge(stored[1], b.g * 32 + stored_at[1])
                    pair_copied(b, 2)
                    pair_copied(b, 3)
                    store_half(b, 1)

                pipeline(act, step)
                for half in range(2):
                    act.wait_ge(stored[half], stored_at[half] + 32 * WIDE_GROUPS)

            @block.vector
            def _(dve):
                links = Links(dve, s["link"], 2 * 6)
                link = links.link
                dve.memset(tT[D:D + 1, :], 1.0).then_inc(s["ones_set"], 1)
                dve.memset(onehot[:], 0.0).then_inc(s["onehot_zeroed"], 1)

                def kept(b):
                    dve.wait_ge(s["h"], b.g * 4 + 4)
                    nc.vector.tensor_tensor(x_all[:, b.tiles, :], h_out[:, :, 3 * D:4 * D], x2[b.h][:], ALU.add).then_inc(s["u"], 1)

                def convolved(b, first):
                    dve.wait_ge(s["conv"], b.g + 1)
                    if not first:
                        dve.wait_ge(s["exp"], b.g)
                    nc.vector.scalar_tensor_tensor(o[:], x_all[:, b.tiles, :], ALPHA, wide_rows(conv_psum), ALU.mult, ALU.add).then_inc(s["o"], 1)

                def step(b, first, last):
                    if first:
                        convolved(b, True)
                    dve.wait_ge(s["o"], b.g + 1)
                    dve.wait_ge(s["exp"], b.g + 1)
                    link(nc.vector.scalar_tensor_tensor(v[:], o[:], 0.0, exped[:], ALU.max, ALU.add))
                    link(nc.vector.scalar_tensor_tensor(v[:], v[:], -1.0, x_all[:, b.tiles, :], ALU.add, ALU.add))
                    norm.centre(link, v[:], s["centred"])
                    if not last:
                        convolved(b.next(), False)
                    norm.variance(dve, link, b.g, s["square"], s["var"])
                    if not first:
                        dve.wait_ge(s["typed"], b.g - 1)
                    norm.scale(dve, link, x2[b.h][:], b.g, s["std"], s["x2"])
                    if not first:
                        kept(b.last())
                    if last:
                        kept(b)

                pipeline(dve, step, links)
        loaded_at = [loaded_at[h] + IN_SLOT[h] * 32 for h in range(2)]
        stored_at = [at + WIDE_GROUPS * 32 for at in stored_at]

        def edge_attention():
            with ExitStack() as c:
                s = c.enter_context(phase_semaphores(nc, "e2_", (
                    "idx_f", "wide", "same", "typed", "typed_psum", "typed_T", "w", "score", "exp",
                    "scat_idx", "msg", "sums", "rows", "rows_free", "link")))
                (idx, cat, side, extra, feat, scat_idx, rows_a, rows_b, idx_f, gidx,
                 same, masked, small, msg, typed, catT, sideT, hiddenT, work, hw) = edge_buffers(c, "e2_")
                block = c.enter_context(nc.Block())
                before_a, before_b, adds_before = gathers_a, gathers_b, adds

                @block.sync
                def _(sp):
                    with sp.Fori(0, STEPS, 1) as it:
                        for h in range(2):
                            g = it * 2 + h
                            sp.wait_ge(in_free[h], it + free_at)
                            sp.dma_start(idx[h][:], io["idx"][bass.ds(g * P, P), :]).then_inc(idx_loaded[h], 16)
                            sp.dma_start(feat[h][:], group_of(io["edge16"], g, F_EDGE)).then_inc(feat_loaded[h], 16)

                @block.gpsimd
                def _(pool):
                    def gather(t, h, it):
                        pool.wait_ge(idx_loaded[h], it * 16 + 16 + idx_at)
                        pool.sem_inc(passed, 1)
                        pool.indirect_dma_start(cat[h][:, t, :], None, h24_t,
                                                bass.IndirectOffsetOnAxis(ap=idx[h][:, t:t + 1], axis=0)
                                                ).then_inc(gath_a[h][t], 16)
                        pool.indirect_dma_start(extra[h][:, t, :], None, h3_t,
                                                bass.IndirectOffsetOnAxis(ap=idx[h][:, TILES + t:TILES + t + 1], axis=0)
                                                ).then_inc(gath_b[h][t], 16)

                    def scatter(t, h, g):
                        k = t % 2
                        pool.wait_ge(added[k], g * (16 * TILES // 2) + 16 * (t // 2) + adds_before)
                        if t == 0:
                            pool.wait_ge(s["scat_idx"], g + 1)
                            pool.wait_ge(s["rows"], g + 1)
                        if t == 1:
                            pool.sem_inc(s["rows_free"], 1)
                        pool.sem_inc(passed, 1)
                        pool.indirect_dma_start(attn_sum[k], bass.IndirectOffsetOnAxis(ap=scat_idx[h][:, t:t + 1], axis=0),
                                                rows_b[h][:, t, :], None, compute_op=ALU.add).then_inc(added[k], 16)

                    for t in range(TILES):
                        gather(t, 0, 0)
                    with pool.Fori(0, STEPS - 1, 1) as it:
                        for t in range(TILES):
                            gather(t, 1, it)
                            scatter(t, 0, it * 2)
                        for t in range(TILES):
                            gather(t, 0, it + 1)
                            scatter(t, 1, it * 2 + 1)
                    for t in range(TILES):
                        gather(t, 1, STEPS - 1)
                        scatter(t, 0, GROUPS - 2)
                    for t in range(TILES):
                        scatter(t, 1, GROUPS - 1)
                    for k in range(2):
                        pool.wait_ge(added[k], GROUPS * TILES * 8 + adds_before)

                @block.vector
                def _(dve):
                    FW = F_EDGE * EDGE_TYPES
                    with dve.Fori(0, STEPS, 1) as it:
                        link, end = linker(dve, s["link"], it, 20)
                        for h in range(2):
                            g = it * 2 + h
                            cols = bass.ds(g * TILES, TILES)
                            dve.wait_ge(s["wide"], g)
                            dve.wait_ge(s["same"], g)
                            dve.wait_ge(idx_loaded[h], it * 16 + 16 + idx_at)
                            nc.vector.tensor_copy(idx_f[:], idx[h][:]).then_inc(s["idx_f"], 1)
                            dve.wait_ge(s["typed_psum"], g)
                            link(nc.vector.tensor_copy(small[0][:, 0:TILES], etype_all[:, cols]))
                            for k in range(EDGE_TYPES):
                                last = nc.vector.tensor_scalar(typed[:, :, FW + k], small[0][:, 0:TILES], float(k), None, ALU.is_equal)
                            link(last)
                            dve.wait_ge(feat_loaded[h], it * 16 + 16)
                            for k in range(EDGE_TYPES):
                                last = nc.vector.tensor_tensor(typed[:, :, k * F_EDGE:(k + 1) * F_EDGE], feat[h][:],
                                                               typed[:, :, FW + k:FW + k + 1].to_broadcast([P, TILES, F_EDGE]), ALU.mult)
                            last.then_inc(s["typed"], 1)
                            dve.wait_ge(s["idx_f"], g + 1)
                            dve.wait_ge(s["sums"], g)
                            dve.wait_ge(s["wide"], g + 1)
                            nc.vector.tensor_tensor(same[:, 0:TILES, :], tiled(bank[0], P),
                                                    idx_f[:, TILES:2 * TILES].unsqueeze(2).to_broadcast([P, TILES, P]), ALU.is_equal
                                                    ).then_inc(s["same"], 1)
                            dve.wait_ge(s["rows_free"], g)
                            nc.vector.tensor_scalar(scat_idx[h][:, 0:TILES], recv_all[:, cols], 1.0, None, ALU.mult).then_inc(s["scat_idx"], 1)
                            for t in range(TILES):
                                dve.wait_ge(gath_a[h][t], it * 16 + 16 + before_a)
                                dve.wait_ge(gath_b[h][t], it * 16 + 16 + before_b)
                            dve.wait_ge(s["w"], g + 1)
                            link(nc.vector.tensor_tensor(hw[:], cat[h][:], tiled(bank[5], 2 * D), ALU.add))
                            link(nc.vector.tensor_tensor(work[0][:], extra[h][:], hw[:, :, D:2 * D], ALU.mult))
                            dve.sem_inc(in_free[h], 1)
                            link(nc.vector.tensor_reduce(small[1][:, 0:TILES], work[0][:], AX.X, ALU.add))
                            score = small[1][:, TILES:2 * TILES]
                            link(nc.vector.tensor_scalar(score, small[1][:, 0:TILES], HEAD_DIM ** -0.5, None, ALU.mult))
                            link(nc.vector.tensor_reduce(small[2][:, 0:TILES], score.unsqueeze(2), AX.X, ALU.max))
                            nc.vector.tensor_tensor(small[2][:, TILES:2 * TILES], score, small[2][:, 0:TILES], ALU.subtract).then_inc(s["score"], 1)
                            dve.wait_ge(s["exp"], g + 1)
                            link(nc.vector.tensor_reduce(small[4][:, 0:TILES], small[3][:, 0:TILES].unsqueeze(2), AX.X, ALU.add))
                            link(nc.vector.reciprocal(small[4][:, TILES:2 * TILES], small[4][:, 0:TILES]))
                            link(nc.vector.tensor_tensor(small[5][:, 0:TILES], small[3][:, 0:TILES], small[4][:, TILES:2 * TILES], ALU.mult))
                            nc.vector.tensor_tensor(msg[:, :, 0:D], hw[:, :, 0:D], over_features(small[5][:, 0:TILES]), ALU.mult).then_inc(s["msg"], 1)
                            dve.wait_ge(s["msg"], g + 1)
                        end()

                @block.tensor
                def _(pe):
                    TW = EDGE_TYPES * (F_EDGE + 1)
                    with pe.Fori(0, STEPS, 1) as it:
                        for h in range(2):
                            g = it * 2 + h
                            pe.wait_ge(s["same"], g)
                            pe.wait_ge(s["idx_f"], g + 1)
                            for t in range(TILES):
                                last = nc.tensor.transpose(bank[0][:, t * P:(t + 1) * P],
                                                           idx_f[:, TILES + t:TILES + t + 1].to_broadcast([P, P]), ident[:])
                            last.then_inc(s["wide"], 1)
                            pe.wait_ge(s["typed_T"], g)
                            pe.wait_ge(s["typed"], g + 1)
                            pe.sem_inc(pe_passed, 1)
                            for t in range(TILES):
                                last = nc.tensor.transpose(bank[3][0:TW, t * P:(t + 1) * P], typed[:, t, :], ident[:])
                            last.then_inc(s["typed_psum"], 1)
                            pe.wait_ge(s["msg"], g)
                            pe.wait_ge(s["typed_T"], g + 1)
                            pe.sem_inc(pe_passed, 1)
                            for t in range(TILES):
                                last = nc.tensor.matmul(bank[5][:, t * P:(t + 1) * P], catT[0:TW, t * P:(t + 1) * P],
                                                        W5[:].rearrange("p a d -> p (a d)"), start=True, stop=True)
                            last.then_inc(s["w"], 1)
                            pe.wait_ge(s["rows"], g)
                            pe.wait_ge(s["same"], g + 1)
                            pe.wait_ge(s["msg"], g + 1)
                            for t in range(TILES):
                                last = nc.tensor.matmul(bank[6][:, t * D:(t + 1) * D], same[:, t, :], msg[:, t, 0:D], start=True, stop=True)
                            last.then_inc(s["sums"], 1)

                @block.scalar
                def _(act):
                    TW = EDGE_TYPES * (F_EDGE + 1)
                    with act.Fori(0, STEPS, 1) as it:
                        for h in range(2):
                            g = it * 2 + h
                            act.wait_ge(s["w"], g)
                            act.wait_ge(s["typed_psum"], g + 1)
                            nc.scalar.activation(catT[0:TW, :], bank[3][0:TW, :], ACT.Copy).then_inc(s["typed_T"], 1)
                            act.wait_ge(s["score"], g + 1)
                            nc.scalar.activation(small[3][:, 0:TILES], small[2][:, TILES:2 * TILES], ACT.Exp).then_inc(s["exp"], 1)
                            act.wait_ge(s["rows_free"], g)
                            act.wait_ge(s["sums"], g + 1)
                            nc.scalar.activation(rows_b[h][:], tiled(bank[6], D), ACT.Copy).then_inc(s["rows"], 1)

        by_order(lambda: window_attention("w2_", attn_sum[0]), edge_attention)
        gathers_a += STEPS * 16
        gathers_b += STEPS * 16
        idx_at += STEPS * 16
        free_at += STEPS
        adds += GROUPS * TILES * 8

        with ExitStack() as c:
            s = c.enter_context(phase_semaphores(nc, "n2_", (
                "sum", "x3", "kept", "x3_psum", "x3_T", "prod", "z", "f", "centred", "square", "var", "std", "link", "ones_set")))
            rows, numbers = wide_buffers(c, "n2_")
            norm = Norm(rows, numbers)
            sum0, sum1 = rows("sum0", D, 2), rows("sum1", D, 2)
            summed = rows("summed", D, 2)
            v, x3 = rows("v"), rows("x3_", D, 2)
            z_out, f_out = rows("z_out", 2 * D, 2), rows("f_out", D, 2)
            x3T = c.enter_context(nc.sbuf_tensor("n2_x3T", [D + 1, WIDE * P], f32))
            x3_psum, z_psum, f_psum = wide_bank[0], wide_bank[1], bank[4]
            block = c.enter_context(nc.Block())

            @block.sync
            def _(sp):
                def load(b, early):
                    if not early:
                        sp.wait_ge(s["sum"], b.g - 1)
                    sp.dma_start(sum0[b.h][:], wide_group_of(attn_sum[0], b.g)).then_inc(loaded[b.h], 16)
                    sp.dma_start(sum1[b.h][:], wide_group_of(attn_sum[1], b.g)).then_inc(loaded[b.h], 16)

                def store(b):
                    sp.wait_ge(s["z"], b.g + 1)
                    sp.dma_start(wide_group_of(z3_t, b.g, 2 * D), z_out[b.h][:]).then_inc(stored[b.h], 16)
                    sp.wait_ge(s["f"], b.g + 1)
                    sp.dma_start(wide_group_of(f3_t, b.g), f_out[b.h][:]).then_inc(stored[b.h], 16)

                def step(b, first, last):
                    if first:
                        load(b, True)
                    if not last:
                        load(b.next(), first)
                    if not first:
                        store(b.last())
                    if last:
                        store(b)

                pipeline(sp, step)
                for h in range(2):
                    sp.wait_ge(stored[h], stored_at[h] + 32 * IN_SLOT[h])

            @block.gpsimd
            def _(pool):
                def add(b, early):
                    if not early:
                        pool.wait_ge(s["centred"], b.g - 1)
                    pool.wait_ge(loaded[b.h], b.round * 32 + 32 + loaded_at[b.h])
                    pool.sem_inc(passed, 1)
                    pool.tensor_tensor(summed[b.h][:], sum0[b.h][:], sum1[b.h][:], ALU.add).then_inc(s["sum"], 1)

                def step(b, first, last):
                    if first:
                        add(b, True)
                    if not last:
                        add(b.next(), first)
                    pool.wait_ge(s["x3"], b.g + 1)
                    pool.sem_inc(passed, 1)
                    pool.tensor_copy(x_all[:, b.tiles, :], x3[b.h][:]).then_inc(s["kept"], 1)

                pipeline(pool, step)

            @block.tensor
            def _(pe):
                def step(b, first, last):
                    if not first:
                        pe.wait_ge(s["x3_T"], b.g)
                    pe.wait_ge(s["x3"], b.g + 1)
                    pe.sem_inc(pe_passed, 1)
                    for t in range(WIDE):
                        ins = nc.tensor.transpose(x3_psum[0:D, t * P:(t + 1) * P], x3[b.h][:, t, :], ident[:])
                    ins.then_inc(s["x3_psum"], 1)
                    if first:
                        pe.wait_ge(s["ones_set"], 1)
                    else:
                        pe.wait_ge(s["f"], b.g)
                    pe.wait_ge(s["x3_T"], b.g + 1)
                    pe.sem_inc(pe_passed, 1)
                    for t in range(WIDE):
                        nc.tensor.matmul(z_psum[:, t * 2 * D:(t + 1) * 2 * D], x3T[:, t * P:(t + 1) * P], Wsign[:, 0:2 * D], start=True, stop=True)
                        ins = nc.tensor.matmul(f_psum[:, t * D:(t + 1) * D], x3T[:, t * P:(t + 1) * P], Wsign[:, 2 * D:3 * D], start=True, stop=True)
                    ins.then_inc(s["prod"], 1)

                pipeline(pe, step)

            @block.scalar
            def _(act):
                def step(b, first, last):
                    if first:
                        norm.act_square(act, b.g, s["centred"], s["square"])
                        norm.act_root(act, b.g, s["var"], s["std"])
                    if not first:
                        act.wait_ge(s["prod"], b.g)
                    act.wait_ge(s["x3_psum"], b.g + 1)
                    nc.scalar.activation(x3T[0:D, :], x3_psum[0:D, :], ACT.Copy).then_inc(s["x3_T"], 1)
                    if not last:
                        norm.act_square(act, b.next().g, s["centred"], s["square"])
                        norm.act_root(act, b.next().g, s["var"], s["std"])
                    act.wait_ge(stored[b.h], b.round * 32 + stored_at[b.h])
                    act.wait_ge(s["prod"], b.g + 1)
                    nc.scalar.activation(z_out[b.h][:], wide_rows(z_psum, 2 * D), ACT.Copy).then_inc(s["z"], 1)
                    nc.scalar.activation(f_out[b.h][:], wide_rows(f_psum), ACT.Copy).then_inc(s["f"], 1)

                pipeline(act, step)

            @block.vector
            def _(dve):
                links = Links(dve, s["link"], 2 * 5)
                link = links.link
                dve.memset(x3T[D:D + 1, :], 1.0).then_inc(s["ones_set"], 1)

                def step(b, first, last):
                    dve.wait_ge(s["sum"], b.g + 1)
                    link(nc.vector.tensor_tensor(v[:], summed[b.h][:], x_all[:, b.tiles, :], ALU.add))
                    norm.centre(link, v[:], s["centred"])
                    norm.variance(dve, link, b.g, s["square"], s["var"])
                    if not first:
                        dve.wait_ge(s["kept"], b.g - 1)
                        dve.wait_ge(s["x3_psum"], b.g - 1)
                    norm.scale(dve, link, x3[b.h][:], b.g, s["std"], s["x3"])

                pipeline(dve, step, links)
        loaded_at = [loaded_at[h] + IN_SLOT[h] * 32 for h in range(2)]
        stored_at = [stored_at[h] + IN_SLOT[h] * 32 for h in range(2)]

        by_order(lambda: window_sums("w3_", None, sign_sum[0], D, gathered_from=z3_halves, signed=True),
                 lambda: edge_sums("e3_", z3_halves, sign_sum, signed=True))
        free_at += STEPS


        with ExitStack() as c:
            s = c.enter_context(phase_semaphores(nc, "n3_", (
                "o", "o_square", "o_sum_sq", "o_root", "y", "centred", "square", "var", "std", "link", "pool_link")))
            rows, numbers = wide_buffers(c, "n3_")
            norm = Norm(rows, numbers)
            sum0, sum1, own = rows("sum0", D, 2), rows("sum1", D, 2), rows("own", D, 2)
            o, y = rows("o", D, 2), rows("y", D, 2)
            o_square, unit, v = rows("o_square"), rows("unit"), rows("v")
            o_sum_sq, o_root, guarded, o_scale = numbers("o_sum_sq", "o_root", "guarded", "o_scale")
            block = c.enter_context(nc.Block())

            @block.sync
            def _(sp):
                def load(b, early):
                    if not early:
                        sp.wait_ge(s["o"], b.g - 1)
                    sp.dma_start(sum0[b.h][:], wide_group_of(sign_sum[0], b.g)).then_inc(loaded[b.h], 16)
                    sp.dma_start(sum1[b.h][:], wide_group_of(sign_sum[1], b.g)).then_inc(loaded[b.h], 16)
                    sp.dma_start(own[b.h][:], wide_group_of(f3_t, b.g)).then_inc(loaded[b.h], 16)

                def store(b):
                    sp.wait_ge(s["y"], b.g + 1)
                    sp.dma_start(wide_group_of(io["out"], b.g), y[b.h][:]).then_inc(stored[b.h], 16)

                def step(b, first, last):
                    if first:
                        load(b, True)
                    if not last:
                        load(b.next(), first)
                    if not first:
                        store(b.last())
                    if last:
                        store(b)

                pipeline(sp, step)
                for h in range(2):
                    sp.wait_ge(stored[h], stored_at[h] + 16 * IN_SLOT[h])

            @block.gpsimd
            def _(pool):
                links = Links(pool, s["pool_link"], 2 * 2, passed)
                link = links.link

                def step(b, first, last):
                    if not first:
                        pool.wait_ge(s["centred"], b.g - 1)
                    pool.wait_ge(loaded[b.h], b.round * 48 + 48 + loaded_at[b.h])
                    pool.sem_inc(passed, 1)
                    link(pool.tensor_tensor(sum0[b.h][:], sum0[b.h][:], sum1[b.h][:], ALU.add))
                    link(pool.tensor_tensor(sum1[b.h][:], sum0[b.h][:], per_row(rcount_all[:, b.tiles]), ALU.mult))
                    pool.tensor_tensor(o[b.h][:], sum1[b.h][:], own[b.h][:], ALU.add).then_inc(s["o"], 1)

                pipeline(pool, step, links)

            @block.scalar
            def _(act):
                def o_squared(b):
                    act.wait_ge(s["o"], b.g + 1)
                    nc.scalar.activation(o_square[:], o[b.h][:], ACT.Square).then_inc(s["o_square"], 1)

                def o_rooted(b):
                    act.wait_ge(s["o_sum_sq"], b.g + 1)
                    nc.scalar.activation(o_root[:], o_sum_sq[:], ACT.Sqrt).then_inc(s["o_root"], 1)

                def step(b, first, last):
                    if first:
                        o_squared(b)
                        o_rooted(b)
                    norm.act_square(act, b.g, s["centred"], s["square"])
                    if not last:
                        act.wait_ge(s["o_sum_sq"], b.g + 1)
                        o_squared(b.next())
                    norm.act_root(act, b.g, s["var"], s["std"])
                    if not last:
                        o_rooted(b.next())

                pipeline(act, step)

            @block.vector
            def _(dve):
                links = Links(dve, s["link"], 2 * 8)
                link = links.link

                def root_of(b):
                    dve.wait_ge(s["o_square"], b.g + 1)
                    nc.vector.tensor_reduce(o_sum_sq[:], o_square[:], AX.X, ALU.add).then_inc(s["o_sum_sq"], 1)

                def step(b, first, last):
                    if first:
                        root_of(b)
                    dve.wait_ge(s["o_root"], b.g + 1)
                    link(nc.vector.tensor_scalar(guarded[:], o_root[:], NORM_EPS, None, ALU.max))
                    link(nc.vector.reciprocal(o_scale[:], guarded[:]))
                    link(nc.vector.tensor_tensor(unit[:], o[b.h][:], per_row(o_scale[:]), ALU.mult))
                    link(nc.vector.tensor_tensor(v[:], unit[:], x_all[:, b.tiles, :], ALU.add))
                    norm.centre(link, v[:], s["centred"])
                    if not last:
                        root_of(b.next())
                    norm.variance(dve, link, b.g, s["square"], s["var"])
                    dve.wait_ge(stored[b.h], b.round * 16 + stored_at[b.h])
                    norm.scale(dve, link, y[b.h][:], b.g, s["std"], s["y"])

                pipeline(dve, step, links)


def kernel(x, src, dst, edge_attr_16, edge_attr_64, edge_type_3, edge_weight, node_type_2, **weights):
    import numpy as np
    import concourse.bacc as bacc
    from concourse.bass_utils import run_bass_kernel_spmd

    def padded(a, value=0):
        a = np.asarray(a)
        return np.pad(a, [(0, ROWS - N)] + [(0, 0)] * (a.ndim - 1), constant_values=value)

    def columns(a, tiles=TILES):
        return np.ascontiguousarray(padded(a).reshape(-1, P, tiles).transpose(1, 0, 2).reshape(P, GROUPS * TILES))

    def in_order(a, pads):
        return np.concatenate([np.asarray(a), pads[:ROWS + WINDOW - N]])

    dst_lin = in_order(dst, np.arange(N, ROWS + WINDOW, dtype=np.int32))
    ends = [a.reshape(ROWS // TILES, TILES) for a in (padded(src, N), dst_lin[:ROWS])]
    named = {
        "x": padded(x), "edge64": padded(edge_attr_64), "edge16": padded(edge_attr_16),
        "idx": np.concatenate(ends, axis=1),
        "dst_lin": dst_lin, "dst_firsts": dst_lin[:ROWS:P],
        "edge16_T": np.concatenate([in_order(edge_attr_16, np.zeros((ROWS, F_EDGE), np.float32)).T] * EDGE_TYPES
                                   + [np.ones((EDGE_TYPES, ROWS + WINDOW), np.float32)]),
        "etype_lin": in_order(edge_type_3, np.zeros(ROWS, np.int32)),
        "src_lin": in_order(src, np.full(ROWS, N, np.int32)), "ew_lin": in_order(edge_weight, np.zeros(ROWS, np.float32)),
        "ew_cols": columns(edge_weight), "etype_cols": columns(edge_type_3), "ntype_cols": columns(node_type_2, WIDE),
    }
    for short in ("We1", "be1", "We2", "be2", "Wn1", "bn1", "Wn2", "bn2"):
        named[short] = weights["L0_gnn_" + short]
    named["W_conv"], named["b_conv"] = weights["L1_gnn_W"], weights["L1_gnn_b"]
    for k in range(1, 6):
        named[f"W{k}"], named[f"b{k}"] = weights[f"L2_gnn_W{k}"], weights[f"L2_gnn_b{k}"]
    named["W_sign"], named["b_sign"] = weights["L3_gnn_W"], weights["L3_gnn_b"]

    nc = bacc.Bacc("TRN2", target_bir_lowering=False, num_devices=1)
    arrays, io = {}, {}
    for name, a in named.items():
        a = np.ascontiguousarray(a)
        arrays["in_" + name] = a
        io[name] = nc.dram_tensor("in_" + name, a.shape, mybir.dt.from_np(a.dtype), kind="ExternalInput").ap()
    io["out"] = nc.dram_tensor("out", (ROWS, D), f32, kind="ExternalOutput").ap()
    build(nc, io)
    result = run_bass_kernel_spmd(nc, [arrays], core_ids=[0]).results[0]["out"]
    return result[:N]
```
